# Optimizing a Trainium2 kernel written in Bass

```python
import numpy as np
import jax
import jax.numpy as jnp

def _softmax(x, axis=-1):
    return jax.nn.softmax(x, axis=axis)

def _gelu(x):
    return jax.nn.gelu(x, approximate=True)

def _silu(x):
    return jax.nn.silu(x)

def _sigmoid(x):
    return jax.nn.sigmoid(x)

def _layernorm(x, axis=-1, eps=1e-05):
    m = jnp.mean(x, axis=axis, keepdims=True)
    v = jnp.var(x, axis=axis, keepdims=True)
    return (x - m) / jnp.sqrt(v + eps)

def _scatter_add(tgt, idx, src, axis=0):
    return tgt.at[idx].add(src)

def _segment_sum(src, seg, n):
    return jax.ops.segment_sum(src, seg, n)
kernel_name = 'mk_xattn_ffn_d1_seqx_r8_a23d23'

def setup_inputs(seed: int=0):
    np.random.seed(seed)
    _w = jnp.asarray

    def _rec_inputs():
        import jax
        import jax.numpy as jnp
        _rk = jax.random.key(seed)
        x = -0.0002928 + 1 * jax.random.normal(jax.random.fold_in(_rk, 1), (32, 64, 128), jnp.float32)
        _lenS = 64 - jax.random.randint(jax.random.fold_in(_rk, 7), (32,), 0, max(1, 64 // 4) + 1, jnp.int32)
        _lenS2 = 64 - jax.random.randint(jax.random.fold_in(_rk, 8), (32,), 0, max(1, 64 // 4) + 1, jnp.int32)
        _ctx_1024P = jax.random.normal(jax.random.fold_in(_rk, 11), (32, 16, 128), jnp.float32)
        _ctx_1024c = jax.random.dirichlet(jax.random.fold_in(_rk, 511), 0.3 * jnp.ones((16,), jnp.float32), (32, 64))
        _ctx_1024t = jnp.einsum('bsk,bkd->bsd', _ctx_1024c, _ctx_1024P)
        _ctx_1024t = _ctx_1024t * jax.lax.rsqrt(jnp.mean(jnp.square(_ctx_1024t)) + 1e-12) * 0.953939
        ctx_1024 = -1.39393e-06 + 0.999914 * (_ctx_1024t + 0.3 * jax.random.normal(jax.random.fold_in(_rk, 611), (32, 64, 128), jnp.float32))
        fside_BxSx3_0 = -0.00590116 + 1.0009 * jax.random.normal(jax.random.fold_in(_rk, 12), (32, 64, 3), jnp.float32)
        return (x, ctx_1024, fside_BxSx3_0)
    x, ctx_1024, fside_BxSx3_0 = _rec_inputs()

    def _L0_xattn_setup():
        import jax, jax.numpy as jnp
        import numpy as np
        D_MODEL = 128
        NHEAD = 16
        HEAD_DIM = D_MODEL // NHEAD
        MAX_DIST = 5.0
        DIST_BINS = 32
        SCALE = float(np.sqrt(HEAD_DIM))
        key = jax.random.key(seed)
        ks = jax.random.split(key, 13)
        B, L = (2, 256)
        s = 1.0 / np.sqrt(D_MODEL)
        return {'query': jax.random.normal(ks[0], (B, L, D_MODEL), jnp.float32), 'key': jax.random.normal(ks[1], (B, L, D_MODEL), jnp.float32), 'value': jax.random.normal(ks[2], (B, L, D_MODEL), jnp.float32), 'positions': jax.random.normal(ks[3], (B, L, 3), jnp.float32), 'Wq': jax.random.normal(ks[4], (D_MODEL, D_MODEL), jnp.float32) * s, 'bq': jnp.zeros((D_MODEL,), jnp.float32), 'Wk': jax.random.normal(ks[5], (D_MODEL, D_MODEL), jnp.float32) * s, 'bk': jnp.zeros((D_MODEL,), jnp.float32), 'Wv': jax.random.normal(ks[6], (D_MODEL, D_MODEL), jnp.float32) * s, 'bv': jnp.zeros((D_MODEL,), jnp.float32), 'Wo': jax.random.normal(ks[7], (D_MODEL, D_MODEL), jnp.float32) * s, 'bo': jnp.zeros((D_MODEL,), jnp.float32), 'dist_emb': jax.random.normal(ks[8], (DIST_BINS + 1, NHEAD), jnp.float32) * 0.02}
    _L0_xattn_all = _L0_xattn_setup()
    _L0_xattn_in = {k: v for k, v in _L0_xattn_all.items() if k in ('Wq', 'bq', 'Wk', 'bk', 'Wv', 'bv', 'Wo', 'bo', 'dist_emb')}
    del _L0_xattn_all

    def _L0_ffn_setup():
        import jax, jax.numpy as jnp
        import numpy as np
        B, S, H, F, E, K = (2, 256, 128, 512, 8, 2)

        def _init_w(key, shape, fan_in):
            return jax.random.normal(key, shape, jnp.float32) * fan_in ** (-0.5)

        def _ffn(x, wi, bi, wo, bo):
            return jax.nn.selu(x @ wi + bi) @ wo + bo
        key = jax.random.key(seed)
        ks = jax.random.split(key, 6)
        return {'x': jax.random.normal(ks[0], (B, S, H), jnp.float32), 'gate_wi': _init_w(ks[1], (H, F), H), 'gate_bi': jnp.zeros((F,), jnp.float32), 'gate_wo': _init_w(ks[2], (F, H), F), 'gate_bo': jnp.zeros((H,), jnp.float32), 'exp_wi': _init_w(ks[3], (E, H, F), H), 'exp_bi': jnp.zeros((E, F), jnp.float32), 'exp_wo': _init_w(ks[4], (E, F, H), F), 'exp_bo': jnp.zeros((E, H), jnp.float32)}
    _L0_ffn_all = _L0_ffn_setup()
    _L0_ffn_in = {k: v for k, v in _L0_ffn_all.items() if k in ('gate_wi', 'gate_bi', 'gate_wo', 'gate_bo', 'exp_wi', 'exp_bi', 'exp_wo', 'exp_bo')}
    del _L0_ffn_all
    return {'x': x, 'ctx_1024': ctx_1024, 'fside_BxSx3_0': fside_BxSx3_0, 'L0_xattn_Wq': _L0_xattn_in['Wq'], 'L0_xattn_bq': _L0_xattn_in['bq'], 'L0_xattn_Wk': _L0_xattn_in['Wk'], 'L0_xattn_bk': _L0_xattn_in['bk'], 'L0_xattn_Wv': _L0_xattn_in['Wv'], 'L0_xattn_bv': _L0_xattn_in['bv'], 'L0_xattn_Wo': _L0_xattn_in['Wo'], 'L0_xattn_bo': _L0_xattn_in['bo'], 'L0_xattn_dist_emb': _L0_xattn_in['dist_emb'], 'L0_ffn_gate_wi': _L0_ffn_in['gate_wi'], 'L0_ffn_gate_bi': _L0_ffn_in['gate_bi'], 'L0_ffn_gate_wo': _L0_ffn_in['gate_wo'], 'L0_ffn_gate_bo': _L0_ffn_in['gate_bo'], 'L0_ffn_exp_wi': _L0_ffn_in['exp_wi'], 'L0_ffn_exp_bi': _L0_ffn_in['exp_bi'], 'L0_ffn_exp_wo': _L0_ffn_in['exp_wo'], 'L0_ffn_exp_bo': _L0_ffn_in['exp_bo']}

def reference(x, ctx_1024, fside_BxSx3_0, L0_xattn_Wq, L0_xattn_bq, L0_xattn_Wk, L0_xattn_bk, L0_xattn_Wv, L0_xattn_bv, L0_xattn_Wo, L0_xattn_bo, L0_xattn_dist_emb, L0_ffn_gate_wi, L0_ffn_gate_bi, L0_ffn_gate_wo, L0_ffn_gate_bo, L0_ffn_exp_wi, L0_ffn_exp_bi, L0_ffn_exp_wo, L0_ffn_exp_bo):
    import jax
    import jax.numpy as jnp

    def _L0_xattn_ref(query, key, value, positions, Wq, bq, Wk, bk, Wv, bv, Wo, bo, dist_emb):
        import jax, jax.numpy as jnp
        import numpy as np
        D_MODEL = 128
        NHEAD = 16
        HEAD_DIM = D_MODEL // NHEAD
        MAX_DIST = 5.0
        DIST_BINS = 32
        SCALE = float(np.sqrt(HEAD_DIM))
        B, L, D = query.shape
        H, hd = (NHEAD, HEAD_DIM)
        Q = (query @ Wq + bq).reshape(B, L, H, hd).transpose(0, 2, 1, 3)
        K = (key @ Wk + bk).reshape(B, L, H, hd).transpose(0, 2, 1, 3)
        V = (value @ Wv + bv).reshape(B, L, H, hd).transpose(0, 2, 1, 3)
        scores = jnp.einsum('bhqd,bhkd->bhqk', Q, K) / SCALE
        diff = positions[:, :, None, :] - positions[:, None, :, :]
        dist = jnp.sqrt(jnp.sum(diff * diff, axis=-1))
        bins = jnp.clip((dist / MAX_DIST * DIST_BINS).astype(jnp.int32), 0, DIST_BINS)
        bias = dist_emb[bins].transpose(0, 3, 1, 2)
        attn = jax.nn.softmax(scores + bias, axis=-1)
        out = jnp.einsum('bhqk,bhkd->bhqd', attn, V)
        out = out.transpose(0, 2, 1, 3).reshape(B, L, D)
        return out @ Wo + bo

    def _L0_ffn_ref(x, gate_wi, gate_bi, gate_wo, gate_bo, exp_wi, exp_bi, exp_wo, exp_bo):
        import jax, jax.numpy as jnp
        import numpy as np
        B, S, H, F, E, K = (2, 256, 128, 512, 8, 2)

        def _init_w(key, shape, fan_in):
            return jax.random.normal(key, shape, jnp.float32) * fan_in ** (-0.5)

        def _ffn(x, wi, bi, wo, bo):
            return jax.nn.selu(x @ wi + bi) @ wo + bo
        Bb, Ss, Hh = x.shape
        xf = x.reshape(-1, Hh)
        gate_logits = _ffn(xf, gate_wi, gate_bi, gate_wo, gate_bo)
        topv, topi = jax.lax.top_k(gate_logits, K)
        topv = topv / jnp.sum(topv, axis=-1, keepdims=True)
        onehot = (topi[..., None] == jnp.arange(E)).astype(x.dtype)
        w = jnp.einsum('nk,nke->ne', topv, onehot)
        h = jax.nn.selu(jnp.einsum('nh,ehf->enf', xf, exp_wi) + exp_bi[:, None, :])
        out_e = jnp.einsum('enf,efh->enh', h, exp_wo) + exp_bo[:, None, :]
        out = jnp.einsum('enh,ne->nh', out_e, w)
        return out.reshape(Bb, Ss, Hh)
    x = x + _L0_xattn_ref(_layernorm(x, axis=-1), ctx_1024, ctx_1024, fside_BxSx3_0, L0_xattn_Wq, L0_xattn_bq, L0_xattn_Wk, L0_xattn_bk, L0_xattn_Wv, L0_xattn_bv, L0_xattn_Wo, L0_xattn_bo, L0_xattn_dist_emb)
    x = x + _L0_ffn_ref(_layernorm(x, axis=-1), L0_ffn_gate_wi, L0_ffn_gate_bi, L0_ffn_gate_wo, L0_ffn_gate_bo, L0_ffn_exp_wi, L0_ffn_exp_bi, L0_ffn_exp_wo, L0_ffn_exp_bo)
    return x

_drawn_inputs = setup_inputs


def setup_inputs(seed=0):
    import zlib

    import numpy as np

    out = dict(_drawn_inputs(seed))
    spreads = {'L0_xattn_bq': (0.0, 0.1),
     'L0_xattn_bk': (0.0, 2.0),
     'L0_xattn_bv': (0.0, 0.1),
     'L0_xattn_bo': (0.0, 0.1),
     'L0_ffn_gate_bi': (0.0, 0.1),
     'L0_ffn_gate_bo': (0.0, 0.1),
     'L0_ffn_exp_bi': (0.0, 0.487),
     'L0_ffn_exp_bo': (0.0, 0.474)}
    factors = {'fside_BxSx3_0': 200.0, 'L0_xattn_dist_emb': 120.707}
    for name, (base, spread) in spreads.items():
        noise = np.random.default_rng([zlib.crc32(name.encode()), seed]).standard_normal(out[name].shape)
        drawn = base * np.exp(spread * noise) if base else spread * noise
        out[name] = jnp.asarray(drawn.astype(out[name].dtype))
    for name, factor in factors.items():
        out[name] = (out[name] * factor).astype(out[name].dtype)
    return out
```

```python
from contextlib import ExitStack

import numpy as np
import concourse.bass as bass
from concourse import mybir

F32 = mybir.dt.float32
BF16 = mybir.dt.bfloat16
I32 = mybir.dt.int32
U32 = mybir.dt.uint32
ALU = mybir.AluOpType
ACT = mybir.ActivationFunctionType
AX = mybir.AxisListType

P = 128
SELU_ALPHA = 1.6732632423543772
SELU_SCALE = 1.0507009873554805
EPS = 1e-5
MAX_DIST = 5.0
CAP = 64
PRODUCTS = [(0, 0), (0, 1), (0, 2), (1, 0), (1, 1), (2, 0)]


def build(nc, x, ctx_in, pos, Wq, bq, Wk, bk, Wv, bv, Wo, bo, emb, g_wi, g_bi, g_wo, g_bo, e_wi, e_bi, e_wo, e_bo, out):
    B, L, D = x.shape
    BINS1, H = emb.shape
    NB = BINS1 - 1
    HD = D // H
    T = B * L // P
    F = g_wi.shape[1]
    FC = F // P
    E = e_wi.shape[0]
    NG = 4
    TG = T // NG
    GTOK = TG * P
    BG = GTOK // L
    JB = P // NB
    IB = L // JB
    HP = H // 2
    NPR = len(PRODUCTS)
    KR = 2 * NPR * HD
    VW = 2 * HD + 2
    SC = HD ** -0.5
    SLOTS = E * CAP
    SCH = SLOTS // P
    assert (L, D, NB, HD, E * CAP) == (64, P, 32, 8, 512)

    st = ExitStack()
    with st:
        def dram(name, shape, dt):
            return nc.dram_tensor(name, shape, dt, kind="Internal").ap()

        def sb(name, shape, dt, where=st):
            return where.enter_context(nc.sbuf_tensor(name, shape, dt))

        def sem(name):
            return st.enter_context(nc.semaphore(name))

        bins_dram = dram("bins_dram", [JB, T, IB, 2, L], BF16)
        parts_dram = {s: dram(f"{s}_parts_dram", [3, P, B * L], BF16) for s in "qk"}

        X = sb("X", [P, T, D], F32)
        ident = sb("ident", [P, P], F32)
        ident_bf = sb("ident_bf", [P, P], BF16)
        lower = sb("lower", [P, P], BF16)
        ones_bf = sb("ones_bf", [P, P], BF16)
        ones_row = sb("ones_row", [1, P], F32)
        stats = sb("stats", [P, T, 6], F32)
        mv = sb("mv", [P, T, 2], F32)
        rstd = sb("rstd", [P, T], F32)
        w_gi = sb("w_gi", [P, F], F32)
        w_go = sb("w_go", [P, FC, D], F32)
        gb_exp = sb("gb_exp", [P, FC], F32)
        gb_lin = sb("gb_lin", [P, FC], F32)
        gbi = sb("gbi", [P, FC], F32)
        gbo_row = sb("gbo_row", [1, D], F32)
        w_ei = sb("w_ei", [P, E, F], F32)
        w_eo = sb("w_eo", [P, E, FC, D], F32)
        ebi = sb("ebi", [P, E, FC], F32)
        ebo = sb("ebo", [P, SCH, D], F32)
        slot_iota = sb("slot_iota", [P, CAP], F32)
        exp_iota = sb("exp_iota", [P, E], F32)
        half_neg = sb("half_neg", [P, T], F32)
        vare = sb("vare", [P, T], F32)
        lnalpha = sb("lnalpha", [P, 1], F32)

        ab = ExitStack()
        posq = sb("posq", [P, T, 3], F32, ab)
        CX = sb("CX", [P, T, D], F32, ab)
        XN = sb("XN", [P, 2, TG, D], F32, ab)
        XT = sb("XT", [P, 2, GTOK], F32, ab)
        CT = sb("CT", [P, 2, GTOK], F32, ab)
        w_att = sb("w_att", [P, 4, D], F32, ab)
        bcols = sb("bcols", [P, 4], F32, ab)
        bo_b = sb("bo_b", [P, D], F32, ab)
        KS = sb("KS", [KR, 2, HP, 2, GTOK], BF16, ab)
        QS = sb("QS", [KR, 2, HP, GTOK], BF16, ab)
        full = {s: sb(f"full_{s}", [P, 2, GTOK], F32, ab) for s in "qk"}
        rest = {s: sb(f"rest_{s}", [P, GTOK], F32, ab) for s in "qk"}
        parts = {s: sb(f"parts_{s}", [P, 2, 3, GTOK], BF16, ab) for s in "qk"}
        VD = sb("VD", [P, B, HP, VW], F32, ab)
        BB = sb("BB", [P, 4, IB * P], BF16, ab)
        OH = sb("OH", [P, 2, IB * P], BF16, ab)
        bin_id = sb("bin_id", [P, 1], F32, ab)
        tab = sb("tab", [P, H], F32, ab)
        tab_last = sb("tab_last", [P, H], F32, ab)
        tab_r = sb("tab_r", [P, H], F32, ab)
        tab_h = sb("tab_h", [P, 3, H], BF16, ab)
        BD = sb("BD", [P, 3, H, JB], BF16, ab)
        base_f = sb("base_f", [1, 2, H], F32, ab)
        base3 = sb("base3", [1, 3, H], BF16, ab)
        PR = sb("PR", [P, 2, H, L], F32, ab)
        PT = sb("PT", [P, 2, HP, P], F32, ab)
        mxp = sb("mxp", [P, 2, H], F32, ab)
        ones1 = sb("ones1", [1, P], BF16, ab)
        mx = sb("mx", [P, H], F32, ab)
        rsum = sb("rsum", [P, H], F32, ab)
        AO = sb("AO", [P, 2, D], F32, ab)
        AOT = sb("AOT", [P, 2, P], F32, ab)
        wf = w_ei[:, :, :].rearrange("p e f -> p (e f)")
        wf2 = w_eo[:, :, :, :].rearrange("p e c h -> p (e c h)")
        posk = wf[:, 0:T * L * 3].rearrange("p (t k c) -> p t k c", t=T, c=3)
        df = wf2[:, 0:T * L * 3].rearrange("p (t k c) -> p t k c", t=T, c=3)
        d2 = wf[:, T * L * 3:T * L * 4].rearrange("p (t k) -> p t k", t=T)
        dv = wf2[:, T * L * 3:T * L * 4].rearrange("p (t k) -> p t k", t=T)
        binv = sb("binv", [P, T, L], BF16, ab)
        ab.close()

        XN2 = sb("XN2", [P, T, D], F32)
        XN2T = sb("XN2T", [P, T * P], F32)
        XS = sb("XS", [P, 3, T, D], BF16)
        xs_r = sb("xs_r", [P, T, D], F32)
        SG = sb("SG", [P, 2, FC, GTOK], F32)
        GE = sb("GE", [P, 2, GTOK], F32)
        GR = sb("GR", [P, 2, GTOK], F32)
        LG = sb("LG", [P, TG, D], F32)
        v8 = sb("v8", [P, T, 8], F32)
        i8 = sb("i8", [P, T, 8], U32)
        i2f = sb("i2f", [P, T, 2], F32)
        vs = sb("vs", [P, T], F32)
        w2 = sb("w2", [P, T, 2], F32)
        eq = sb("eq", [P, 2, T, E], F32)
        wq2 = sb("wq2", [P, 2, T, E], F32)
        Wt = sb("Wt", [P, T, E], F32)
        Wr = sb("Wr", [P, T, E], F32)
        W3 = sb("W3", [P, T, 3, E], BF16)
        Fb = sb("Fb", [P, T + 1, E], BF16)
        slot = sb("slot", [P, T, E], F32)
        cnt = sb("cnt", [P, 1], F32)
        cnt_i = sb("cnt_i", [P, 1], I32)
        G = sb("G", [P, T, SLOTS], BF16)
        GT = sb("GT", [P, T, SCH, P], BF16)
        XG = sb("XG", [P, SLOTS], F32)
        hb = sb("hb", [P, 2, 2, FC, CAP], F32)
        he = sb("he", [P, 2, 2, FC, CAP], F32)
        hr = sb("hr", [P, 2, 2, FC, CAP], F32)
        SE = sb("SE", [P, SCH, 2, FC, CAP], F32)
        wsr = sb("wsr", [P, SCH, E], F32)
        wsl = sb("wsl", [P, SCH], F32)
        Y1 = sb("Y1", [P, SCH, D], F32)
        Y = sb("Y", [P, SCH, D], F32)
        Y3 = sb("Y3", [P, 3, SCH, D], BF16)

        bank = [st.enter_context(nc.psum_tensor(f"bank{i}", [P, 512], F32)) for i in range(8)]
        SPS = [bank[0], bank[1], bank[2], bank[3]]
        PTP = [bank[4], bank[5]]
        OPS, MPS = bank[6], bank[7]

        d_pos, d_x, d_watt, d_small, d_tab = map(sem, ("d_pos", "d_x", "d_watt", "d_small", "d_tab"))
        d_gate, d_ew, d_binw, d_out = map(sem, ("d_gate", "d_ew", "d_binw", "d_out"))
        d_cx = [sem(f"d_cx{g}") for g in range(NG)]
        d_bb = [sem(f"d_bb{i}") for i in range(4)]
        d_part = {s: [sem(f"d_{s}part{i}") for i in range(2)] for s in "qk"}
        d_stack = {s: [sem(f"d_{s}stack{i}") for i in range(2)] for s in "qk"}
        pool_const = sem("pool_const")
        var_done, rstd_done, sqrt_done = map(sem, ("var_done", "rstd_done", "sqrt_done"))
        dve_c = sem("dve_c")
        act_c = sem("act_c")
        pool_c = sem("pool_c")
        sq_done, d2_done, bins_done, bcol_ready = map(sem, ("df_done", "sq_done", "bins_done", "bcol_ready"))
        d2_clamped = sem("d2_clamped")
        bd_ready = sem("bd_ready")
        ct_tr, ct_ev, xn_done, xt_tr, xt_ev = map(sem, ("ct_tr", "ct_ev", "xn_done", "xt_tr", "xt_ev"))
        k_mm, k_full, k_parts, q_mm, q_full, q_parts = map(sem, ("k_mm", "k_full", "k_parts", "q_mm", "q_full", "q_parts"))
        v_mm, v_top, v_bot = map(sem, ("v_mm", "v_top", "v_bot"))
        oh_done, s_mm, sub_done, exp_done, p_tr, pt_ev = map(sem, ("oh_done", "s_mm", "sub_done", "exp_done", "p_tr", "pt_ev"))
        pv_mm, ao_done, ao_tr, aot_ev, wo_mm, x2_done = map(sem, ("pv_mm", "ao_done", "ao_tr", "aot_ev", "wo_mm", "x2_done"))
        xb_done = sem("xb_done")
        n2_done, n2_tr, n2_ev, h_mm, ge_done, gr_done, sg_done = map(sem, ("n2_done", "n2_tr", "n2_ev", "h_mm", "ge_done", "gr_done", "sg_done"))
        lg_mm, lg_ev, top_done, f_done, slot_mm, cnt_done, xs_done = map(sem, ("lg_mm", "lg_ev", "top_done", "f_done", "slot_mm", "cnt_done", "xs_done"))
        g_done, xg_mm, xg_ev, gt_tr, gt_ev, ws_mm = map(sem, ("g_done", "xg_mm", "xg_ev", "gt_tr", "gt_ev", "ws_mm"))
        eh_mm, hb_done, he_done, se_done, y_mm, y3_done, sc_mm, acc_done = map(
            sem, ("eh_mm", "hb_done", "he_done", "se_done", "y_mm", "y3_done", "sc_mm", "acc_done"))
        gw_done = sem("gw_done")
        gt_ev2, slot_next, wsr_done, wsl_done, hr_done = map(sem, ("gt_ev2", "slot_next", "wsr_done", "wsl_done", "hr_done"))
        y1_done, yw_done, ya_done, yb_done, yc_done = map(sem, ("y1_done", "yw_done", "ya_done", "yb_done", "yc_done"))

        def chain(eng, s):
            n = [0]

            def link(ins):
                n[0] += 1
                ins.then_inc(s, 1)
                eng.wait_ge(s, n[0])
            return link

        xt_dram = x.rearrange("b l d -> (b l) d").rearrange("(t p) d -> p t d", p=P)
        cx_dram = ctx_in.rearrange("b l d -> (b l) d").rearrange("(t p) d -> p t d", p=P)
        out_dram = out.rearrange("b l d -> (b l) d").rearrange("(t p) d -> p t d", p=P)
        col = lambda v: v.rearrange("(p a) -> p a", a=1)

        block = st.enter_context(nc.Block())

        @block.sync
        def _(sp):
            sp.dma_start(posq[:, :, :], pos.rearrange("b l c -> (b l) c").rearrange("(t p) c -> p t c", p=P)).then_inc(d_pos, 16)
            for b2 in range(2):
                src = pos.rearrange("(t b) k c -> b t (k c)", b=2)[b2:b2 + 1]
                sp.dma_start(posk[b2 * L:(b2 + 1) * L].rearrange("p t k c -> p t (k c)"),
                             src.broadcast_to([L, T, L * 3])).then_inc(d_pos, 16)
            for g in range(NG):
                sp.dma_start(CX[:, TG * g:TG * (g + 1), :], cx_dram[:, TG * g:TG * (g + 1), :]).then_inc(d_cx[g], 16)
            sp.wait_ge(bins_done, 1)
            for j in range(JB):
                for b2 in range(2):
                    r = b2 * L + IB * j
                    sp.dma_start(bins_dram[j, :, :, b2, :].rearrange("t i m -> i t m"), binv[r:r + IB, :, :]).then_inc(d_binw, 16)
            sp.wait_ge(d_binw, 16 * 2 * JB)

            def spread_bins(t):
                if t >= 4:
                    sp.wait_ge(oh_done, t - 3)
                for j in range(JB):
                    sp.dma_start(BB[NB * j:NB * (j + 1), t % 4, :],
                                 bins_dram[j:j + 1, t].rearrange("a i b m -> a (i b m)").broadcast_to([NB, IB * P])
                                 ).then_inc(d_bb[t % 4], 16)

            def store_parts(s, g):
                sp.wait_ge({"q": q_parts, "k": k_parts}[s], g + 1)
                sp.dma_start(parts_dram[s][:, :, GTOK * g:GTOK * (g + 1)].rearrange("s p n -> p s n"),
                             parts[s][:, g % 2, :, :]).then_inc(d_part[s][g % 2], 16)

            def stack_parts(s, g):
                sp.wait_ge(d_part[s][g % 2], 16 * (g // 2 + 1))
                if g >= 2:
                    sp.wait_ge(s_mm, TG * (g - 1))
                view = parts_dram[s].rearrange("s (c h d) n -> s h d c n", h=2, d=HD)
                for h2 in range(2):
                    for n, pr in enumerate(PRODUCTS):
                        row = (h2 * NPR + n) * HD
                        part = pr[0] if s == "q" else pr[1]
                        dst = QS[row:row + HD, g % 2] if s == "q" else KS[row:row + HD, g % 2, :, h2, :]
                        sp.dma_start(dst, view[part, h2, :, :, GTOK * g:GTOK * (g + 1)]).then_inc(d_stack[s][g % 2], 16)

            spread_bins(0)
            sp.wait_ge(pool_const, 2)
            store_parts("k", 0)
            spread_bins(1)
            stack_parts("k", 0)
            store_parts("q", 0)
            store_parts("k", 1)
            stack_parts("q", 0)
            stack_parts("k", 1)
            store_parts("q", 1)
            stack_parts("q", 1)
            spread_bins(2)
            spread_bins(3)
            store_parts("k", 2)
            store_parts("q", 2)
            store_parts("k", 3)
            store_parts("q", 3)
            for t in range(4, T):
                if t == 6:
                    stack_parts("k", 2)
                    stack_parts("q", 2)
                if t == 10:
                    stack_parts("k", 3)
                    stack_parts("q", 3)
                spread_bins(t)
            sp.wait_ge(gw_done, 1)
            sp.dma_start(out_dram, X[:, :, :]).then_inc(d_out, 16)
            sp.wait_ge(d_out, 16)

        @block.gpsimd
        def _(pool):
            link = chain(pool, pool_c)
            link(nc.gpsimd.memset(ident[:, :], 0.0))
            nc.gpsimd.affine_select(out=ident[:, :], in_=ident[:, :], compare_op=ALU.not_equal, fill=1.0,
                                    base=0, pattern=[[-1, P]], channel_multiplier=1).then_inc(pool_const, 1)
            nc.gpsimd.memset(KS[:, :, :, :, :].rearrange("p a c h n -> p (a c h n)").bitcast(F32), 0.0).then_inc(pool_const, 1)
            pool.wait_ge(pool_const, 2)
            for j in range(JB):
                last = nc.gpsimd.iota(bin_id[NB * j:NB * (j + 1), :], [[0, 1]], base=0, channel_multiplier=1, allow_small_or_imprecise_dtypes=True)
            last.then_inc(pool_const, 1)
            pool.wait_ge(pool_const, 3)
            link(nc.gpsimd.memset(half_neg[:, :], -0.5))
            link(nc.gpsimd.memset(VD[:, :, :, :], 0.0))
            link(nc.gpsimd.memset(VD[0:L, :, :, 2 * HD:2 * HD + 1], 1.0))
            nc.gpsimd.memset(VD[L:P, :, :, 2 * HD + 1:VW], 1.0).then_inc(pool_const, 1)
            pool.wait_ge(pool_const, 4)
            pool.wait_ge(var_done, 1)
            nc.gpsimd.tensor_tensor(rstd[:, :], vare[:, :], half_neg[:, :], ALU.pow).then_inc(rstd_done, 1)
            for g in range(NG):
                pool.wait_ge(k_full, g + 1)
                if g >= 2:
                    pool.wait_ge(d_part["k"][g % 2], 16 * (g // 2))
                f, p3 = full["k"][:, g % 2, :], parts["k"][:, g % 2]
                link(nc.gpsimd.tensor_copy(p3[:, 0, :], f))
                link(nc.gpsimd.tensor_tensor(rest["k"][:, :], f, p3[:, 0, :], ALU.subtract))
                link(nc.gpsimd.tensor_copy(p3[:, 1, :], rest["k"][:, :]))
                nc.gpsimd.tensor_tensor(p3[:, 2, :], rest["k"][:, :], p3[:, 1, :], ALU.subtract).then_inc(k_parts, 1)
                pool.wait_ge(k_parts, g + 1)
            link(nc.gpsimd.memset(lower[:, :], 1.0))
            link(nc.gpsimd.affine_select(out=lower[:, :], in_=lower[:, :], compare_op=ALU.is_gt, fill=0.0,
                                         base=0, pattern=[[1, P]], channel_multiplier=-1))
            link(nc.gpsimd.memset(ones_bf[:, :], 1.0))
            link(nc.gpsimd.memset(ones_row[:, :], 1.0))
            link(nc.gpsimd.memset(lnalpha[:, :], float(np.log(SELU_ALPHA))))
            link(nc.gpsimd.iota(slot_iota[:, :], [[1, CAP]], base=0, channel_multiplier=0, allow_small_or_imprecise_dtypes=True))
            link(nc.gpsimd.iota(exp_iota[:, :], [[1, E]], base=0, channel_multiplier=0, allow_small_or_imprecise_dtypes=True))
            nc.gpsimd.tensor_copy(ident_bf[:, :], ident[:, :]).then_inc(pool_const, 1)
            pool.wait_ge(var_done, 2)
            nc.gpsimd.tensor_tensor(rstd[:, :], vare[:, :], half_neg[:, :], ALU.pow).then_inc(rstd_done, 1)

        @block.scalar
        def _(act):
            link = chain(act, act_c)
            act.dma_start(w_att[:, 0, :], Wq).then_inc(d_watt, 16)
            act.dma_start(w_att[:, 1, :], Wk).then_inc(d_watt, 16)
            act.dma_start(w_att[:, 2, :], Wv).then_inc(d_watt, 16)
            act.dma_start(w_att[:, 3, :], Wo).then_inc(d_watt, 16)
            for i, v in enumerate((bq, bk, bv)):
                act.dma_start(bcols[:, i:i + 1], col(v)).then_inc(d_small, 16)
            act.dma_start(X[:, :, :], xt_dram).then_inc(d_x, 16)
            for j in range(JB):
                act.dma_start(tab[NB * j:NB * (j + 1), :], emb[0:NB, :]).then_inc(d_tab, 16)
            act.dma_start(tab_last[:, :], emb[NB:NB + 1, :].broadcast_to([P, H])).then_inc(d_tab, 16)
            act.dma_start(base_f[0:1, 0, :], emb[NB:NB + 1, :]).then_inc(d_tab, 16)
            act.dma_start(bo_b[:, :], bo.rearrange("(a n) -> a n", a=1).broadcast_to([P, D])).then_inc(d_small, 16)
            act.dma_start(w_gi[:, :], g_wi).then_inc(d_gate, 16)
            act.dma_start(w_go[:, :, :], g_wo.rearrange("(c p) h -> p c h", p=P)).then_inc(d_gate, 16)
            act.dma_start(gbi[:, :], g_bi.rearrange("(c p) -> p c", p=P), allow_slow_non_contiguous=True).then_inc(d_gate, 16)
            act.dma_start(gbo_row[:, :], g_bo.rearrange("(a n) -> a n", a=1)).then_inc(d_gate, 16)
            act.wait_ge(sq_done, 1)
            nc.scalar.activation(df, df, ACT.Square).then_inc(d2_done, 1)
            act.wait_ge(d2_clamped, 1)
            nc.scalar.activation(dv, d2, ACT.Sqrt).then_inc(sqrt_done, 1)
            act.wait_ge(bcol_ready, 1)
            act.wait_ge(d_small, 64)

            def evac_ct(g):
                act.wait_ge(ct_tr, g + 1)
                if g >= 2:
                    act.wait_ge(k_mm, g - 1)
                    act.wait_ge(v_mm, g - 1)
                nc.scalar.activation(CT[:, g % 2, :].rearrange("p (b i j) -> p b i j", b=BG, j=JB),
                                     PTP[g % 2][:, :].rearrange("p (b j i) -> p b i j", b=BG, j=JB), ACT.Copy).then_inc(ct_ev, 1)

            def full_k(g):
                act.wait_ge(k_mm, g + 1)
                if g >= 2:
                    act.wait_ge(k_parts, g - 1)
                nc.scalar.activation(full["k"][:, g % 2, :], SPS[g % 2][:, :], ACT.Identity, bias=bcols[:, 1:2]).then_inc(k_full, 1)

            def v_bottom(n):
                act.wait_ge(v_mm, n + 1)
                nc.scalar.activation(VD[L:P, BG * n:BG * (n + 1), :, HD:2 * HD],
                                     (OPS, MPS)[n % 2][L:P, :].rearrange("p (b c d) -> p b c d", b=BG, c=HP),
                                     ACT.Copy).then_inc(v_bot, 1)

            act.wait_ge(pool_const, 4)
            evac_ct(0)
            evac_ct(1)
            for g in range(NG):
                full_k(g)
                v_bottom(g)
                if g + 2 < NG:
                    evac_ct(g + 2)
            for g in range(NG):
                act.wait_ge(q_mm, g + 1)
                if g >= 2:
                    act.wait_ge(q_parts, g - 1)
                nc.scalar.activation(full["q"][:, g % 2, :], SPS[2 + g % 2][:, :], ACT.Identity, bias=bcols[:, 3:4], scale=SC).then_inc(q_full, 1)
            act.wait_ge(bins_done, 1)
            act.dma_start(w_ei[:, :, :], e_wi.rearrange("e p f -> p e f")).then_inc(d_ew, 16)
            act.dma_start(w_eo[:, :, :, :], e_wo.rearrange("e (c p) h -> p e c h", p=P)).then_inc(d_ew, 16)
            act.dma_start(ebi[:, :, :], e_bi.rearrange("e (c p) -> p e c", p=P), allow_slow_non_contiguous=True).then_inc(d_ew, 16)
            for u in range(2):
                act.dma_start(ebo[u * CAP:(u + 1) * CAP, :, :],
                              e_bo.rearrange("(c u) h -> u c h", u=2)[u:u + 1].broadcast_to([CAP, SCH, D])).then_inc(d_ew, 16)

            def aot(t):
                act.wait_ge(ao_tr, t + 1)
                if t >= 2:
                    act.wait_ge(wo_mm, t - 1)
                nc.scalar.activation(AOT[:, t % 2, :], MPS[:, 0:P], ACT.Identity, bias=bcols[:, 2:3]).then_inc(aot_ev, 1)

            for t in range(T):
                act.wait_ge(sub_done, t + 1)
                nc.scalar.activation(PR[:, t % 2], PR[:, t % 2], ACT.Exp).then_inc(exp_done, 1)
                if t >= 2:
                    act.wait_ge(pv_mm, t - 1)
                for half in range(2):
                    act.wait_ge(p_tr, 2 * t + half + 1)
                    nc.scalar.activation(PT[:, t % 2, 4 * half:4 * half + 4, :].rearrange("p c n -> p (c n)"),
                                         PTP[half][:, :], ACT.Copy).then_inc(pt_ev, 1)
                if t >= 1:
                    aot(t - 1)
            aot(T - 1)

            def evac_n2(g):
                act.wait_ge(n2_tr, g + 1)
                nc.scalar.activation(XN2T[:, GTOK * g:GTOK * (g + 1)], PTP[g % 2][:, :], ACT.Copy).then_inc(n2_ev, 1)

            act.wait_ge(bd_ready, 2)
            evac_n2(0)
            for g in range(NG):
                if g + 1 < NG:
                    evac_n2(g + 1)
                for c in range(FC):
                    n = FC * g + c
                    act.wait_ge(h_mm, n + 1)
                    if n >= 2:
                        act.wait_ge(sg_done, n - 1)
                    nc.scalar.activation(GE[:, n % 2, :], SPS[n % 4][:, :], ACT.Exp, bias=gb_exp[:, c:c + 1]).then_inc(ge_done, 1)
            act.wait_ge(cnt_done, 1)
            rounds = act.value_load(cnt_i[0:1, 0:1], min_val=1, max_val=B * L // CAP)
            with act.Fori(0, rounds) as r:
                act.wait_ge(xg_mm, r + 1)
                nc.scalar.activation(XG[:, :], OPS[:, :], ACT.Copy).then_inc(xg_ev, 1)
                for n in range(T // 2):
                    if n % 2 == 0:
                        act.wait_ge(gt_tr, r * (T // 2) + n + 1)
                        nc.scalar.activation(GT[:, 2 * n:2 * n + 2, :, :].rearrange("p t c n -> p (t c n)"),
                                             PTP[0][:, :].bitcast(BF16), ACT.Copy).then_inc(gt_ev, 1)
                for c in range(SCH):
                    act.wait_ge(hb_done, r * SCH + c + 1)
                    nc.scalar.activation(he[:, c % 2], hb[:, c % 2], ACT.Exp, bias=lnalpha[:, 0:1]).then_inc(he_done, 1)

        @block.vector
        def _(dve):
            link = chain(dve, dve_c)
            dve.wait_ge(d_pos, 48)
            nc.vector.tensor_tensor(df, posq[:, :, :].unsqueeze(2).broadcast_to([P, T, L, 3]), posk, ALU.subtract).then_inc(sq_done, 1)
            dve.wait_ge(d_small, 64)
            link(nc.vector.tensor_scalar(bcols[:, 3:4], bcols[:, 0:1], SC, None, ALU.mult))
            link(nc.vector.memset(ones1[:, :], 1.0))
            nc.vector.memset(BD[:, :, :, :], 0.0).then_inc(bcol_ready, 1)
            dve.wait_ge(d2_done, 1)
            link(nc.vector.tensor_tensor(d2, df[:, :, :, 0], df[:, :, :, 1], ALU.add))
            link(nc.vector.tensor_tensor(d2, d2, df[:, :, :, 2], ALU.add))
            nc.vector.tensor_scalar(d2, d2, 1e-30, 1e30, ALU.max, ALU.min).then_inc(d2_clamped, 1)
            dve.wait_ge(sqrt_done, 1)
            rt, sm = df[:, :, :, 0], df[:, :, :, 1]
            link(nc.vector.reciprocal(rt, dv))
            link(nc.vector.tensor_tensor(rt, d2, rt, ALU.mult))
            link(nc.vector.tensor_tensor(sm, rt, dv, ALU.add))
            link(nc.vector.tensor_scalar(dv, sm, 0.5 / MAX_DIST, float(NB), ALU.mult, ALU.mult))
            link(nc.vector.tensor_scalar(dv, dv, float(NB), None, ALU.min))
            link(nc.vector.tensor_scalar(d2, dv, 2.0 ** 23, -2.0 ** 23, ALU.add, ALU.add))
            link(nc.vector.tensor_tensor(rt, d2, dv, ALU.is_gt))
            nc.vector.tensor_tensor(binv[:, :, :], d2, rt, ALU.subtract).then_inc(bins_done, 1)

            dve.wait_ge(d_tab, 16 * (JB + 2))
            def table_parts(first, last, r, p3):
                link(nc.vector.tensor_tensor(first, first, last, ALU.subtract) if last is not None
                     else nc.vector.tensor_copy(p3[:, 0], first))
                if last is not None:
                    link(nc.vector.tensor_copy(p3[:, 0], first))
                link(nc.vector.tensor_tensor(r, first, p3[:, 0], ALU.subtract))
                link(nc.vector.tensor_copy(p3[:, 1], r))
                link(nc.vector.tensor_tensor(p3[:, 2], r, p3[:, 1], ALU.subtract))
            table_parts(tab[:, :], tab_last[:, :], tab_r[:, :], tab_h[:, :, :])
            table_parts(base_f[:, 0, :], None, base_f[:, 1, :], base3[:, :, :])
            for j in range(JB):
                q = slice(NB * j, NB * (j + 1))
                last = nc.vector.tensor_copy(BD[q, :, :, j], tab_h[q, :, :])
            last.then_inc(bd_ready, 1)

            def moments():
                for t in range(T):
                    last = nc.vector.bn_stats(stats[:, t, :], X[:, t, :])
                link(last)
                for t in range(T):
                    last = nc.vector.bn_aggr(mv[:, t, :], stats[:, t, :])
                link(last)
                nc.vector.tensor_scalar(vare[:, :], mv[:, :, 1], EPS, None, ALU.add).then_inc(var_done, 1)

            def layer_norm(src, dst, t):
                return nc.vector.tensor_scalar(dst, src, mv[:, t, 0:1], rstd[:, t:t + 1], ALU.subtract, ALU.mult)

            def v_upper(n):
                dve.wait_ge(v_mm, n + 1)
                nc.vector.tensor_copy(VD[0:L, BG * n:BG * (n + 1), :, 0:HD],
                                      (OPS, MPS)[n % 2][0:L, :].rearrange("p (b c d) -> p b c d", b=BG, c=HP)).then_inc(v_top, 1)

            def ln_group(g):
                if g >= 2:
                    dve.wait_ge(xt_tr, g - 1)
                for u in range(TG):
                    last = layer_norm(X[:, TG * g + u, :], XN[:, g % 2, u, :], TG * g + u)
                last.then_inc(xn_done, 1)

            dve.wait_ge(d_x, 16)
            moments()
            dve.wait_ge(rstd_done, 1)
            dve.wait_ge(pool_const, 4)
            for g in range(NG):
                if g < 2:
                    ln_group(g)
                v_upper(g)

            def q_side(g):
                dve.wait_ge(xt_tr, g + 1)
                if g >= 2:
                    dve.wait_ge(q_mm, g - 1)
                nc.vector.tensor_copy(XT[:, g % 2, :], PTP[g % 2][:, :]).then_inc(xt_ev, 1)

            def q_split(g):
                dve.wait_ge(q_full, g + 1)
                if g >= 2:
                    dve.wait_ge(d_part["q"][g % 2], 16 * (g // 2))
                f, p3 = full["q"][:, g % 2, :], parts["q"][:, g % 2]
                link(nc.vector.tensor_copy(p3[:, 0, :], f))
                link(nc.vector.tensor_tensor(rest["q"][:, :], f, p3[:, 0, :], ALU.subtract))
                link(nc.vector.tensor_copy(p3[:, 1, :], rest["q"][:, :]))
                nc.vector.tensor_tensor(p3[:, 2, :], rest["q"][:, :], p3[:, 1, :], ALU.subtract).then_inc(q_parts, 1)

            q_side(0)
            q_side(1)
            q_split(0)
            ln_group(2)
            q_side(2)
            q_split(1)
            ln_group(3)
            q_side(3)
            q_split(2)
            q_split(3)
            dve.wait_ge(xn_done, NG)
            link(nc.vector.tensor_tensor(X[:, :, :], X[:, :, :], bo_b[:, :].unsqueeze(1).broadcast_to([P, T, D]), ALU.add))

            dve.wait_ge(pool_const, 4)

            def one_hot(t):
                dve.wait_ge(d_bb[t % 4], 64 * (t // 4 + 1))
                if t >= 2:
                    dve.wait_ge(s_mm, t - 1)
                nc.vector.tensor_scalar(OH[:, t % 2, :], BB[:, t % 4, :], bin_id[:, 0:1], None, ALU.is_equal).then_inc(oh_done, 1)

            def residual(t):
                dve.wait_ge(wo_mm, t + 1)
                nc.vector.tensor_tensor(X[:, t, :], X[:, t, :], MPS[:, P:2 * P], ALU.add).then_inc(x2_done, 1)

            def normalise(t):
                dve.wait_ge(pv_mm, t + 1)
                o = OPS[:, 0:HP * VW].rearrange("p (c w) -> p c w", w=VW)
                link(nc.vector.reciprocal(rsum[:, :].rearrange("p (c h) -> p c h", h=2), o[:, :, 2 * HD:VW]))
                if t >= 2:
                    dve.wait_ge(ao_tr, t - 1)
                nc.vector.tensor_tensor(AO[:, t % 2, :].rearrange("p (c h d) -> p c h d", c=HP, h=2),
                                        o[:, :, 0:2 * HD].rearrange("p c (h d) -> p c h d", h=2),
                                        rsum[:, :].rearrange("p (c h) -> p c h", h=2).unsqueeze(3).broadcast_to([P, HP, 2, HD]),
                                        ALU.mult).then_inc(ao_done, 1)

            one_hot(0)
            for t in range(T):
                if t >= 2:
                    residual(t - 2)
                if t + 1 < T:
                    one_hot(t + 1)
                dve.wait_ge(s_mm, t + 1)
                two = 2 * (t % 2)
                link(nc.vector.reduce_max(mxp[:, 0, :], SPS[two][:, :].rearrange("p (h k) -> p h k", h=H), AX.X))
                link(nc.vector.reduce_max(mxp[:, 1, :], SPS[two + 1][:, :].rearrange("p (h k) -> p h k", h=H), AX.X))
                link(nc.vector.tensor_tensor(mx[:, :], mxp[:, 0, :], mxp[:, 1, :], ALU.max))
                if t >= 2:
                    dve.wait_ge(p_tr, 2 * (t - 1))
                for ih in range(2):
                    last = nc.vector.tensor_tensor(PR[:, t % 2].rearrange("p h (i k) -> p i h k", i=2)[:, ih],
                                                   SPS[two + ih][:, :].rearrange("p (h k) -> p h k", h=H),
                                                   mx[:, :].unsqueeze(2).broadcast_to([P, H, L // 2]), ALU.subtract)
                last.then_inc(sub_done, 1)
                if t >= 1:
                    normalise(t - 1)
            residual(T - 2)
            normalise(T - 1)
            residual(T - 1)
            dve.wait_ge(x2_done, T)

            dve.wait_ge(d_gate, 64)
            link(nc.vector.tensor_scalar(w_go[:, :, :], w_go[:, :, :], SELU_SCALE, None, ALU.mult))
            link(nc.vector.tensor_scalar(gb_lin[:, :], gbi[:, :], -SELU_ALPHA, None, ALU.add))
            nc.vector.tensor_scalar(gb_exp[:, :], gbi[:, :], float(np.log(SELU_ALPHA)), None, ALU.add).then_inc(bd_ready, 1)
            moments()
            dve.wait_ge(rstd_done, 2)
            for g in range(NG):
                for u in range(TG):
                    last = layer_norm(X[:, TG * g + u, :], XN2[:, TG * g + u, :], TG * g + u)
                last.then_inc(n2_done, 1)

            def top2(g):
                dve.wait_ge(lg_mm, g + 1)
                link(nc.vector.tensor_copy(LG[:, :, :].rearrange("p t h -> p (t h)"), (OPS, MPS)[g % 2][:, :]))
                for u in range(TG):
                    t = TG * g + u
                    link(nc.vector.max(v8[:, t, :], LG[:, u, :]))
                    link(nc.vector.max_index(i8[:, t, :], v8[:, t, :], LG[:, u, :]))
                nc.vector.memset(cnt[:, :], 0.0).then_inc(lg_ev, 1)

            for g in range(NG):
                for c in range(FC):
                    n = FC * g + c
                    dve.wait_ge(ge_done, n + 1)
                    link(nc.vector.tensor_scalar(GR[:, n % 2, :], SPS[n % 4][:, :], gb_lin[:, c:c + 1], -SELU_ALPHA, ALU.add, ALU.max))
                    if c == 0 and g >= 2:
                        dve.wait_ge(lg_mm, g - 1)
                    nc.vector.scalar_tensor_tensor(out=SG[:, g % 2, c, :], in0=GE[:, n % 2, :], scalar=SELU_ALPHA,
                                                   in1=GR[:, n % 2, :], op0=ALU.min, op1=ALU.add).then_inc(sg_done, 1)
                if g >= 1:
                    top2(g - 1)
            top2(NG - 1)
            dve.wait_ge(lg_ev, NG)

            link(nc.vector.tensor_copy(i2f[:, :, :], i8[:, :, 0:2]))
            link(nc.vector.tensor_tensor(vs[:, :], v8[:, :, 0], v8[:, :, 1], ALU.add))
            link(nc.vector.reciprocal(vs[:, :], vs[:, :]))
            link(nc.vector.tensor_tensor(w2[:, :, :], v8[:, :, 0:2], vs[:, :].unsqueeze(2).broadcast_to([P, T, 2]), ALU.mult))
            dve.wait_ge(pool_const, 5)
            for k in range(2):
                link(nc.vector.tensor_tensor(eq[:, k], i2f[:, :, k:k + 1].broadcast_to([P, T, E]),
                                             exp_iota[:, :].unsqueeze(1).broadcast_to([P, T, E]), ALU.is_equal))
            link(nc.vector.memset(Fb[:, T:T + 1, :], 0.0))
            nc.vector.tensor_tensor(Fb[:, 0:T, :], eq[:, 0], eq[:, 1], ALU.add).then_inc(f_done, 1)
            for k in range(2):
                link(nc.vector.tensor_tensor(wq2[:, k], eq[:, k], w2[:, :, k:k + 1].broadcast_to([P, T, E]), ALU.mult))
            link(nc.vector.tensor_tensor(Wt[:, :, :], wq2[:, 0], wq2[:, 1], ALU.add))
            link(nc.vector.tensor_copy(W3[:, :, 0, :], Wt[:, :, :]))
            link(nc.vector.tensor_tensor(Wr[:, :, :], Wt[:, :, :], W3[:, :, 0, :], ALU.subtract))
            link(nc.vector.tensor_copy(W3[:, :, 1, :], Wr[:, :, :]))
            link(nc.vector.tensor_tensor(W3[:, :, 2, :], Wr[:, :, :], W3[:, :, 1, :], ALU.subtract))
            dve.wait_ge(f_done, 1)
            link(nc.vector.tensor_scalar(slot[:, :, :], Fb[:, 0:T, :], -2.0 * B * L, 2.0 * B * L, ALU.mult, ALU.add))
            dve.wait_ge(slot_mm, 1)
            pl = MPS[:, 0:(T + 1) * E].rearrange("p (t e) -> p t e", e=E)
            link(nc.vector.tensor_tensor(slot[:, :, :], slot[:, :, :], pl[:, 0:T, :], ALU.add))
            link(nc.vector.reduce_max(cnt[:, :], pl[:, T, :], AX.X))
            link(nc.vector.tensor_scalar(cnt[:, :], cnt[:, :], float(CAP - 1), float(CAP), ALU.add, ALU.max))
            link(nc.vector.tensor_copy(cnt_i[:, :], cnt[:, :]))
            nc.vector.tensor_scalar(cnt_i[:, :], cnt_i[:, :], 6, None, ALU.logical_shift_right).then_inc(cnt_done, 1)
            link(nc.vector.tensor_copy(XS[:, 0], XN2[:, :, :]))
            link(nc.vector.tensor_tensor(xs_r[:, :, :], XN2[:, :, :], XS[:, 0], ALU.subtract))
            link(nc.vector.tensor_copy(XS[:, 1], xs_r[:, :, :]))
            nc.vector.tensor_tensor(XS[:, 2], xs_r[:, :, :], XS[:, 1], ALU.subtract).then_inc(xs_done, 1)
            dve.wait_ge(cnt_done, 1)
            dve.wait_ge(d_ew, 80)
            rounds = dve.value_load(cnt_i[0:1, 0:1], min_val=1, max_val=B * L // CAP)
            with dve.Fori(0, rounds) as r:
                for t in range(T):
                    nc.vector.tensor_tensor(G[:, t, :].rearrange("p (e s) -> p e s", e=E),
                                            slot[:, t, :].unsqueeze(2).broadcast_to([P, E, CAP]),
                                            slot_iota[:, :].unsqueeze(1).broadcast_to([P, E, CAP]), ALU.is_equal).then_inc(g_done, 1)
                for n in range(T // 2):
                    if n % 2 == 1:
                        dve.wait_ge(gt_tr, r * (T // 2) + n + 1)
                        nc.vector.tensor_copy(GT[:, 2 * n:2 * n + 2, :, :].rearrange("p t c n -> p (t c n)"),
                                              PTP[1][:, :].bitcast(BF16)).then_inc(gt_ev2, 1)
                dve.wait_ge(g_done, r * T + T)
                nc.vector.tensor_scalar(slot[:, :, :], slot[:, :, :], -float(CAP), None, ALU.add).then_inc(slot_next, 1)
                dve.wait_ge(ws_mm, r + 1)
                nc.vector.reduce_sum(wsr[:, :, :], MPS[:, 0:SCH * 3 * E].rearrange("p (c s e) -> p c e s", c=SCH, s=3), AX.X).then_inc(wsr_done, 1)
                dve.wait_ge(wsr_done, r + 1)
                flat = wsr[:, :, :].rearrange("p c e -> p (c e)")
                for u in range(2):
                    nc.vector.tensor_copy(wsl[u * CAP:(u + 1) * CAP, :],
                                          flat[u * CAP:(u + 1) * CAP, u:u + (SCH - 1) * (E + 2) + 1:E + 2]).then_inc(wsl_done, 1)
                for c in range(SCH):
                    dve.wait_ge(eh_mm, r * SCH + c + 1)
                    if c >= 2:
                        dve.wait_ge(he_done, r * SCH + c - 1)
                    nc.vector.tensor_tensor(hb[:, c % 2], SPS[c][:, :].rearrange("p (u f s) -> p u f s", u=2, f=FC),
                                            ebi[:, 2 * c:2 * c + 2, :].unsqueeze(3).broadcast_to([P, 2, FC, CAP]), ALU.add).then_inc(hb_done, 1)
                    dve.wait_ge(hb_done, r * SCH + c + 1)
                    nc.vector.tensor_scalar(hr[:, c % 2], hb[:, c % 2], -SELU_ALPHA, -SELU_ALPHA, ALU.add, ALU.max).then_inc(hr_done, 1)
                    dve.wait_ge(hr_done, r * SCH + c + 1)
                    dve.wait_ge(he_done, r * SCH + c + 1)
                    nc.vector.scalar_tensor_tensor(out=SE[:, c], in0=he[:, c % 2], scalar=SELU_ALPHA, in1=hr[:, c % 2],
                                                   op0=ALU.min, op1=ALU.add).then_inc(se_done, 1)
                dve.wait_ge(y_mm, r + 1)
                nc.vector.scalar_tensor_tensor(out=Y1[:, :, :], in0=OPS[:, :].rearrange("p (c h) -> p c h", c=SCH), scalar=SELU_SCALE,
                                               in1=ebo[:, :, :], op0=ALU.mult, op1=ALU.add).then_inc(y1_done, 1)
                dve.wait_ge(y1_done, r + 1)
                dve.wait_ge(wsl_done, 2 * r + 2)
                nc.vector.tensor_tensor(Y[:, :, :], Y1[:, :, :], wsl[:, :].unsqueeze(2).broadcast_to([P, SCH, D]), ALU.mult).then_inc(yw_done, 1)
                dve.wait_ge(yw_done, r + 1)
                nc.vector.tensor_copy(Y3[:, 0], Y[:, :, :]).then_inc(ya_done, 1)
                dve.wait_ge(ya_done, r + 1)
                nc.vector.tensor_tensor(Y1[:, :, :], Y[:, :, :], Y3[:, 0], ALU.subtract).then_inc(yb_done, 1)
                dve.wait_ge(yb_done, r + 1)
                nc.vector.tensor_copy(Y3[:, 1], Y1[:, :, :]).then_inc(yc_done, 1)
                dve.wait_ge(yc_done, r + 1)
                nc.vector.tensor_tensor(Y3[:, 2], Y1[:, :, :], Y3[:, 1], ALU.subtract).then_inc(y3_done, 1)
                for g in range(NG):
                    dve.wait_ge(sc_mm, r * NG + g + 1)
                    xg_ = X[:, TG * g:TG * (g + 1), :].rearrange("p t h -> p (t h)")
                    nc.vector.tensor_tensor(xg_, xg_, SPS[g][:, :], ALU.add).then_inc(acc_done, 1)
                dve.wait_ge(acc_done, r * NG + NG)
            nc.vector.memset(cnt[:, :], 0.0).then_inc(gw_done, 1)

        @block.tensor
        def _(pe):
            mm, tr = nc.tensor.matmul, nc.tensor.transpose

            def ctx_transposes(g):
                pe.wait_ge(d_cx[g], 16)
                if g >= 2:
                    pe.wait_ge(ct_ev, g - 1)
                for u in range(TG):
                    last = tr(PTP[g % 2][:, u * P:(u + 1) * P], CX[:, TG * g + u, :], ident[:, :])
                last.then_inc(ct_tr, 1)

            def project_kv(g):
                pe.wait_ge(ct_ev, g + 1)
                if g >= 2:
                    pe.wait_ge(k_full, g - 1)
                mm(SPS[g % 2][:, :], w_att[:, 1, :], CT[:, g % 2, :], start=True, stop=True).then_inc(k_mm, 1)
                if g >= 2:
                    pe.wait_ge(v_top, g - 1)
                    pe.wait_ge(v_bot, g - 1)
                wv = w_att[:, 2, :].rearrange("p (c h d) -> p h c d", h=2, d=HD)
                for b in range(BG):
                    for h2 in range(2):
                        last = mm((OPS, MPS)[g % 2][h2 * L:(h2 + 1) * L, b * L:(b + 1) * L],
                                  CT[:, g % 2, b * L:(b + 1) * L], wv[:, h2], start=True, stop=True)
                last.then_inc(v_mm, 1)

            pe.wait_ge(pool_const, 1)
            ctx_transposes(0)
            ctx_transposes(1)
            pe.wait_ge(d_watt, 64)
            for g in range(NG):
                project_kv(g)
                if g + 2 < NG:
                    ctx_transposes(g + 2)

            def x_transposes(g):
                pe.wait_ge(xn_done, g + 1)
                pe.wait_ge(ct_ev, NG)
                if g >= 2:
                    pe.wait_ge(xt_ev, g - 1)
                for u in range(TG):
                    last = tr(PTP[g % 2][:, u * P:(u + 1) * P], XN[:, g % 2, u, :], ident[:, :])
                last.then_inc(xt_tr, 1)

            def project_q(g):
                pe.wait_ge(xt_ev, g + 1)
                if g >= 2:
                    pe.wait_ge(q_full, g - 1)
                mm(SPS[2 + g % 2][:, :], w_att[:, 0, :], XT[:, g % 2, :], start=True, stop=True).then_inc(q_mm, 1)

            x_transposes(0)
            x_transposes(1)
            for g in range(NG):
                project_q(g)
                if g + 2 < NG:
                    x_transposes(g + 2)

            def scores(t):
                g, two = t // TG, 2 * (t % 2)
                if t == 0:
                    pe.wait_ge(bd_ready, 1)
                    pe.wait_ge(k_full, NG)
                    pe.wait_ge(q_full, NG)
                if t >= 2:
                    pe.wait_ge(sub_done, t - 1)
                for ih in range(2):
                    for s in range(3):
                        mm(SPS[two + ih][:, :], ones1[0:1, :],
                           base3[0:1, s, :].unsqueeze(2).broadcast_to([1, H, L // 2]), start=(s == 0), stop=False, skip_group_check=True)
                pe.wait_ge(oh_done, t + 1)
                for i in range(IB):
                    ih, i8_ = i // 8, i % 8
                    o = SPS[two + ih][:, :].rearrange("p (h i j) -> p i h j", h=H, i=8)[:, i8_]
                    for s in range(3):
                        mm(o, OH[:, t % 2, i * P:(i + 1) * P], BD[:, s], start=False, stop=False, skip_group_check=True)
                if t % TG == 0:
                    for s in "qk":
                        pe.wait_ge(d_stack[s][g % 2], 16 * 2 * NPR * (g // 2 + 1))
                for b2 in range(2):
                    q0 = (t % TG) * P + b2 * L
                    for c in range(HP):
                        for ih in range(2):
                            last = mm(SPS[two + ih][b2 * L:(b2 + 1) * L, c * L:(c + 1) * L],
                                      QS[:, g % 2, c, q0:q0 + L],
                                      KS[:, g % 2, c, :, q0 + ih * (L // 2):q0 + (ih + 1) * (L // 2)],
                                      start=False, stop=True, skip_group_check=True)
                last.then_inc(s_mm, 1)

            def p_transposes(t):
                pe.wait_ge(exp_done, t + 1)
                for half in range(2):
                    if t >= 1:
                        pe.wait_ge(pt_ev, 2 * (t - 1) + half + 1)
                    for c in range(4):
                        cc = 4 * half + c
                        last = tr(PTP[half][:, c * P:(c + 1) * P], PR[:, t % 2, 2 * cc:2 * cc + 2, :].rearrange("p h k -> p (h k)"), ident[:, :])
                    last.then_inc(p_tr, 1)

            def p_v(t):
                if t >= 1:
                    pe.wait_ge(ao_done, t)
                else:
                    pe.wait_ge(v_top, NG)
                    pe.wait_ge(v_bot, NG)
                for c in range(HP):
                    if c % 4 == 0:
                        pe.wait_ge(pt_ev, 2 * t + c // 4 + 1)
                    for b2 in range(2):
                        last = mm(OPS[b2 * L:(b2 + 1) * L, c * VW:(c + 1) * VW], PT[:, t % 2, c, b2 * L:(b2 + 1) * L],
                                  VD[:, 2 * t + b2, c, :], start=True, stop=True)
                last.then_inc(pv_mm, 1)

            def ao_transpose(t):
                pe.wait_ge(ao_done, t + 1)
                if t >= 1:
                    pe.wait_ge(x2_done, t)
                tr(MPS[:, 0:P], AO[:, t % 2, :], ident[:, :]).then_inc(ao_tr, 1)

            def out_project(t):
                pe.wait_ge(aot_ev, t + 1)
                mm(MPS[:, P:2 * P], AOT[:, t % 2, :], w_att[:, 3, :], start=True, stop=True).then_inc(wo_mm, 1)

            scores(0)
            for t in range(T):
                if t + 1 < T:
                    scores(t + 1)
                p_transposes(t)
                if t >= 1:
                    ao_transpose(t - 1)
                p_v(t)
                if t >= 1:
                    out_project(t - 1)
            ao_transpose(T - 1)
            out_project(T - 1)

            def n2_transposes(g):
                pe.wait_ge(n2_done, g + 1)
                if g >= 2:
                    pe.wait_ge(n2_ev, g - 1)
                for u in range(TG):
                    last = tr(PTP[g % 2][:, u * P:(u + 1) * P], XN2[:, TG * g + u, :], ident[:, :])
                last.then_inc(n2_tr, 1)

            def logits(g):
                pe.wait_ge(sg_done, FC * (g + 1))
                if g >= 2:
                    pe.wait_ge(lg_ev, g - 1)
                o = (OPS, MPS)[g % 2]
                for u in range(TG):
                    for c in range(FC):
                        mm(o[:, u * D:(u + 1) * D], SG[:, g % 2, c, u * P:(u + 1) * P], w_go[:, c, :], start=(c == 0), stop=False)
                    last = mm(o[:, u * D:(u + 1) * D], ones_row[0:1, :], gbo_row[0:1, :], start=False, stop=True)
                last.then_inc(lg_mm, 1)

            pe.wait_ge(pt_ev, 2 * T)
            pe.wait_ge(x2_done, T)
            pe.wait_ge(pool_const, 5)
            n2_transposes(0)
            for g in range(NG):
                if g + 1 < NG:
                    n2_transposes(g + 1)
                pe.wait_ge(n2_ev, g + 1)
                for c in range(FC):
                    n = FC * g + c
                    if n >= 4:
                        pe.wait_ge(sg_done, n - 3)
                    mm(SPS[n % 4][:, :], w_gi[:, c * P:(c + 1) * P], XN2T[:, GTOK * g:GTOK * (g + 1)], start=True, stop=True).then_inc(h_mm, 1)
                if g >= 1:
                    logits(g - 1)
            logits(NG - 1)
            pe.wait_ge(f_done, 1)
            pe.wait_ge(lg_ev, NG)
            for t in range(T):
                mm(MPS[:, (t + 1) * E:(T + 1) * E], ones_bf[:, :], Fb[:, t:t + 1, :].broadcast_to([P, T - t, E]),
                   start=(t == 0), stop=False, skip_group_check=True)
            mm(MPS[:, 0:(T + 1) * E], lower[:, :], Fb[:, :, :].rearrange("p t e -> p (t e)"),
               start=False, stop=True, skip_group_check=True).then_inc(slot_mm, 1)
            pe.wait_ge(xs_done, 1)
            pe.wait_ge(cnt_done, 1)
            pe.wait_ge(d_ew, 80)
            rounds = pe.value_load(cnt_i[0:1, 0:1], min_val=1, max_val=B * L // CAP)
            with pe.Fori(0, rounds) as r:
                for t in range(T):
                    pe.wait_ge(g_done, r * T + t + 1)
                    for s in range(3):
                        last = mm(OPS[:, :], XS[:, s, t, :], G[:, t, :], start=(t == 0 and s == 0), stop=(t == T - 1 and s == 2))
                last.then_inc(xg_mm, 1)
                for c in range(SCH):
                    for t in range(T):
                        last = mm(MPS[:, c * 3 * E:(c + 1) * 3 * E], G[:, t, c * P:(c + 1) * P],
                                  W3[:, t].rearrange("p s e -> p (s e)"), start=(t == 0), stop=(t == T - 1))
                last.then_inc(ws_mm, 1)
                for n in range(T // 2):
                    if n >= 2:
                        if n % 2 == 0:
                            pe.wait_ge(gt_ev, r * (T // 4) + n // 2)
                        else:
                            pe.wait_ge(gt_ev2, r * (T // 4) + n // 2)
                    pb = PTP[n % 2][:, :].bitcast(BF16)
                    for u in range(2):
                        for c in range(SCH):
                            o = (u * SCH + c) * P
                            last = tr(pb[:, o:o + P], G[:, 2 * n + u, c * P:(c + 1) * P], ident_bf[:, :])
                    last.then_inc(gt_tr, 1)
                pe.wait_ge(xg_ev, r + 1)
                for c in range(SCH):
                    for u in range(2):
                        for f in range(FC):
                            e = 2 * c + u
                            o = (u * FC + f) * CAP
                            last = mm(SPS[c][:, o:o + CAP], w_ei[:, e, f * P:(f + 1) * P], XG[:, e * CAP:(e + 1) * CAP], start=True, stop=True)
                    last.then_inc(eh_mm, 1)
                for c in range(SCH):
                    pe.wait_ge(se_done, r * SCH + c + 1)
                    for u in range(2):
                        for f in range(FC):
                            last = mm(OPS[u * CAP:(u + 1) * CAP, c * D:(c + 1) * D], SE[:, c, u, f, :], w_eo[:, 2 * c + u, f, :],
                                      start=(f == 0), stop=(f == FC - 1))
                last.then_inc(y_mm, 1)
                pe.wait_ge(gt_ev, r * (T // 4) + T // 4)
                pe.wait_ge(gt_ev2, r * (T // 4) + T // 4)
                pe.wait_ge(y3_done, r + 1)
                for g in range(NG):
                    for u in range(TG):
                        t = TG * g + u
                        for c in range(SCH):
                            for s in range(3):
                                last = mm(SPS[g][:, u * D:(u + 1) * D], GT[:, t, c, :], Y3[:, s, c, :],
                                          start=(c == 0 and s == 0), stop=(c == SCH - 1 and s == 2))
                    last.then_inc(sc_mm, 1)


_INS = ['x', 'ctx_1024', 'fside_BxSx3_0', 'L0_xattn_Wq', 'L0_xattn_bq', 'L0_xattn_Wk', 'L0_xattn_bk', 'L0_xattn_Wv',
        'L0_xattn_bv', 'L0_xattn_Wo', 'L0_xattn_bo', 'L0_xattn_dist_emb', 'L0_ffn_gate_wi', 'L0_ffn_gate_bi',
        'L0_ffn_gate_wo', 'L0_ffn_gate_bo', 'L0_ffn_exp_wi', 'L0_ffn_exp_bi', 'L0_ffn_exp_wo', 'L0_ffn_exp_bo']


def kernel(**inputs):
    import numpy as _np
    import concourse.bacc as _bacc
    from concourse import mybir as _mybir
    from concourse.bass_utils import run_bass_kernel_spmd as _run

    nc = _bacc.Bacc("TRN2", target_bir_lowering=False, num_devices=1)
    arrays, args = {}, []
    for name in _INS:
        a = _np.ascontiguousarray(inputs[name])
        arrays[f"in_{name}_dram"] = a
        args.append(nc.dram_tensor(f"in_{name}_dram", a.shape, _mybir.dt.from_np(a.dtype), kind="ExternalInput").ap())
    out = nc.dram_tensor("out_dram", inputs['x'].shape, _mybir.dt.float32, kind="ExternalOutput").ap()
    build(nc, *args, out)
    r = _run(nc, [arrays], core_ids=[0])
    return r.results[0]["out_dram"]
```

```python
from contextlib import ExitStack

import numpy as np
import concourse.bass as bass
from concourse import mybir

F32 = mybir.dt.float32
BF16 = mybir.dt.bfloat16
I32 = mybir.dt.int32
U32 = mybir.dt.uint32
ALU = mybir.AluOpType
ACT = mybir.ActivationFunctionType
AX = mybir.AxisListType

P = 128
SELU_ALPHA = 1.6732632423543772
SELU_SCALE = 1.0507009873554805
EPS = 1e-5
TWO_ONES = float(np.array([0x3F803F80], np.uint32).view(np.float32)[0])
MAX_DIST = 5.0
CAND = 32
CAP = 128
PRODUCTS = [(0, 0), (0, 1), (0, 2), (1, 0), (1, 1), (2, 0)]


def build(nc, x, ctx_in, pos, Wq, bq, Wk, bk, Wv, bv, Wo, bo, emb, g_wi, g_bi, g_wo, g_bo, e_wi, e_bi, e_wo, e_bo, out):
    B, L, D = x.shape
    BINS1, H = emb.shape
    NB = BINS1 - 1
    HD = D // H
    T = B * L // P
    F = g_wi.shape[1]
    FC = F // P
    E = e_wi.shape[0]
    NG = 4
    TG = T // NG
    GTOK = TG * P
    BG = GTOK // L
    JB = P // NB
    IB = L // JB
    HP = H // 2
    NPR = len(PRODUCTS)
    PR_ROWS = 2 * NPR * HD
    BR = 2 * 3
    KR = PR_ROWS + BR
    VW = 2 * HD + 2
    SC = HD ** -0.5
    SLOTS = E * CAP
    NC = T * CAND // P
    XWW = 3 * D + 4 * E
    MAXRI = T * CAND // CAP
    assert (L, D, NB, HD, P // CAND, CAP) == (64, P, 32, 8, TG, P)

    st = ExitStack()
    with st:
        def dram(name, shape, dt):
            return nc.dram_tensor(name, shape, dt, kind="Internal").ap()

        def sb(name, shape, dt, where=st):
            return where.enter_context(nc.sbuf_tensor(name, shape, dt))

        def sem(name):
            return st.enter_context(nc.semaphore(name))

        part_dram = {s: dram(f"part_dram_{s}", [P, NPR, B * L], BF16) for s in "qk"}
        bins_dram = dram("bins_dram", [T, JB, IB, 2, L], BF16)

        X = sb("X", [P, T, D], F32)
        ident = sb("ident", [P, P], F32)
        ident_bf = sb("ident_bf", [P, P], BF16)
        lower = sb("lower", [P, P], BF16)
        ones_bf = sb("ones_bf", [P, P], BF16)
        ones_row = sb("ones_row", [1, P], F32)
        stats = sb("stats", [P, T, 6], F32)
        mv = sb("mv", [P, T, 2], F32)
        rstd = sb("rstd", [P, T], F32)
        w_gi = sb("w_gi", [P, F], F32)
        w_go = sb("w_go", [P, FC, D], F32)
        gb_exp = sb("gb_exp", [P, FC], F32)
        gb_lin = sb("gb_lin", [P, FC], F32)
        gbi = sb("gbi", [P, FC], F32)
        gbo_b = sb("gbo_b", [P, D], F32)
        w_ei = sb("w_ei", [P, E, F], F32)
        w_eo = sb("w_eo", [P, E, FC, D], F32)
        ebi = sb("ebi", [P, E, FC], F32)
        ebo = sb("ebo", [P, E, D], F32)
        slot_iota = sb("slot_iota", [P, CAP], F32)
        XN2 = sb("XN2", [P, T, D], F32)
        XW = sb("XW", [P, T, XWW], BF16)
        x2r = sb("x2r", [P, TG, D], F32)
        exp_iota = sb("exp_iota", [P, E], F32)
        half_neg = sb("half_neg", [P, T], F32)
        vare = sb("vare", [P, T], F32)
        lnalpha = sb("lnalpha", [P, 1], F32)

        ab = ExitStack()
        posq = sb("posq", [P, T, 3], F32, ab)
        CX = sb("CX", [P, T, D], F32, ab)
        XN = sb("XN", [P, 2, TG, D], F32, ab)
        XCT = sb("XCT", [P, 4, GTOK], F32, ab)
        XT, CT = XCT[:, 0:2, :], XCT[:, 2:4, :]
        w_q = sb("w_q", [P, D], F32, ab)
        w_att = sb("w_att", [P, 4, D], F32, ab)
        bcols = sb("bcols", [P, 4], F32, ab)
        bo_b = sb("bo_b", [P, D], F32, ab)
        KS = sb("KS", [KR, 2, HP, 2, GTOK], BF16, ab)
        QS = sb("QS", [KR, 2, HP, GTOK], BF16, ab)
        rest = sb("rest", [P, GTOK], F32, ab)
        parts = {s: sb(f"parts_{s}", [P, 2, 3, GTOK], BF16, ab) for s in "qk"}
        VD = sb("VD", [P, B, HP, VW], F32, ab)
        BB = sb("BB", [P, 4, IB * P], BF16, ab)
        OH = sb("OH", [P, 2, IB * P], BF16, ab)
        bin_id = sb("bin_id", [P, 1], F32, ab)
        tab = sb("tab", [P, H], F32, ab)
        tab_last = sb("tab_last", [P, H], F32, ab)
        tab_r = sb("tab_r", [P, H], F32, ab)
        tab_h = sb("tab_h", [P, 3, H], BF16, ab)
        BD = sb("BD", [P, 3, H, JB], BF16, ab)
        base_f = sb("base_f", [KR, 2, 2, HP], F32, ab)[PR_ROWS:KR]
        base_s = sb("base_s", [KR, 3, 2, HP], BF16, ab)[PR_ROWS:KR]
        base_m = sb("base_m", [KR, HP], F32, ab)[PR_ROWS:KR]
        PR = CX[:, :, :].rearrange("p (a t) (h k) -> p a (t h) k", a=2, k=L)
        PT = XCT[:, :, :].rearrange("p (a b) (c n) -> p a (b c) n", a=2, n=P)
        mxp = sb("mxp", [P, 2, H], F32, ab)
        mx = sb("mx", [P, H], F32, ab)
        rsum = sb("rsum", [P, H], F32, ab)
        AO = sb("AO", [P, 2, D], F32, ab)
        AOT = sb("AOT", [P, 2, P], F32, ab)
        wf = w_ei[:, :, :].rearrange("p e f -> p (e f)")
        wf2 = w_eo[:, :, :, :].rearrange("p e c h -> p (e c h)")
        posk = wf[:, 0:T * L * 3].rearrange("p (t k c) -> p t k c", t=T, c=3)
        df = wf2[:, 0:T * L * 3].rearrange("p (t k c) -> p t k c", t=T, c=3)
        d2 = wf[:, T * L * 3:T * L * 4].rearrange("p (t k) -> p t k", t=T)
        rt, sm = df[:, :, :, 0], df[:, :, :, 1]
        dv = wf2[:, T * L * 3:T * L * 4].rearrange("p (t k) -> p t k", t=T)
        binv = sb("binv", [P, T, L], BF16, ab)
        ab.close()

        XN2T = sb("XN2T", [P, T * P], F32)
        SG = sb("SG", [P, 2, FC, GTOK], F32)
        GE = sb("GE", [P, 2, GTOK], F32)
        GR = sb("GR", [P, 2, GTOK], F32)
        LG = sb("LG", [P, TG, D], F32)
        v8 = sb("v8", [P, T, 8], F32)
        i8 = sb("i8", [P, T, 8], U32)
        i2f = sb("i2f", [P, T, 2], F32)
        vs = sb("vs", [P, T], F32)
        w2 = sb("w2", [P, T, 2], F32)
        eq = sb("eq", [P, 2, T, E], F32)
        we = sb("we", [P, 2, T, E], F32)
        Wt = sb("Wt", [P, T, E], F32)
        Wr = sb("Wr", [P, T, E], F32)
        Ub = sb("Ub", [P, T], BF16)
        rank = sb("rank", [P, T], F32)
        cnt = sb("cnt", [P, E + 2], F32)
        cnt_i = sb("cnt_i", [P, 2], I32)
        G1 = sb("G1", [P, T, P], BF16)
        GT1 = sb("GT1", [P, T, P], BF16)
        XC = sb("XC", [P, NC, XWW], BF16)
        slot = sb("slot", [P, NC, E], F32)
        OC = sb("OC", [P, NC, D], F32)
        OCr = sb("OCr", [P, NC, D], F32)
        OC3 = sb("OC3", [P, 3, NC, D], BF16)
        G2 = sb("G2", [P, NC, SLOTS], BF16)
        GT2 = sb("GT2", [P, NC, E, P], BF16)
        XG = sb("XG", [P, SLOTS], F32)
        he = sb("he", [P, 2, FC, CAP], F32)
        hr = sb("hr", [P, 2, FC, CAP], F32)
        SE = sb("SE", [P, E, FC, CAP], F32)
        eb_exp = sb("eb_exp", [P, E, FC], F32)
        eb_lin = sb("eb_lin", [P, E, FC], F32)
        wsl = sb("wsl", [P, E], F32)
        Y1 = sb("Y1", [P, E, D], F32)
        Y = sb("Y", [P, E, D], F32)
        Y3 = sb("Y3", [P, 3, E, D], BF16)

        bank = [st.enter_context(nc.psum_tensor(f"bank{i}", [P, 512], F32)) for i in range(8)]
        SPS = [bank[0], bank[1], bank[2], bank[3]]
        PTP = [bank[4], bank[5]]
        OPS, MPS = bank[6], bank[7]

        d_pos, bins_done, d_binw, oh_done, q_parts, k_parts, s_mm, pool_const = map(sem, (
            "d_pos", "bins_done", "d_binw", "oh_done", "q_parts", "k_parts", "s_mm", "pool_const"))
        pool_c, out_ready, d_out, var_done, rstd_done, d_small, xn_done, xb_done = map(sem, (
            "pool_c", "out_ready", "d_out", "var_done", "rstd_done", "d_small", "xn_done", "xb_done"))
        var2_done, rstd2_done, d_watt, d_tab, ct_tr, k_mm, v_mm, ct_ev = map(sem, (
            "var2_done", "rstd2_done", "d_watt", "d_tab", "ct_tr", "k_mm", "v_mm", "ct_ev"))
        k_hi, v_ev, xt_tr, q_mm, xt_ev, q_hi, bcol_ready, df_done = map(sem, (
            "k_hi", "v_ev", "xt_tr", "q_mm", "xt_ev", "q_hi", "bcol_ready", "df_done"))
        f_done, sq_done, d2_clamped, sqrt_done, near_done, edge_done, ge_done, d_gate = map(sem, (
            "f_done", "sq_done", "d2_clamped", "sqrt_done", "near_done", "edge_done", "ge_done", "d_gate"))
        d_ew, ao_tr, wo_mm, aot_ev, sub_done, exp_done, pv_mm, p_tr = map(sem, (
            "d_ew", "ao_tr", "wo_mm", "aot_ev", "sub_done", "exp_done", "pv_mm", "p_tr"))
        pt_ev, n2_tr, n2_ev, consts2, h_mm, sg_done, cnt_done, xc_mm = map(sem, (
            "pt_ev", "n2_tr", "n2_ev", "consts2", "h_mm", "sg_done", "cnt_done", "xc_mm"))
        xc_ev_a, g1_tr, gt1_ev_a, xg_mm, xg_ev, g2_tr, gt2_ev, eh_mm = map(sem, (
            "xc_ev_a", "g1_tr", "gt1_ev_a", "xg_mm", "xg_ev", "g2_tr", "gt2_ev", "eh_mm"))
        se_done, he_done, dve_c, bd_zero, wq_scaled, k_r, q_r, bd_ready = map(sem, (
            "se_done", "he_done", "dve_c", "bd_zero", "wq_scaled", "k_r", "q_r", "bd_ready"))
        x2_done, mv2_done, n2_done, ao_done, lg_mm, lg_ev, rank_mm, cnt_half = map(sem, (
            "x2_done", "mv2_done", "n2_done", "ao_done", "lg_mm", "lg_ev", "rank_mm", "cnt_half"))
        dve_outer, g1_done, xc_ev_v, slot_mm, gt1_ev_v, dve_inner, g2_done, ws_mm = map(sem, (
            "dve_outer", "g1_done", "xc_ev_v", "slot_mm", "gt1_ev_v", "dve_inner", "g2_done", "ws_mm"))
        wsl_done, hr_done, y_mm, y1_done, yb_done, y3_done, sc_mm, oc3_done = map(sem, (
            "wsl_done", "hr_done", "y_mm", "y1_done", "yb_done", "y3_done", "sc_mm", "oc3_done"))
        back_mm, d_watt2, d_bo, base_ready, base_rows = map(sem, (
            "back_mm", "d_watt2", "d_bo", "base_ready", "base_rows"))
        d_cx = [sem(f"d_cx{g}") for g in range(NG)]
        d_x = [sem(f"d_x{g}") for g in range(NG)]
        d_bb = [sem(f"d_bb{i}") for i in range(4)]
        d_part = {s: [sem(f"d_{s}part{i}") for i in range(2)] for s in "qk"}
        d_stack = {s: [sem(f"d_{s}stack{i}") for i in range(2)] for s in "qk"}
        STORES = 3
        STACKS = {"k": 2, "q": 1}

        def chain(eng, s, first=0):
            n = [0]

            def link(ins):
                n[0] += 1
                ins.then_inc(s, 1)
                eng.wait_ge(s, first + n[0])
            return link, n

        xt_dram = x.rearrange("b l d -> (b l) d").rearrange("(t p) d -> p t d", p=P)
        cx_dram = ctx_in.rearrange("b l d -> (b l) d").rearrange("(t p) d -> p t d", p=P)
        out_dram = out.rearrange("b l d -> (b l) d").rearrange("(t p) d -> p t d", p=P)
        col = lambda v: v.rearrange("(p a) -> p a", a=1)
        row = lambda v: v.rearrange("(a n) -> a n", a=1)
        tiles = lambda g: slice(TG * g, TG * (g + 1))

        block = st.enter_context(nc.Block())

        @block.sync
        def _(sp):
            sp.dma_start(posq[:, :, :], pos.rearrange("b l c -> (b l) c").rearrange("(t p) c -> p t c", p=P)).then_inc(d_pos, 16)
            for b2 in range(2):
                src = pos.rearrange("(t b) k c -> b t (k c)", b=2)[b2:b2 + 1]
                sp.dma_start(posk[b2 * L:(b2 + 1) * L].rearrange("p t k c -> p t (k c)"),
                             src.broadcast_to([L, T, L * 3])).then_inc(d_pos, 16)
            for g in range(NG):
                sp.dma_start(X[:, tiles(g), :], xt_dram[:, tiles(g), :]).then_inc(d_x[g], 16)

            def store_bins():
                sp.wait_ge(bins_done, 1)
                for b2 in range(2):
                    sp.dma_start(bins_dram[:, :, :, b2, :].rearrange("t j i m -> (j i) t m"), binv[b2 * L:(b2 + 1) * L, :, :]).then_inc(d_binw, 16)
                sp.wait_ge(d_binw, 32)

            def spread_bins(t):
                if t >= 4:
                    sp.wait_ge(oh_done, t - 3)
                sp.dma_start(BB[:, t % 4, :], bins_dram[t].rearrange("j i b m -> j (i b m)").unsqueeze(1).broadcast_to([JB, NB, IB * P])
                             ).then_inc(d_bb[t % 4], 16)

            def store_parts(s, g):
                sp.wait_ge({"q": q_parts, "k": k_parts}[s], g + 1)
                now = slice(GTOK * g, GTOK * (g + 1))
                dst, src = part_dram[s][:, :, now], parts[s][:, g % 2]
                for first, last in ((0, 3), (3, 5), (5, 6)):
                    if s == "k":
                        take = src[:, 0:last - first, :]
                    else:
                        i = PRODUCTS[first][0]
                        take = src[:, i:i + 1, :].broadcast_to([P, last - first, GTOK])
                    sp.dma_start(dst[:, first:last, :], take).then_inc(d_part[s][g % 2], 16)

            def stack_parts(s, g):
                sp.wait_ge(d_part[s][g % 2], 16 * STORES * (g // 2 + 1))
                if g >= 2:
                    sp.wait_ge(s_mm, TG * (g - 1))
                now = slice(GTOK * g, GTOK * (g + 1))
                if s == "q":
                    sp.dma_start(QS[0:PR_ROWS, g % 2], part_dram["q"][:, :, now].rearrange("(c r) n t -> (r n) c t", c=HP)
                                 ).then_inc(d_stack["q"][g % 2], 16)
                    return
                for h2 in range(2):
                    sp.dma_start(KS[h2 * PR_ROWS // 2:(h2 + 1) * PR_ROWS // 2, g % 2, :, h2, :],
                                 part_dram["k"][:, :, now].rearrange("(c h d) n t -> h (d n) c t", h=2, d=HD)[h2]
                                 ).then_inc(d_stack["k"][g % 2], 16)

            sp.wait_ge(pool_const, 2)
            store_parts("k", 0)
            stack_parts("k", 0)
            store_bins()
            spread_bins(0)
            store_parts("q", 0)
            store_parts("k", 1)
            stack_parts("q", 0)
            spread_bins(1)
            stack_parts("k", 1)
            store_parts("q", 1)
            spread_bins(2)
            stack_parts("q", 1)
            spread_bins(3)
            store_parts("k", 2)
            store_parts("q", 2)
            store_parts("k", 3)
            store_parts("q", 3)
            for t in range(4, T):
                if t in (2 * TG, 3 * TG):
                    stack_parts("k", t // TG)
                    stack_parts("q", t // TG)
                spread_bins(t)
            for g in range(NG):
                sp.wait_ge(out_ready, 1)
                sp.dma_start(out_dram[:, tiles(g), :], X[:, tiles(g), :]).then_inc(d_out, 16)
            sp.wait_ge(d_out, 16 * NG)

        @block.gpsimd
        def _(pool):
            link, _n = chain(pool, pool_c)
            link(nc.gpsimd.memset(ident[:, :], 0.0))
            nc.gpsimd.affine_select(out=ident[:, :], in_=ident[:, :], compare_op=ALU.not_equal, fill=1.0,
                                    base=0, pattern=[[-1, P]], channel_multiplier=1).then_inc(pool_const, 1)
            link(nc.gpsimd.memset(KS[:, :, :, :, :].rearrange("p a c h n -> p (a c h n)").bitcast(F32), 0.0))
            last = nc.gpsimd.memset(KS[PR_ROWS:KR, :, :, 1, :].rearrange("p a c n -> p (a c) n").bitcast(F32), TWO_ONES)
            link(last)
            nc.gpsimd.memset(KS[PR_ROWS:PR_ROWS + 3, :, :, 0, :].rearrange("p a c n -> p (a c) n").bitcast(F32), TWO_ONES).then_inc(pool_const, 1)
            pool.wait_ge(pool_const, 2)
            link(nc.gpsimd.memset(VD[:, :, :, :], 0.0))
            link(nc.gpsimd.memset(VD[0:L, :, :, 2 * HD:2 * HD + 1], 1.0))
            nc.gpsimd.memset(VD[L:P, :, :, 2 * HD + 1:VW], 1.0).then_inc(pool_const, 1)
            pool.wait_ge(pool_const, 3)
            for j in range(JB):
                last = nc.gpsimd.iota(bin_id[NB * j:NB * (j + 1), :], [[0, 1]], base=0, channel_multiplier=1, allow_small_or_imprecise_dtypes=True)
            last.then_inc(pool_const, 1)
            pool.wait_ge(pool_const, 4)
            link(nc.gpsimd.memset(half_neg[:, :], -0.5))
            pool.wait_ge(var_done, 1)
            nc.gpsimd.tensor_tensor(rstd[:, :], vare[:, :], half_neg[:, :], ALU.pow).then_inc(rstd_done, 1)
            pool.wait_ge(rstd_done, 1)
            link(nc.gpsimd.memset(lower[:, :], 1.0))
            link(nc.gpsimd.affine_select(out=lower[:, :], in_=lower[:, :], compare_op=ALU.is_gt, fill=0.0,
                                         base=0, pattern=[[1, P]], channel_multiplier=-1))
            link(nc.gpsimd.memset(ones_bf[:, :], 1.0))
            link(nc.gpsimd.iota(slot_iota[:, :], [[1, CAP]], base=0, channel_multiplier=0, allow_small_or_imprecise_dtypes=True))
            link(nc.gpsimd.iota(exp_iota[:, :], [[1, E]], base=0, channel_multiplier=0, allow_small_or_imprecise_dtypes=True))
            nc.gpsimd.tensor_copy(ident_bf[:, :], ident[:, :]).then_inc(pool_const, 1)
            pool.wait_ge(pool_const, 5)
            pool.wait_ge(d_bo, 16)
            pool.wait_ge(xn_done, NG)
            nc.gpsimd.tensor_tensor(X[:, :, :], X[:, :, :], bo_b[:, :].unsqueeze(1).broadcast_to([P, T, D]), ALU.add).then_inc(xb_done, 1)
            pool.wait_ge(xb_done, 1)
            for g in range(NG):
                pool.wait_ge(var2_done, g + 1)
                nc.gpsimd.tensor_tensor(rstd[:, tiles(g)], vare[:, tiles(g)], half_neg[:, tiles(g)], ALU.pow).then_inc(rstd2_done, 1)

        @block.scalar
        def _(act):
            act.dma_start(tab[:, :], emb[0:NB, :].unsqueeze(0).broadcast_to([JB, NB, H])).then_inc(d_tab, 16)
            act.dma_start(tab_last[:, :], emb[NB:NB + 1, :].broadcast_to([P, H])).then_inc(d_tab, 16)
            act.dma_start(base_f[:, 0].rearrange("p h c -> p (h c)"), emb[NB:NB + 1, :].broadcast_to([BR, H])).then_inc(d_tab, 16)
            for g in range(NG):
                act.dma_start(CX[:, tiles(g), :], cx_dram[:, tiles(g), :]).then_inc(d_cx[g], 16)
                if g == 0:
                    for i, w in ((1, Wk), (2, Wv)):
                        act.dma_start(w_att[:, i, :], w).then_inc(d_watt, 16)
                    for i, v in enumerate((bq, bk, bv)):
                        act.dma_start(bcols[:, i:i + 1], col(v)).then_inc(d_small, 16)
            for i, w in ((0, Wq), (3, Wo)):
                act.dma_start(w_att[:, i, :], w).then_inc(d_watt2, 16)
            act.dma_start(bo_b[:, :], row(bo).broadcast_to([P, D])).then_inc(d_bo, 16)

            def base_values(a):
                nc.scalar.activation(QS[PR_ROWS:KR, a, :, :], base_m[:, :].unsqueeze(2).broadcast_to([BR, HP, GTOK]), ACT.Copy).then_inc(base_rows, 1)

            def evac_ct(g):
                act.wait_ge(ct_tr, g + 1)
                if g >= 2:
                    act.wait_ge(k_mm, g - 1)
                    act.wait_ge(v_mm, g - 1)
                nc.scalar.activation(CT[:, g % 2, :].rearrange("p (b i j) -> p b i j", b=BG, j=JB),
                                     PTP[g % 2][:, :].rearrange("p (b j i) -> p b i j", b=BG, j=JB), ACT.Copy).then_inc(ct_ev, 1)

            def k_first(g):
                act.wait_ge(k_mm, g + 1)
                if g >= 2:
                    act.wait_ge(d_part["k"][g % 2], 16 * STORES * (g // 2))
                nc.scalar.activation(parts["k"][:, g % 2, 0, :], bank[g][:, :], ACT.Identity, bias=bcols[:, 1:2]).then_inc(k_hi, 1)

            def values(g):
                act.wait_ge(v_mm, g + 1)
                for h2 in range(2):
                    q = slice(h2 * L, (h2 + 1) * L)
                    nc.scalar.activation(VD[q, BG * g:BG * (g + 1), :, h2 * HD:(h2 + 1) * HD],
                                         (OPS, MPS)[g % 2][q, :].rearrange("p (b c d) -> p b c d", b=BG, c=HP), ACT.Copy).then_inc(v_ev, 1)

            def evac_xt(g):
                act.wait_ge(xt_tr, g + 1)
                if g >= 2:
                    act.wait_ge(q_mm, g - 1)
                nc.scalar.activation(XT[:, g % 2, :], PTP[g % 2][:, :], ACT.Copy).then_inc(xt_ev, 1)

            def q_first(g):
                act.wait_ge(q_mm, g + 1)
                if g >= 2:
                    act.wait_ge(d_part["q"][g % 2], 16 * STORES * (g // 2))
                nc.scalar.activation(parts["q"][:, g % 2, 0, :], bank[g][:, :], ACT.Identity, bias=bcols[:, 3:4]).then_inc(q_hi, 1)

            act.wait_ge(base_ready, 1)
            base_values(0)
            evac_ct(0)
            evac_ct(1)
            act.wait_ge(df_done, 1)
            nc.scalar.activation(df, df, ACT.Square).then_inc(sq_done, 1)
            act.wait_ge(bcol_ready, 1)
            k_first(0)
            act.wait_ge(pool_const, 3)
            values(0)
            evac_ct(2)
            k_first(1)
            values(1)
            evac_ct(3)
            act.wait_ge(d2_clamped, 1)
            nc.scalar.activation(dv, d2, ACT.Sqrt).then_inc(sqrt_done, 1)
            values(2)
            act.wait_ge(near_done, 1)
            nc.scalar.activation(sm, rt, ACT.Square, scale=MAX_DIST / NB).then_inc(edge_done, 1)
            evac_xt(0)
            q_first(0)
            evac_xt(1)
            k_first(2)
            values(3)
            q_first(1)
            k_first(3)
            evac_xt(2)
            evac_xt(3)
            q_first(2)
            q_first(3)
            base_values(1)
            def aot(t):
                act.wait_ge(ao_tr, t + 1)
                if t >= 2:
                    act.wait_ge(wo_mm, t - 1)
                nc.scalar.activation(AOT[:, t % 2, :], MPS[:, 0:P], ACT.Identity, bias=bcols[:, 2:3]).then_inc(aot_ev, 1)

            for t in range(T):
                act.wait_ge(sub_done, t + 1)
                nc.scalar.activation(PR[:, t % 2], PR[:, t % 2], ACT.Exp).then_inc(exp_done, 1)
                if t >= 2:
                    act.wait_ge(pv_mm, t - 1)
                for half in range(2):
                    act.wait_ge(p_tr, 2 * t + half + 1)
                    nc.scalar.activation(PT[:, t % 2, 4 * half:4 * half + 4, :].rearrange("p c n -> p (c n)"),
                                         PTP[half][:, :], ACT.Copy).then_inc(pt_ev, 1)
                if t >= 1:
                    aot(t - 1)
                if t == 0:
                    act.dma_start(w_gi[:, :], g_wi).then_inc(d_gate, 16)
                    act.dma_start(w_go[:, :, :], g_wo.rearrange("(c p) h -> p c h", p=P)).then_inc(d_gate, 16)
                    act.dma_start(gbi[:, :], g_bi.rearrange("(c p) -> p c", p=P), allow_slow_non_contiguous=True).then_inc(d_gate, 16)
                    act.dma_start(gbo_b[:, :], row(g_bo).broadcast_to([P, D])).then_inc(d_gate, 16)
                if 3 <= t < 3 + E:
                    e = t - 3
                    act.dma_start(w_ei[:, e, :], e_wi[e]).then_inc(d_ew, 16)
                    act.dma_start(w_eo[:, e, :, :], e_wo[e].rearrange("(c p) h -> p c h", p=P)).then_inc(d_ew, 16)
                if t == 3 + E:
                    act.dma_start(ebi[:, :, :], e_bi.rearrange("e (c p) -> p e c", p=P), allow_slow_non_contiguous=True).then_inc(d_ew, 16)
                    act.dma_start(ebo[:, :, :].rearrange("p e h -> p (e h)"), e_bo.rearrange("(a e) h -> a (e h)", a=1).broadcast_to([P, E * D])).then_inc(d_ew, 16)
            aot(T - 1)

            def evac_n2(g):
                act.wait_ge(n2_tr, g + 1)
                nc.scalar.activation(XN2T[:, GTOK * g:GTOK * (g + 1)], PTP[g % 2][:, :], ACT.Copy).then_inc(n2_ev, 1)

            act.wait_ge(pv_mm, T)
            act.wait_ge(consts2, 1)
            evac_n2(0)
            for g in range(NG):
                if g + 1 < NG:
                    evac_n2(g + 1)
                for c in range(FC):
                    n = FC * g + c
                    act.wait_ge(h_mm, n + 1)
                    if n >= 2:
                        act.wait_ge(sg_done, n - 1)
                    nc.scalar.activation(GE[:, n % 2, :], SPS[n % 4][:, :], ACT.Exp, bias=gb_exp[:, c:c + 1]).then_inc(ge_done, 1)
            act.wait_ge(consts2, 2)
            act.wait_ge(cnt_done, 1)
            outer = act.value_load(cnt_i[0:1, 0:1], min_val=1, max_val=P // CAND)
            inner = act.value_load(cnt_i[0:1, 1:2], min_val=1, max_val=MAXRI)
            with act.Fori(0, outer) as ro:
                for q in range(2):
                    act.wait_ge(xc_mm, ro * NC + q + 1)
                    nc.scalar.activation(XC[:, q, :], bank[q][:, 0:XWW], ACT.Copy).then_inc(xc_ev_a, 1)
                act.wait_ge(g1_tr, ro * 2 + 1)
                nc.scalar.activation(GT1[:, 0:T // 2, :].rearrange("p t n -> p (t n)"), PTP[0][:, :].bitcast(BF16), ACT.Copy).then_inc(gt1_ev_a, 1)
                with act.Fori(ro * inner, ro * inner + inner) as k:
                    for i in range(2):
                        act.wait_ge(xg_mm, k * 2 + i + 1)
                        nc.scalar.activation(XG[:, i * 512:(i + 1) * 512], (OPS, MPS)[i][:, :], ACT.Copy).then_inc(xg_ev, 1)
                    for q in range(NC):
                        act.wait_ge(g2_tr, k * NC + q + 1)
                        nc.scalar.activation(GT2[:, q].rearrange("p e n -> p (e n)"), PTP[q % 2][:, :].bitcast(BF16), ACT.Copy).then_inc(gt2_ev, 1)
                    for e in range(E):
                        act.wait_ge(eh_mm, k * E + e + 1)
                        if e >= 2:
                            act.wait_ge(se_done, k * E + e - 1)
                        for c in range(FC):
                            last = nc.scalar.activation(he[:, e % 2, c, :], bank[e % 4][:, c * CAP:(c + 1) * CAP], ACT.Exp, bias=eb_exp[:, e, c:c + 1])
                        last.then_inc(he_done, 1)

        @block.vector
        def _(dve):
            link, _n = chain(dve, dve_c)

            nc.vector.memset(BD[:, :, :, :], 0.0).then_inc(bd_zero, 1)
            dve.wait_ge(d_tab, 48)
            link(nc.vector.tensor_tensor(tab[:, :], tab[:, :], tab_last[:, :], ALU.subtract))
            link(nc.vector.tensor_copy(tab_h[:, 0], tab[:, :]))
            link(nc.vector.tensor_tensor(tab_r[:, :], tab[:, :], tab_h[:, 0], ALU.subtract))
            link(nc.vector.tensor_copy(tab_h[:, 1], tab_r[:, :]))
            link(nc.vector.tensor_tensor(tab_h[:, 2], tab_r[:, :], tab_h[:, 1], ALU.subtract))
            dve.wait_ge(bd_zero, 1)
            for j in range(JB):
                q = slice(NB * j, NB * (j + 1))
                nc.vector.tensor_copy(BD[q, :, :, j], tab_h[q, :, :]).then_inc(bd_ready, 1)
            odd_even = base_f[:, 0].rearrange("p (two c2) (c1 h) -> p (two c2 c1) h", two=1, h=2)
            link(nc.vector.tensor_copy(base_f[:, 1, 0, :], odd_even[:, :, 0]))
            link(nc.vector.tensor_tensor(base_f[:, 1, 1, :], odd_even[:, :, 1], odd_even[:, :, 0], ALU.subtract))
            for s in range(3):
                link(nc.vector.tensor_copy(base_s[:, s], base_f[:, 1]))
                if s < 2:
                    link(nc.vector.tensor_tensor(base_f[:, 1], base_f[:, 1], base_s[:, s], ALU.subtract))
            dve.wait_ge(pool_const, 1)
            link(nc.vector.memset(base_m[:, :], 0.0))
            for r in range(BR):
                last = nc.vector.scalar_tensor_tensor(out=base_m[:, :], in0=base_s[:, r % 3, r // 3], scalar=ident[PR_ROWS:KR, PR_ROWS + r:PR_ROWS + r + 1],
                                                      in1=base_m[:, :], op0=ALU.mult, op1=ALU.add)
                if r < BR - 1:
                    link(last)
            last.then_inc(base_ready, 1)
            dve.wait_ge(d_pos, 48)
            nc.vector.tensor_tensor(df, posq[:, :, :].unsqueeze(2).broadcast_to([P, T, L, 3]), posk, ALU.subtract).then_inc(df_done, 1)
            dve.wait_ge(d_small, 48)
            nc.vector.tensor_scalar(bcols[:, 3:4], bcols[:, 0:1], SC, None, ALU.mult).then_inc(bcol_ready, 1)
            dve.wait_ge(d_watt2, 32)
            nc.vector.tensor_scalar(w_q[:, :], w_att[:, 0, :], SC, None, ALU.mult).then_inc(wq_scaled, 1)

            def moments(t):
                link(nc.vector.bn_stats(stats[:, t, :], X[:, t, :]))
                return nc.vector.bn_aggr(mv[:, t, :], stats[:, t, :])

            for g in range(NG):
                dve.wait_ge(d_x[g], 16)
                for t in range(TG * g, TG * g + TG):
                    last = nc.vector.bn_stats(stats[:, t, :], X[:, t, :])
            link(last)
            for t in range(T):
                last = nc.vector.bn_aggr(mv[:, t, :], stats[:, t, :])
            link(last)
            nc.vector.tensor_scalar(vare[:, :], mv[:, :, 1], EPS, None, ALU.add).then_inc(var_done, 1)

            dve.wait_ge(sq_done, 1)
            link(nc.vector.tensor_tensor(d2, df[:, :, :, 0], df[:, :, :, 1], ALU.add))
            link(nc.vector.tensor_tensor(d2, d2, df[:, :, :, 2], ALU.add))
            nc.vector.tensor_scalar(d2, d2, 1e-30, 1e30, ALU.max, ALU.min).then_inc(d2_clamped, 1)

            def split(s, g):
                hi, mm_, bias, done_r, done = ((k_hi, k_mm, bcols[:, 1:2], k_r, k_parts), (q_hi, q_mm, bcols[:, 3:4], q_r, q_parts))[s == "q"]
                dve.wait_ge(hi, g + 1)
                p3 = parts[s][:, g % 2]
                nc.vector.scalar_tensor_tensor(out=rest[:, :], in0=bank[g][:, :], scalar=bias, in1=p3[:, 0, :],
                                               op0=ALU.add, op1=ALU.subtract).then_inc(done_r, 1)
                dve.wait_ge(done_r, g + 1)
                link(nc.vector.tensor_copy(p3[:, 1, :], rest[:, :]))
                nc.vector.tensor_tensor(p3[:, 2, :], rest[:, :], p3[:, 1, :], ALU.subtract).then_inc(done, 1)
                dve.wait_ge(done, g + 1)

            def layer_norm(src, dst, t):
                return nc.vector.tensor_scalar(dst, src, mv[:, t, 0:1], rstd[:, t:t + 1], ALU.subtract, ALU.mult)

            def ln_group(g):
                if g >= 2:
                    dve.wait_ge(xt_tr, g - 1)
                for u in range(TG):
                    last = layer_norm(X[:, TG * g + u, :], XN[:, g % 2, u, :], TG * g + u)
                last.then_inc(xn_done, 1)

            split("k", 0)
            dve.wait_ge(sqrt_done, 1)
            link(nc.vector.tensor_scalar(dv, dv, NB / MAX_DIST, float(NB), ALU.mult, ALU.min))
            nc.vector.tensor_scalar(rt, dv, 2.0 ** 23, -2.0 ** 23, ALU.add, ALU.add).then_inc(near_done, 1)
            dve.wait_ge(rstd_done, 1)
            ln_group(0)
            dve.wait_ge(edge_done, 1)
            link(nc.vector.tensor_tensor(dv, sm, d2, ALU.is_gt))
            nc.vector.tensor_tensor(binv[:, :, :], rt, dv, ALU.subtract).then_inc(bins_done, 1)
            ln_group(1)
            split("q", 0)
            split("k", 1)

            def one_hot(t):
                dve.wait_ge(d_bb[t % 4], 16 * (t // 4 + 1))
                if t >= 2:
                    dve.wait_ge(s_mm, t - 1)
                nc.vector.tensor_scalar(OH[:, t % 2, :], BB[:, t % 4, :], bin_id[:, 0:1], None, ALU.is_equal).then_inc(oh_done, 1)

            def residual(t):
                dve.wait_ge(wo_mm, t + 1)
                nc.vector.tensor_tensor(X[:, t, :], X[:, t, :], MPS[:, P:2 * P], ALU.add).then_inc(x2_done, 1)
                dve.wait_ge(x2_done, t + 1)
                moments(t).then_inc(mv2_done, 1)
                if t % TG == TG - 1:
                    dve.wait_ge(mv2_done, t + 1)
                    g = t // TG
                    nc.vector.tensor_scalar(vare[:, tiles(g)], mv[:, tiles(g), 1], EPS, None, ALU.add).then_inc(var2_done, 1)

            def norm2(g):
                dve.wait_ge(rstd2_done, g + 1)
                for u in range(TG):
                    last = layer_norm(X[:, TG * g + u, :], XN2[:, TG * g + u, :], TG * g + u)
                last.then_inc(n2_done, 1)
                dve.wait_ge(n2_done, g + 1)

            def parts2(g):
                xw = [XW[:, tiles(g), s * D:(s + 1) * D] for s in range(3)]
                link(nc.vector.tensor_copy(xw[0], XN2[:, tiles(g), :]))
                link(nc.vector.tensor_tensor(x2r[:, :, :], XN2[:, tiles(g), :], xw[0], ALU.subtract))
                link(nc.vector.tensor_copy(xw[1], x2r[:, :, :]))
                link(nc.vector.tensor_tensor(xw[2], x2r[:, :, :], xw[1], ALU.subtract))

            def normalise(t):
                dve.wait_ge(pv_mm, t + 1)
                o = OPS[:, 0:HP * VW].rearrange("p (c w) -> p c w", w=VW)
                link(nc.vector.reciprocal(rsum[:, :].rearrange("p (c h) -> p c h", h=2), o[:, :, 2 * HD:VW]))
                if t >= 2:
                    dve.wait_ge(ao_tr, t - 1)
                nc.vector.tensor_tensor(AO[:, t % 2, :].rearrange("p (c h d) -> p c h d", c=HP, h=2),
                                        o[:, :, 0:2 * HD].rearrange("p c (h d) -> p c h d", h=2),
                                        rsum[:, :].rearrange("p (c h) -> p c h", h=2).unsqueeze(3).broadcast_to([P, HP, 2, HD]),
                                        ALU.mult).then_inc(ao_done, 1)

            dve.wait_ge(pool_const, 4)
            split("q", 1)
            one_hot(0)
            split("k", 2)
            ln_group(2)
            split("k", 3)
            ln_group(3)
            one_hot(1)
            split("q", 2)
            split("q", 3)
            for t in range(T):
                if t == 2:
                    dve.wait_ge(xb_done, 1)
                dve.wait_ge(s_mm, t + 1)
                two = 2 * (t % 2)
                nc.vector.reduce_max(mxp[:, 0, :], SPS[two][:, :].rearrange("p (h k) -> p h k", h=H), AX.X)
                link(nc.vector.reduce_max(mxp[:, 1, :], SPS[two + 1][:, :].rearrange("p (h k) -> p h k", h=H), AX.X))
                link(nc.vector.tensor_tensor(mx[:, :], mxp[:, 0, :], mxp[:, 1, :], ALU.max))
                if t >= 2:
                    dve.wait_ge(p_tr, 2 * (t - 1))
                for ih in range(2):
                    last = nc.vector.tensor_tensor(PR[:, t % 2].rearrange("p h (i k) -> p i h k", i=2)[:, ih],
                                                   SPS[two + ih][:, :].rearrange("p (h k) -> p h k", h=H),
                                                   mx[:, :].unsqueeze(2).broadcast_to([P, H, L // 2]), ALU.subtract)
                last.then_inc(sub_done, 1)
                if t + 2 < T:
                    one_hot(t + 2)
                if t >= 1:
                    normalise(t - 1)
                if t >= 2:
                    residual(t - 2)
                if t >= 6 and t % TG == 2:
                    norm2(t // TG - 1)
                if t >= 7 and t % TG == 3:
                    parts2(t // TG - 1)
            residual(T - 2)
            normalise(T - 1)
            residual(T - 1)

            dve.wait_ge(d_gate, 64)
            link(nc.vector.tensor_scalar(w_go[:, :, :], w_go[:, :, :], SELU_SCALE, None, ALU.mult))
            link(nc.vector.tensor_scalar(gb_lin[:, :], gbi[:, :], -SELU_ALPHA, None, ALU.add))
            nc.vector.tensor_scalar(gb_exp[:, :], gbi[:, :], float(np.log(SELU_ALPHA)), None, ALU.add).then_inc(consts2, 1)
            dve.wait_ge(pv_mm, T)
            dve.wait_ge(s_mm, T)
            norm2(NG - 1)
            dve.wait_ge(pool_const, 5)

            def top2(g):
                dve.wait_ge(lg_mm, g + 1)
                nc.vector.tensor_tensor(LG[:, :, :], (OPS, MPS)[g % 2][:, :].rearrange("p (t h) -> p t h", t=TG),
                                        gbo_b[:, :].unsqueeze(1).broadcast_to([P, TG, D]), ALU.add).then_inc(lg_ev, 1)
                dve.wait_ge(lg_ev, g + 1)
                for u in range(TG):
                    last = nc.vector.max(v8[:, TG * g + u, :], LG[:, u, :])
                link(last)
                for u in range(TG):
                    last = nc.vector.max_index(i8[:, TG * g + u, :], v8[:, TG * g + u, :], LG[:, u, :])
                link(last)

            def choose(g):
                ts = tiles(g)
                e_ = lambda a: a[:, :].unsqueeze(1).broadcast_to([P, TG, E])
                link(nc.vector.tensor_copy(i2f[:, ts, :], i8[:, ts, 0:2]))
                for k_ in range(2):
                    last = nc.vector.tensor_tensor(eq[:, k_, ts], i2f[:, ts, k_:k_ + 1].broadcast_to([P, TG, E]), e_(exp_iota), ALU.is_equal)
                link(last)
                link(nc.vector.tensor_tensor(XW[:, ts, 3 * D + 3 * E:], eq[:, 0, ts], eq[:, 1, ts], ALU.add))
                nc.vector.reduce_max(Ub[:, ts], XW[:, ts, 3 * D + 3 * E:], AX.X).then_inc(f_done, 1)
                link(nc.vector.tensor_tensor(vs[:, ts], v8[:, ts, 0], v8[:, ts, 1], ALU.add))
                link(nc.vector.reciprocal(vs[:, ts], vs[:, ts]))
                link(nc.vector.tensor_tensor(w2[:, ts, :], v8[:, ts, 0:2], vs[:, ts].unsqueeze(2).broadcast_to([P, TG, 2]), ALU.mult))
                for k_ in range(2):
                    last = nc.vector.tensor_tensor(we[:, k_, ts], eq[:, k_, ts], w2[:, ts, k_:k_ + 1].broadcast_to([P, TG, E]), ALU.mult)
                link(last)
                link(nc.vector.tensor_tensor(Wt[:, ts, :], we[:, 0, ts], we[:, 1, ts], ALU.add))
                w3 = [XW[:, ts, 3 * D + s * E:3 * D + (s + 1) * E] for s in range(3)]
                link(nc.vector.tensor_copy(w3[0], Wt[:, ts, :]))
                link(nc.vector.tensor_tensor(Wr[:, ts, :], Wt[:, ts, :], w3[0], ALU.subtract))
                link(nc.vector.tensor_copy(w3[1], Wr[:, ts, :]))
                link(nc.vector.tensor_tensor(w3[2], Wr[:, ts, :], w3[1], ALU.subtract))

            for g in range(NG):
                for c in range(FC):
                    n = FC * g + c
                    dve.wait_ge(ge_done, n + 1)
                    link(nc.vector.tensor_scalar(GR[:, n % 2, :], SPS[n % 4][:, :], gb_lin[:, c:c + 1], -SELU_ALPHA, ALU.add, ALU.max))
                    if c == 0 and g >= 2:
                        dve.wait_ge(lg_mm, g - 1)
                    nc.vector.scalar_tensor_tensor(out=SG[:, g % 2, c, :], in0=GE[:, n % 2, :], scalar=SELU_ALPHA,
                                                   in1=GR[:, n % 2, :], op0=ALU.min, op1=ALU.add).then_inc(sg_done, 1)
                if g == 0:
                    parts2(NG - 1)
                    link(nc.vector.memset(G1[:, :, :], 0.0))
                    dve.wait_ge(d_ew, 16 * (2 * E + 2))
                    nc.vector.tensor_scalar(eb_lin[:, :, :], ebi[:, :, :], -SELU_ALPHA, None, ALU.add)
                    nc.vector.tensor_scalar(eb_exp[:, :, :], ebi[:, :, :], float(np.log(SELU_ALPHA)), None, ALU.add).then_inc(consts2, 1)
                    dve.wait_ge(consts2, 2)
                if g >= 1:
                    top2(g - 1)
                    choose(g - 1)
            top2(NG - 1)
            choose(NG - 1)
            FAR = 4.0 * B * L
            link(nc.vector.tensor_scalar(rank[:, :], Ub[:, :], -FAR, FAR, ALU.mult, ALU.add))
            dve.wait_ge(rank_mm, 1)
            link(nc.vector.tensor_tensor(rank[:, :], rank[:, :], MPS[:, T * E:T * E + T], ALU.add))
            nc.vector.reduce_max(cnt[:, 0:1], MPS[:, T * E + T:T * E + 2 * T], AX.X)
            link(nc.vector.reduce_sum(cnt[:, 2:], MPS[:, 0:T * E].rearrange("p (t e) -> p e t", e=E), AX.X))
            link(nc.vector.reduce_max(cnt[:, 1:2], cnt[:, 2:], AX.X))
            nc.vector.tensor_scalar(cnt[:, 0:1], cnt[:, 0:1], float(CAND - 1), float(CAND), ALU.add, ALU.max)
            link(nc.vector.tensor_scalar(cnt[:, 1:2], cnt[:, 1:2], float(CAP - 1), float(CAP), ALU.add, ALU.max))
            link(nc.vector.tensor_scalar(cnt[:, 1:2], cnt[:, 1:2], float(MAXRI * CAP), None, ALU.min))
            link(nc.vector.tensor_copy(cnt_i[:, :], cnt[:, 0:2]))
            nc.vector.tensor_scalar(cnt_i[:, 0:1], cnt_i[:, 0:1], CAND.bit_length() - 1, None, ALU.logical_shift_right).then_inc(cnt_half, 1)
            nc.vector.tensor_scalar(cnt_i[:, 1:2], cnt_i[:, 1:2], CAP.bit_length() - 1, None, ALU.logical_shift_right).then_inc(cnt_done, 1)
            dve.wait_ge(cnt_half, 1)
            dve.wait_ge(cnt_done, 1)
            outer = dve.value_load(cnt_i[0:1, 0:1], min_val=1, max_val=P // CAND)
            inner = dve.value_load(cnt_i[0:1, 1:2], min_val=1, max_val=MAXRI)
            OSTEPS, ISTEPS = 8, 8
            with dve.Fori(0, outer) as ro:
                olink, on = chain(dve, dve_outer, ro * OSTEPS)
                for j in range(TG):
                    last = nc.vector.tensor_tensor(G1[:, j::TG, j * CAND:(j + 1) * CAND],
                                                   rank[:, j::TG].unsqueeze(2).broadcast_to([P, NC, CAND]),
                                                   slot_iota[:, 0:CAND].unsqueeze(1).broadcast_to([P, NC, CAND]), ALU.is_equal)
                last.then_inc(g1_done, 1)
                dve.wait_ge(g1_done, ro + 1)
                olink(nc.vector.tensor_scalar(rank[:, :], rank[:, :], -float(CAND), None, ALU.add))
                for q in range(2, NC):
                    dve.wait_ge(xc_mm, ro * NC + q + 1)
                    nc.vector.tensor_copy(XC[:, q, :], bank[q][:, 0:XWW]).then_inc(xc_ev_v, 1)
                olink(nc.vector.memset(OC[:, :, :], 0.0))
                dve.wait_ge(xc_ev_a, ro * 2 + 2)
                dve.wait_ge(xc_ev_v, ro * 2 + 2)
                olink(nc.vector.tensor_scalar(slot[:, :, :], XC[:, :, 3 * D + 3 * E:], -FAR, FAR, ALU.mult, ALU.add))
                dve.wait_ge(slot_mm, ro + 1)
                olink(nc.vector.tensor_tensor(slot[:, :, :], slot[:, :, :], MPS[:, 0:NC * E].rearrange("p (q e) -> p q e", e=E), ALU.add))
                dve.wait_ge(g1_tr, ro * 2 + 2)
                nc.vector.tensor_copy(GT1[:, T // 2:T, :].rearrange("p t n -> p (t n)"), PTP[1][:, :].bitcast(BF16)).then_inc(gt1_ev_v, 1)
                with dve.Fori(ro * inner, ro * inner + inner) as k:
                    ilink, inn = chain(dve, dve_inner, k * ISTEPS)
                    for q in range(NC):
                        last = nc.vector.tensor_tensor(G2[:, q, :].rearrange("p (e s) -> p e s", e=E),
                                                       slot[:, q, :].unsqueeze(2).broadcast_to([P, E, CAP]),
                                                       slot_iota[:, :].unsqueeze(1).broadcast_to([P, E, CAP]), ALU.is_equal)
                        last.then_inc(g2_done, 1)
                    dve.wait_ge(g2_done, k * NC + NC)
                    ilink(nc.vector.tensor_scalar(slot[:, :, :], slot[:, :, :], -float(CAP), None, ALU.add))
                    dve.wait_ge(ws_mm, k + 1)
                    nc.vector.reduce_sum(wsl[:, :], OPS[:, 0:3 * E].rearrange("p (e s) -> p e s", s=3), AX.X).then_inc(wsl_done, 1)
                    for e in range(E):
                        dve.wait_ge(he_done, k * E + e + 1)
                        for c in range(FC):
                            last = nc.vector.tensor_scalar(hr[:, e % 2, c, :], bank[e % 4][:, c * CAP:(c + 1) * CAP],
                                                           eb_lin[:, e, c:c + 1], -SELU_ALPHA, ALU.add, ALU.max)
                        last.then_inc(hr_done, 1)
                        dve.wait_ge(hr_done, k * E + e + 1)
                        nc.vector.scalar_tensor_tensor(out=SE[:, e], in0=he[:, e % 2], scalar=SELU_ALPHA, in1=hr[:, e % 2],
                                                       op0=ALU.min, op1=ALU.add).then_inc(se_done, 1)
                    for i in range(2):
                        es = slice(4 * i, 4 * i + 4)
                        dve.wait_ge(y_mm, k * 2 + i + 1)
                        if i == 0:
                            dve.wait_ge(wsl_done, k + 1)
                        nc.vector.scalar_tensor_tensor(out=Y1[:, es], in0=(OPS, MPS)[i][:, :].rearrange("p (e h) -> p e h", e=4),
                                                       scalar=SELU_SCALE, in1=ebo[:, es, :], op0=ALU.mult, op1=ALU.add).then_inc(y1_done, 1)
                        dve.wait_ge(y1_done, k * 2 + i + 1)
                        ilink(nc.vector.tensor_tensor(Y[:, es], Y1[:, es], wsl[:, es].unsqueeze(2).broadcast_to([P, 4, D]), ALU.mult))
                        ilink(nc.vector.tensor_copy(Y3[:, 0, es], Y[:, es]))
                        ilink(nc.vector.tensor_tensor(Y1[:, es], Y[:, es], Y3[:, 0, es], ALU.subtract))
                        nc.vector.tensor_copy(Y3[:, 1, es], Y1[:, es]).then_inc(yb_done, 1)
                        dve.wait_ge(yb_done, k * 2 + i + 1)
                        nc.vector.tensor_tensor(Y3[:, 2, es], Y1[:, es], Y3[:, 1, es], ALU.subtract).then_inc(y3_done, 1)
                    dve.wait_ge(sc_mm, k + 1)
                    ilink(nc.vector.tensor_tensor(OC[:, :, :], OC[:, :, :], bank[4][:, :].rearrange("p (q h) -> p q h", q=NC), ALU.add))
                    assert inn[0] == ISTEPS, inn
                olink(nc.vector.tensor_copy(OC3[:, 0], OC[:, :, :]))
                olink(nc.vector.tensor_tensor(OCr[:, :, :], OC[:, :, :], OC3[:, 0], ALU.subtract))
                olink(nc.vector.tensor_copy(OC3[:, 1], OCr[:, :, :]))
                nc.vector.tensor_tensor(OC3[:, 2], OCr[:, :, :], OC3[:, 1], ALU.subtract).then_inc(oc3_done, 1)
                for q in range(NC):
                    dve.wait_ge(back_mm, ro * NC + q + 1)
                    last = nc.vector.tensor_tensor(X[:, tiles(q), :], X[:, tiles(q), :], bank[q][:, :].rearrange("p (t h) -> p t h", t=TG), ALU.add)
                olink(last)
                assert on[0] == OSTEPS, on
            nc.vector.memset(cnt[:, :], 0.0).then_inc(out_ready, 1)

        @block.tensor
        def _(pe):
            mm, tr = nc.tensor.matmul, nc.tensor.transpose

            def ctx_transposes(g):
                pe.wait_ge(d_cx[g], 16)
                if g >= 2:
                    pe.wait_ge(ct_ev, g - 1)
                for u in range(TG):
                    last = tr(PTP[g % 2][:, u * P:(u + 1) * P], CX[:, TG * g + u, :], ident[:, :])
                last.then_inc(ct_tr, 1)

            def project_kv(g):
                pe.wait_ge(ct_ev, g + 1)
                mm(bank[g][:, :], w_att[:, 1, :], CT[:, g % 2, :], start=True, stop=True).then_inc(k_mm, 1)
                if g >= 2:
                    pe.wait_ge(v_ev, 2 * (g - 1))
                wv = w_att[:, 2, :].rearrange("p (c h d) -> p h c d", h=2, d=HD)
                for b in range(BG):
                    for h2 in range(2):
                        last = mm((OPS, MPS)[g % 2][h2 * L:(h2 + 1) * L, b * L:(b + 1) * L],
                                  CT[:, g % 2, b * L:(b + 1) * L], wv[:, h2], start=True, stop=True)
                last.then_inc(v_mm, 1)

            pe.wait_ge(pool_const, 1)
            ctx_transposes(0)
            ctx_transposes(1)
            pe.wait_ge(d_watt, 32)
            for g in range(NG):
                project_kv(g)
                if g + 2 < NG:
                    ctx_transposes(g + 2)

            def x_transposes(g):
                pe.wait_ge(xn_done, g + 1)
                if g >= 2:
                    pe.wait_ge(xt_ev, g - 1)
                else:
                    pe.wait_ge(ct_ev, NG)
                for u in range(TG):
                    last = tr(PTP[g % 2][:, u * P:(u + 1) * P], XN[:, g % 2, u, :], ident[:, :])
                last.then_inc(xt_tr, 1)

            def project_q(g):
                pe.wait_ge(xt_ev, g + 1)
                pe.wait_ge(k_r, g + 1)
                mm(bank[g][:, :], w_q[:, :], XT[:, g % 2, :], start=True, stop=True).then_inc(q_mm, 1)

            pe.wait_ge(wq_scaled, 1)
            for g in range(NG):
                x_transposes(g)
                project_q(g)

            def biases(t):
                two = 2 * (t % 2)
                if t == 0:
                    pe.wait_ge(bd_ready, JB)
                if t < 2:
                    pe.wait_ge(q_r, 2 * (t + 1))
                else:
                    pe.wait_ge(sub_done, t - 1)
                pe.wait_ge(oh_done, t + 1)
                for i in range(IB):
                    ih, i8_ = i // 8, i % 8
                    o = SPS[two + ih][:, :].rearrange("p (h i j) -> p i h j", h=H, i=8)[:, i8_]
                    for s in range(3):
                        mm(o, OH[:, t % 2, i * P:(i + 1) * P], BD[:, s], start=(i8_ == 0 and s == 0), stop=False, skip_group_check=True)

            def scores(t):
                g, two = t // TG, 2 * (t % 2)
                if t % TG == 0 and g < 2:
                    pe.wait_ge(base_rows, g + 1)
                if t % TG == 0:
                    for s in "qk":
                        pe.wait_ge(d_stack[s][g % 2], 16 * STACKS[s] * (g // 2 + 1))
                for b2 in range(2):
                    q0 = (t % TG) * P + b2 * L
                    for c in range(HP):
                        for ih in range(2):
                            last = mm(SPS[two + ih][b2 * L:(b2 + 1) * L, c * L:(c + 1) * L],
                                      QS[:, g % 2, c, q0:q0 + L],
                                      KS[:, g % 2, c, :, q0 + ih * (L // 2):q0 + (ih + 1) * (L // 2)],
                                      start=False, stop=True, skip_group_check=True)
                last.then_inc(s_mm, 1)

            def p_transposes(t):
                pe.wait_ge(exp_done, t + 1)
                for half in range(2):
                    if t >= 1:
                        pe.wait_ge(pt_ev, 2 * (t - 1) + half + 1)
                    else:
                        pe.wait_ge(xt_ev, NG)
                    for c in range(4):
                        cc = 4 * half + c
                        last = tr(PTP[half][:, c * P:(c + 1) * P], PR[:, t % 2, 2 * cc:2 * cc + 2, :].rearrange("p h k -> p (h k)"), ident[:, :])
                    last.then_inc(p_tr, 1)

            def p_v(t):
                if t >= 1:
                    pe.wait_ge(ao_done, t)
                else:
                    pe.wait_ge(v_ev, 2 * NG)
                for c in range(HP):
                    if c % 4 == 0:
                        pe.wait_ge(pt_ev, 2 * t + c // 4 + 1)
                    for b2 in range(2):
                        last = mm(OPS[b2 * L:(b2 + 1) * L, c * VW:(c + 1) * VW], PT[:, t % 2, c, b2 * L:(b2 + 1) * L],
                                  VD[:, 2 * t + b2, c, :], start=True, stop=True)
                last.then_inc(pv_mm, 1)

            def ao_transpose(t):
                pe.wait_ge(ao_done, t + 1)
                if t >= 1:
                    pe.wait_ge(x2_done, t)
                tr(MPS[:, 0:P], AO[:, t % 2, :], ident[:, :]).then_inc(ao_tr, 1)

            def out_project(t):
                pe.wait_ge(aot_ev, t + 1)
                mm(MPS[:, P:2 * P], AOT[:, t % 2, :], w_att[:, 3, :], start=True, stop=True).then_inc(wo_mm, 1)

            for t in range(2):
                biases(t)
                scores(t)
            for t in range(T):
                p_transposes(t)
                if t >= 1:
                    ao_transpose(t - 1)
                if t + 2 < T:
                    biases(t + 2)
                p_v(t)
                if t >= 1:
                    out_project(t - 1)
                if t + 2 < T:
                    scores(t + 2)
            ao_transpose(T - 1)
            out_project(T - 1)

            def n2_transposes(g):
                pe.wait_ge(n2_done, g + 1)
                if g >= 2:
                    pe.wait_ge(n2_ev, g - 1)
                for u in range(TG):
                    last = tr(PTP[g % 2][:, u * P:(u + 1) * P], XN2[:, TG * g + u, :], ident[:, :])
                last.then_inc(n2_tr, 1)

            def logits(g):
                pe.wait_ge(sg_done, FC * (g + 1))
                if g >= 2:
                    pe.wait_ge(lg_ev, g - 1)
                else:
                    pe.wait_ge(x2_done, T)
                o = (OPS, MPS)[g % 2]
                for u in range(TG):
                    for c in range(FC):
                        last = mm(o[:, u * D:(u + 1) * D], SG[:, g % 2, c, u * P:(u + 1) * P], w_go[:, c, :], start=(c == 0), stop=(c == FC - 1))
                last.then_inc(lg_mm, 1)

            pe.wait_ge(pt_ev, 2 * T)
            pe.wait_ge(pool_const, 5)
            n2_transposes(0)
            for g in range(NG):
                if g + 1 < NG:
                    n2_transposes(g + 1)
                pe.wait_ge(n2_ev, g + 1)
                if g == 0:
                    pe.wait_ge(d_gate, 64)
                    pe.wait_ge(sub_done, T)
                for c in range(FC):
                    n = FC * g + c
                    if n >= 4:
                        pe.wait_ge(sg_done, n - 3)
                    mm(SPS[n % 4][:, :], w_gi[:, c * P:(c + 1) * P], XN2T[:, GTOK * g:GTOK * (g + 1)], start=True, stop=True).then_inc(h_mm, 1)
                if g >= 1:
                    logits(g - 1)
            logits(NG - 1)
            pe.wait_ge(f_done, NG)
            mm(MPS[:, 0:T * E].rearrange("p (t e) -> p t e", e=E), ones_bf[:, :], XW[:, :, 3 * D + 3 * E:], start=True, stop=True)
            mm(MPS[:, T * E:T * E + T], lower[:, :], Ub[:, :], start=True, stop=True)
            mm(MPS[:, T * E + T:T * E + 2 * T], ones_bf[:, :], Ub[:, :], start=True, stop=True).then_inc(rank_mm, 1)
            pe.wait_ge(cnt_done, 1)
            pe.wait_ge(d_ew, 16 * (2 * E + 2))
            outer = pe.value_load(cnt_i[0:1, 0:1], min_val=1, max_val=P // CAND)
            inner = pe.value_load(cnt_i[0:1, 1:2], min_val=1, max_val=MAXRI)
            with pe.Fori(0, outer) as ro:
                pe.wait_ge(g1_done, ro + 1)
                for q in range(NC):
                    for j in range(TG):
                        last = mm(bank[q][:, 0:XWW], G1[:, TG * q + j, :], XW[:, TG * q + j, :], start=(j == 0), stop=(j == TG - 1))
                    last.then_inc(xc_mm, 1)
                for half in range(2):
                    pb = PTP[half][:, :].bitcast(BF16)
                    for u in range(T // 2):
                        last = tr(pb[:, u * P:(u + 1) * P], G1[:, half * (T // 2) + u, :], ident_bf[:, :])
                    last.then_inc(g1_tr, 1)
                pe.wait_ge(xc_ev_a, ro * 2 + 2)
                pe.wait_ge(xc_ev_v, ro * 2 + 2)
                member = XC[:, :, 3 * D + 3 * E:]
                for q in range(NC - 1):
                    mm(MPS[:, (q + 1) * E:NC * E].rearrange("p (q e) -> p q e", e=E), ones_bf[:, :],
                       member[:, q:q + 1, :].broadcast_to([P, NC - 1 - q, E]), start=(q == 0), stop=False, skip_group_check=True)
                mm(MPS[:, 0:NC * E].rearrange("p (q e) -> p q e", e=E), lower[:, :], member, start=False, stop=True,
                   skip_group_check=True).then_inc(slot_mm, 1)
                pe.wait_ge(gt1_ev_a, ro + 1)
                pe.wait_ge(gt1_ev_v, ro + 1)
                with pe.Fori(ro * inner, ro * inner + inner) as k:
                    for q in range(NC):
                        pe.wait_ge(g2_done, k * NC + q + 1)
                        for s in range(3):
                            for i in range(2):
                                last = mm((OPS, MPS)[i][:, :], XC[:, q, s * D:(s + 1) * D], G2[:, q, i * 512:(i + 1) * 512],
                                          start=(q == 0 and s == 0), stop=(q == NC - 1 and s == 2))
                                if q == NC - 1 and s == 2:
                                    last.then_inc(xg_mm, 1)
                    for q in range(NC):
                        if q >= 2:
                            pe.wait_ge(gt2_ev, k * NC + q - 1)
                        pb = PTP[q % 2][:, :].bitcast(BF16)
                        for e in range(E):
                            last = tr(pb[:, e * P:(e + 1) * P], G2[:, q, e * CAP:(e + 1) * CAP], ident_bf[:, :])
                        last.then_inc(g2_tr, 1)
                    pe.wait_ge(xg_ev, k * 2 + 2)
                    for e in range(E):
                        for q in range(NC):
                            last = mm(OPS[:, 3 * e:3 * e + 3], G2[:, q, e * CAP:(e + 1) * CAP],
                                      XC[:, q, 3 * D + e:3 * D + 3 * E:E], start=(q == 0), stop=(q == NC - 1))
                    last.then_inc(ws_mm, 1)

                    def hidden(e):
                        if e >= 4:
                            pe.wait_ge(se_done, k * E + e - 3)
                        for c in range(FC):
                            last = mm(bank[e % 4][:, c * CAP:(c + 1) * CAP], w_ei[:, e, c * P:(c + 1) * P], XG[:, e * CAP:(e + 1) * CAP],
                                      start=True, stop=True)
                        last.then_inc(eh_mm, 1)

                    def output(e):
                        pe.wait_ge(se_done, k * E + e + 1)
                        if e == 0:
                            pe.wait_ge(wsl_done, k + 1)
                        for c in range(FC):
                            last = mm((OPS, MPS)[e // 4][:, (e % 4) * D:(e % 4 + 1) * D], SE[:, e, c, :], w_eo[:, e, c, :],
                                      start=(c == 0), stop=(c == FC - 1))
                        if e % 4 == 3:
                            last.then_inc(y_mm, 1)

                    for e in range(E + 2):
                        if e < E:
                            hidden(e)
                        if e >= 2:
                            output(e - 2)
                    pe.wait_ge(gt2_ev, k * NC + NC)
                    for i in range(2):
                        pe.wait_ge(y3_done, k * 2 + i + 1)
                        for q in range(NC):
                            for e in range(4 * i, 4 * i + 4):
                                for s in range(3):
                                    last = mm(bank[4][:, q * D:(q + 1) * D], GT2[:, q, e, :], Y3[:, s, e, :],
                                              start=(i == 0 and q == 0 and e == 0 and s == 0), stop=(e == E - 1 and s == 2), skip_group_check=True)
                    last.then_inc(sc_mm, 1)
                pe.wait_ge(oc3_done, ro + 1)
                for q in range(NC):
                    for j in range(TG):
                        for s in range(3):
                            last = mm(bank[q][:, j * D:(j + 1) * D], GT1[:, TG * q + j, :], OC3[:, s, q, :], start=(s == 0), stop=(s == 2))
                    last.then_inc(back_mm, 1)


_INS = ['x', 'ctx_1024', 'fside_BxSx3_0', 'L0_xattn_Wq', 'L0_xattn_bq', 'L0_xattn_Wk', 'L0_xattn_bk', 'L0_xattn_Wv',
        'L0_xattn_bv', 'L0_xattn_Wo', 'L0_xattn_bo', 'L0_xattn_dist_emb', 'L0_ffn_gate_wi', 'L0_ffn_gate_bi',
        'L0_ffn_gate_wo', 'L0_ffn_gate_bo', 'L0_ffn_exp_wi', 'L0_ffn_exp_bi', 'L0_ffn_exp_wo', 'L0_ffn_exp_bo']


def kernel(**inputs):
    import numpy as _np
    import concourse.bacc as _bacc
    from concourse import mybir as _mybir
    from concourse.bass_utils import run_bass_kernel_spmd as _run

    nc = _bacc.Bacc("TRN2", target_bir_lowering=False, num_devices=1)
    arrays, args = {}, []
    for name in _INS:
        a = _np.ascontiguousarray(inputs[name])
        arrays[f"in_{name}_dram"] = a
        args.append(nc.dram_tensor(f"in_{name}_dram", a.shape, _mybir.dt.from_np(a.dtype), kind="ExternalInput").ap())
    out = nc.dram_tensor("out_dram", inputs['x'].shape, _mybir.dt.float32, kind="ExternalOutput").ap()
    build(nc, *args, out)
    r = _run(nc, [arrays], core_ids=[0])
    return r.results[0]["out_dram"]
```

```python
from contextlib import ExitStack

import numpy as np
import concourse.bass as bass
from concourse import mybir

F32 = mybir.dt.float32
BF16 = mybir.dt.bfloat16
I32 = mybir.dt.int32
U32 = mybir.dt.uint32
ALU = mybir.AluOpType
ACT = mybir.ActivationFunctionType
AX = mybir.AxisListType

P = 128
SELU_ALPHA = 1.6732632423543772
SELU_SCALE = 1.0507009873554805
EPS = 1e-5
TWO_ONES = float(np.array([0x3F803F80], np.uint32).view(np.float32)[0])
MAX_DIST = 5.0
CAND = 32
CAP = 128
PRODUCTS = [(0, 0), (0, 1), (0, 2), (1, 0), (1, 1), (2, 0)]


def build(nc, x, ctx_in, pos, Wq, bq, Wk, bk, Wv, bv, Wo, bo, emb, g_wi, g_bi, g_wo, g_bo, e_wi, e_bi, e_wo, e_bo, out):
    B, L, D = x.shape
    BINS1, H = emb.shape
    NB = BINS1 - 1
    HD = D // H
    T = B * L // P
    F = g_wi.shape[1]
    FC = F // P
    E = e_wi.shape[0]
    NG = 4
    TG = T // NG
    GTOK = TG * P
    BG = GTOK // L
    JB = P // NB
    IB = L // JB
    HP = H // 2
    NPR = len(PRODUCTS)
    PR_ROWS = 2 * NPR * HD
    BR = 2 * 3
    KR = PR_ROWS + BR
    VW = 2 * HD + 2
    SC = HD ** -0.5
    SLOTS = E * CAP
    NC = T * CAND // P
    XWW = 3 * D + 4 * E
    MAXRI = T * CAND // CAP
    assert (L, D, NB, HD, P // CAND, CAP) == (64, P, 32, 8, TG, P)

    st = ExitStack()
    with st:
        def dram(name, shape, dt):
            return nc.dram_tensor(name, shape, dt, kind="Internal").ap()

        def sb(name, shape, dt, where=st):
            return where.enter_context(nc.sbuf_tensor(name, shape, dt))

        def sem(name):
            return st.enter_context(nc.semaphore(name))

        part_dram = {s: dram(f"part_dram_{s}", [P, NPR, B * L], BF16) for s in "qk"}
        bins_dram = dram("bins_dram", [T, JB, IB, 2, L], BF16)

        X = sb("X", [P, T, D], F32)
        ident = sb("ident", [P, P], F32)
        ident_bf = sb("ident_bf", [P, P], BF16)
        lower = sb("lower", [P, P], BF16)
        ones_bf = sb("ones_bf", [P, P], BF16)
        ones_row = sb("ones_row", [2, P], F32)
        stats = sb("stats", [P, T, 6], F32)
        mv = sb("mv", [P, T, 2], F32)
        rstd = sb("rstd", [P, T], F32)
        w_gi = sb("w_gi", [P, F], F32)
        w_go = sb("w_go", [P, FC, D], F32)
        gb_exp = sb("gb_exp", [P, FC], F32)
        gbi = sb("gbi", [P, FC], F32)
        gbo_b = sb("gbo_b", [P, D], F32)
        neg_alpha = sb("neg_alpha", [P, P], F32)
        w_ei = sb("w_ei", [P, E, F], F32)
        w_eo = sb("w_eo", [P, E, FC, D], F32)
        ebi = sb("ebi", [P, E, FC], F32)
        ebo_rows = sb("ebo_rows", [2, E, D], F32)
        slot_iota = sb("slot_iota", [P, CAP], F32)
        XN2 = sb("XN2", [P, T, D], F32)
        XW = sb("XW", [P, T, XWW], BF16)
        x2r = sb("x2r", [P, TG, D], F32)
        exp_iota = sb("exp_iota", [P, E], F32)
        half_neg = sb("half_neg", [P, T], F32)
        vare = sb("vare", [P, T], F32)
        shift = sb("shift", [P, T], F32)
        lnalpha = sb("lnalpha", [P, 1], F32)

        ab = ExitStack()
        posq = sb("posq", [P, T, 3], F32, ab)
        CX = sb("CX", [P, T, D], F32, ab)
        XN = sb("XN", [P, 2, TG, D], F32, ab)
        XCT = sb("XCT", [P, 4, GTOK], F32, ab)
        XT, CT = XCT[:, 0:2, :], XCT[:, 2:4, :]
        w_q = sb("w_q", [P, D], F32, ab)
        w_att = sb("w_att", [P, 4, D], F32, ab)
        bcols = sb("bcols", [P, 4], F32, ab)
        bo_b = sb("bo_b", [P, D], F32, ab)
        KS = sb("KS", [KR, 2, HP, 2, GTOK], BF16, ab)
        QS = sb("QS", [KR, 2, HP, GTOK], BF16, ab)
        rest = sb("rest", [P, GTOK], F32, ab)
        parts = {s: sb(f"parts_{s}", [P, 2, 3, GTOK], BF16, ab) for s in "qk"}
        VD = sb("VD", [P, B, HP, VW], F32, ab)
        BB = sb("BB", [P, 4, IB * P], BF16, ab)
        OH = sb("OH", [P, 2, IB * P], BF16, ab)
        bin_id = sb("bin_id", [P, 1], F32, ab)
        tab = sb("tab", [P, H], F32, ab)
        tab_last = sb("tab_last", [P, H], F32, ab)
        tab_r = sb("tab_r", [P, H], F32, ab)
        tab_h = sb("tab_h", [P, 3, H], BF16, ab)
        BD = sb("BD", [P, 3, H, JB], BF16, ab)
        base_f = sb("base_f", [KR, 2, 2, HP], F32, ab)[PR_ROWS:KR]
        base_s = sb("base_s", [KR, 3, 2, HP], BF16, ab)[PR_ROWS:KR]
        base_m = sb("base_m", [KR, HP], F32, ab)[PR_ROWS:KR]
        PR = CX[:, :, :].rearrange("p (a t) (h k) -> p a (t h) k", a=2, k=L)
        PT = XCT[:, :, :].rearrange("p (a b) (c n) -> p a (b c) n", a=2, n=P)
        mx = sb("mx", [P, 2, H], F32, ab)
        rsum = sb("rsum", [P, H], F32, ab)
        AO = sb("AO", [P, 2, D], F32, ab)
        AOT = sb("AOT", [P, 2, P], F32, ab)
        wf = w_ei[:, :, :].rearrange("p e f -> p (e f)")
        wf2 = w_eo[:, :, :, :].rearrange("p e c h -> p (e c h)")
        posk = wf[:, 0:T * L * 3].rearrange("p (t k c) -> p t k c", t=T, c=3)
        df = wf2[:, 0:T * L * 3].rearrange("p (t k c) -> p t k c", t=T, c=3)
        d2 = wf[:, T * L * 3:T * L * 4].rearrange("p (t k) -> p t k", t=T)
        rt, sm = df[:, :, :, 0], df[:, :, :, 1]
        dv = wf2[:, T * L * 3:T * L * 4].rearrange("p (t k) -> p t k", t=T)
        binv = sb("binv", [P, T, L], BF16, ab)
        ab.close()

        G1 = sb("G1", [P, T, P], BF16)
        GT1 = sb("GT1", [P, T, P], BF16)
        XC = sb("XC", [P, NC, XWW], BF16)
        OC = sb("OC", [P, NC, D], F32)
        OCr = sb("OCr", [P, NC, D], F32)
        OC3 = sb("OC3", [P, 3, NC, D], BF16)
        G2 = sb("G2", [P, NC, SLOTS], BF16)
        XN2T = sb("XN2T", [P, T * P], F32)
        SG = sb("SG", [P, 2, FC, GTOK], F32)
        GE = sb("GE", [P, 2, GTOK], F32)
        GR = sb("GR", [P, 2, GTOK], F32)
        LG = sb("LG", [P, TG, D], F32)
        v8 = sb("v8", [P, T, 8], F32)
        i8 = sb("i8", [P, T, 8], U32)
        i2f = sb("i2f", [P, T, 2], F32)
        vs = sb("vs", [P, T], F32)
        w2 = sb("w2", [P, T, 2], F32)
        eq = sb("eq", [P, 2, T, E], F32)
        we = sb("we", [P, 2, T, E], F32)
        Wt = sb("Wt", [P, T, E], F32)
        Wr = sb("Wr", [P, T, E], F32)
        Ub = sb("Ub", [P, T], BF16)
        rank = sb("rank", [P, T], F32)
        cnt = sb("cnt", [P, E + 2], F32)
        cnt_i = sb("cnt_i", [P, 2], I32)
        slot = sb("slot", [P, NC, E], F32)
        GT2 = sb("GT2", [P, NC, E, P], BF16)
        XG = sb("XG", [P, SLOTS], F32)
        he = sb("he", [P, 2, FC, CAP], F32)
        hr = sb("hr", [P, 2, FC, CAP], F32)
        SE = sb("SE", [P, E, FC, CAP], F32)
        eb_exp = sb("eb_exp", [P, E, FC], F32)
        eb_lin = sb("eb_lin", [P, E, FC], F32)
        memc = sb("memc", [P, NC, E], BF16)
        wsl = sb("wsl", [P, E], F32)
        Yr = sb("Yr", [P, 2, 2, D], F32)
        Y3 = sb("Y3", [P, 3, E, D], BF16)

        pair = [st.enter_context(nc.psum_tensor(f"pair{i}", [P, 1024], F32)) for i in range(4)]
        bank = [pair[i // 2][:, 512 * (i % 2):512 * (i % 2) + 512] for i in range(8)]
        SPS = [bank[0], bank[1], bank[2], bank[3]]
        PTP = [bank[4], bank[5]]
        OPS, MPS = bank[6], bank[7]
        YB = [OPS, MPS, PTP[1], OPS]
        NY = len(YB)
        SCB = [PTP[0], SPS[0]]
        BKB = [SPS[1], SPS[2], SPS[3], SPS[0]]
        LGB = [PTP[0], PTP[1], MPS, SPS[0]]

        d_pos, bins_done, d_binw, oh_done, q_parts, k_parts, s_mm, pool_const = map(sem, (
            "d_pos", "bins_done", "d_binw", "oh_done", "q_parts", "k_parts", "s_mm", "pool_const"))
        pool_c, d_out, var_done, rstd_done, d_small, xn_done, xb_done = map(sem, (
            "pool_c", "d_out", "var_done", "rstd_done", "d_small", "xn_done", "xb_done"))
        var2_done, rstd2_done, d_watt, d_tab, ct_tr, k_mm, v_mm, ct_ev = map(sem, (
            "var2_done", "rstd2_done", "d_watt", "d_tab", "ct_tr", "k_mm", "v_mm", "ct_ev"))
        k_hi, v_ev, xt_tr, q_mm, xt_ev, q_hi, bcol_ready, df_done = map(sem, (
            "k_hi", "v_ev", "xt_tr", "q_mm", "xt_ev", "q_hi", "bcol_ready", "df_done"))
        f_done, sq_done, d2_clamped, sqrt_done, near_done, edge_done, ge_done, d_gate = map(sem, (
            "f_done", "sq_done", "d2_clamped", "sqrt_done", "near_done", "edge_done", "ge_done", "d_gate"))
        d_ew, ao_tr, wo_mm, aot_ev, sub_done, exp_done, pv_mm, p_tr = map(sem, (
            "d_ew", "ao_tr", "wo_mm", "aot_ev", "sub_done", "exp_done", "pv_mm", "p_tr"))
        pt_ev, n2_tr, n2_ev, consts2, h_mm, sg_done, cnt_done, xc_mm = map(sem, (
            "pt_ev", "n2_tr", "n2_ev", "consts2", "h_mm", "sg_done", "cnt_done", "xc_mm"))
        xc_ev, g1_tr, xg_mm, xg_ev, g2_tr, gt2_ev, eh_mm = map(sem, (
            "xc_ev", "g1_tr", "xg_mm", "xg_ev", "g2_tr", "gt2_ev", "eh_mm"))
        se_done, he_done, dve_c, bd_zero, wq_scaled, k_r, q_r, bd_ready = map(sem, (
            "se_done", "he_done", "dve_c", "bd_zero", "wq_scaled", "k_r", "q_r", "bd_ready"))
        x2_done, mv2_done, n2_done, ao_done, lg_mm, lg_ev, rank_mm, cnt_half = map(sem, (
            "x2_done", "mv2_done", "n2_done", "ao_done", "lg_mm", "lg_ev", "rank_mm", "cnt_half"))
        dve_outer, g1_done, slot_mm, dve_inner, g2_done, ws_mm = map(sem, (
            "dve_outer", "g1_done", "slot_mm", "dve_inner", "g2_done", "ws_mm"))
        wsl_done, hr_done, y_mm, yb_done, y3_done, sc_mm = map(sem, (
            "wsl_done", "hr_done", "y_mm", "yb_done", "y3_done", "sc_mm"))
        oc3_done = [sem(f"oc3_done{half}") for half in range(2)]
        shift_done, p0_done, p1_done, p2_done, x2r_done, eb_mm, eb_row = map(sem, (
            "shift_done", "p0_done", "p1_done", "p2_done", "x2r_done", "eb_mm", "eb_row"))
        mem_mm, mem_ev, y0_done, yr_done, gt1_ev, eo_scaled, g1_zero, vs_done, w3_done = map(sem, (
            "mem_mm", "mem_ev", "y0_done", "yr_done", "gt1_ev", "eo_scaled", "g1_zero", "vs_done", "w3_done"))
        gb_mm, gb_ready, back_mm, d_watt2, d_bo, base_ready, base_rows = map(sem, (
            "gb_mm", "gb_ready", "back_mm", "d_watt2", "d_bo", "base_ready", "base_rows"))
        rsum_done, stats_done, vd_zero = map(sem, ("rsum_done", "stats_done", "vd_zero"))
        d_cx = [sem(f"d_cx{g}") for g in range(NG)]
        d_x = [sem(f"d_x{g}") for g in range(NG)]
        x_back = [sem(f"x_back{q}") for q in range(NC)]
        d_bb = [sem(f"d_bb{i}") for i in range(4)]
        d_part = {s: [sem(f"d_{s}part{i}") for i in range(2)] for s in "qk"}
        d_stack = {s: [sem(f"d_{s}stack{i}") for i in range(2)] for s in "qk"}
        STORES = 3
        STACKS = {"k": 2, "q": 1}

        def chain(eng, s, first=0):
            n = [0]

            def link(ins):
                n[0] += 1
                ins.then_inc(s, 1)
                eng.wait_ge(s, first + n[0])
            return link, n

        xt_dram = x.rearrange("b l d -> (b l) d").rearrange("(t p) d -> p t d", p=P)
        cx_dram = ctx_in.rearrange("b l d -> (b l) d").rearrange("(t p) d -> p t d", p=P)
        out_dram = out.rearrange("b l d -> (b l) d").rearrange("(t p) d -> p t d", p=P)
        col = lambda v: v.rearrange("(p a) -> p a", a=1)
        row = lambda v: v.rearrange("(a n) -> a n", a=1)
        tiles = lambda g: slice(TG * g, TG * (g + 1))

        block = st.enter_context(nc.Block())

        @block.sync
        def _(sp):
            sp.dma_start(posq[:, :, :], pos.rearrange("b l c -> (b l) c").rearrange("(t p) c -> p t c", p=P)).then_inc(d_pos, 16)
            for b2 in range(2):
                src = pos.rearrange("(t b) k c -> b t (k c)", b=2)[b2:b2 + 1]
                sp.dma_start(posk[b2 * L:(b2 + 1) * L].rearrange("p t k c -> p t (k c)"),
                             src.broadcast_to([L, T, L * 3])).then_inc(d_pos, 16)
            for g in range(NG):
                sp.dma_start(X[:, tiles(g), :], xt_dram[:, tiles(g), :]).then_inc(d_x[g], 16)

            def store_bins():
                sp.wait_ge(bins_done, 1)
                for b2 in range(2):
                    sp.dma_start(bins_dram[:, :, :, b2, :].rearrange("t j i m -> (j i) t m"), binv[b2 * L:(b2 + 1) * L, :, :]).then_inc(d_binw, 16)

            def spread_bins(t):
                if t == 0:
                    sp.wait_ge(d_binw, 32)
                if t >= 4:
                    sp.wait_ge(oh_done, t - 3)
                sp.dma_start(BB[:, t % 4, :], bins_dram[t].rearrange("j i b m -> j (i b m)").unsqueeze(1).broadcast_to([JB, NB, IB * P])
                             ).then_inc(d_bb[t % 4], 16)

            def store_parts(s, g):
                sp.wait_ge({"q": q_parts, "k": k_parts}[s], g + 1)
                now = slice(GTOK * g, GTOK * (g + 1))
                dst, src = part_dram[s][:, :, now], parts[s][:, g % 2]
                for first, last in ((0, 3), (3, 5), (5, 6)):
                    if s == "k":
                        take = src[:, 0:last - first, :]
                    else:
                        i = PRODUCTS[first][0]
                        take = src[:, i:i + 1, :].broadcast_to([P, last - first, GTOK])
                    sp.dma_start(dst[:, first:last, :], take).then_inc(d_part[s][g % 2], 16)

            def stack_parts(s, g):
                sp.wait_ge(d_part[s][g % 2], 16 * STORES * (g // 2 + 1))
                if g >= 2:
                    sp.wait_ge(s_mm, TG * (g - 1))
                now = slice(GTOK * g, GTOK * (g + 1))
                if s == "q":
                    sp.dma_start(QS[0:PR_ROWS, g % 2], part_dram["q"][:, :, now].rearrange("(c r) n t -> (r n) c t", c=HP)
                                 ).then_inc(d_stack["q"][g % 2], 16)
                    return
                for h2 in range(2):
                    sp.dma_start(KS[h2 * PR_ROWS // 2:(h2 + 1) * PR_ROWS // 2, g % 2, :, h2, :],
                                 part_dram["k"][:, :, now].rearrange("(c h d) n t -> h (d n) c t", h=2, d=HD)[h2]
                                 ).then_inc(d_stack["k"][g % 2], 16)

            sp.wait_ge(pool_const, 2)
            store_parts("k", 0)
            stack_parts("k", 0)
            store_bins()
            store_parts("q", 0)
            spread_bins(0)
            store_parts("k", 1)
            stack_parts("q", 0)
            store_parts("q", 1)
            spread_bins(1)
            stack_parts("k", 1)
            spread_bins(2)
            stack_parts("q", 1)
            spread_bins(3)
            for t in range(4, T):
                spread_bins(t)
                if t < TG + 2:
                    store_parts("k", t - 2)
                    store_parts("q", t - 2)
                if t in (2 * TG - 1, 3 * TG - 1):
                    stack_parts("k", (t + 1) // TG)
                    stack_parts("q", (t + 1) // TG)
                if t == TG + 2:
                    sp.dma_start(w_gi[:, :], g_wi).then_inc(d_gate, 16)
                    sp.dma_start(w_go[:, :, :], g_wo.rearrange("(c p) h -> p c h", p=P)).then_inc(d_gate, 16)
                    sp.dma_start(gbi[:, :], g_bi.rearrange("(c p) -> p c", p=P), allow_slow_non_contiguous=True).then_inc(d_gate, 16)
                    sp.dma_start(gbo_b[:, :], row(g_bo).broadcast_to([P, D])).then_inc(d_gate, 16)
                if t >= T - E:
                    e = t - (T - E)
                    sp.dma_start(w_ei[:, e, :], e_wi[e]).then_inc(d_ew, 16)
                    sp.dma_start(w_eo[:, e, :, :], e_wo[e].rearrange("(c p) h -> p c h", p=P)).then_inc(d_ew, 16)
            sp.dma_start(ebi[:, :, :], e_bi.rearrange("e (c p) -> p e c", p=P), allow_slow_non_contiguous=True).then_inc(d_ew, 16)
            sp.dma_start(ebo_rows[1:2, :, :], e_bo.rearrange("(a e) h -> a e h", a=1)).then_inc(d_ew, 16)
            sp.wait_ge(cnt_done, 1)
            outer = sp.value_load(cnt_i[0:1, 0:1], min_val=1, max_val=P // CAND)
            for g in range(NG):
                sp.wait_ge(x_back[g], outer)
                sp.dma_start(out_dram[:, tiles(g), :], X[:, tiles(g), :]).then_inc(d_out, 16)
            sp.wait_ge(d_out, 16 * NG)

        @block.gpsimd
        def _(pool):
            link, _n = chain(pool, pool_c)
            link(nc.gpsimd.memset(ident[:, :], 0.0))
            nc.gpsimd.affine_select(out=ident[:, :], in_=ident[:, :], compare_op=ALU.not_equal, fill=1.0,
                                    base=0, pattern=[[-1, P]], channel_multiplier=1).then_inc(pool_const, 1)
            link(nc.gpsimd.memset(KS[:, :, :, :, :].rearrange("p a c h n -> p (a c h n)").bitcast(F32), 0.0))
            last = nc.gpsimd.memset(KS[PR_ROWS:KR, :, :, 1, :].rearrange("p a c n -> p (a c) n").bitcast(F32), TWO_ONES)
            link(last)
            nc.gpsimd.memset(KS[PR_ROWS:PR_ROWS + 3, :, :, 0, :].rearrange("p a c n -> p (a c) n").bitcast(F32), TWO_ONES).then_inc(pool_const, 1)
            pool.wait_ge(pool_const, 2)
            pool.wait_ge(vd_zero, 1)
            link(nc.gpsimd.memset(VD[0:L, :, :, 2 * HD:2 * HD + 1], 1.0))
            nc.gpsimd.memset(VD[L:P, :, :, 2 * HD + 1:VW], 1.0).then_inc(pool_const, 1)
            pool.wait_ge(pool_const, 3)
            for j in range(JB):
                last = nc.gpsimd.iota(bin_id[NB * j:NB * (j + 1), :], [[0, 1]], base=0, channel_multiplier=1, allow_small_or_imprecise_dtypes=True)
            last.then_inc(pool_const, 1)
            pool.wait_ge(pool_const, 4)
            link(nc.gpsimd.memset(half_neg[:, :], -0.5))
            link(nc.gpsimd.memset(neg_alpha[:, :], -SELU_ALPHA))
            link(nc.gpsimd.memset(lnalpha[:, :], float(np.log(SELU_ALPHA))))
            link(nc.gpsimd.memset(ones_row[:, :], 1.0))
            pool.wait_ge(var_done, 1)
            nc.gpsimd.tensor_tensor(rstd[:, :], vare[:, :], half_neg[:, :], ALU.pow).then_inc(rstd_done, 1)
            pool.wait_ge(rstd_done, 1)
            link(nc.gpsimd.memset(lower[:, :], 1.0))
            link(nc.gpsimd.affine_select(out=lower[:, :], in_=lower[:, :], compare_op=ALU.is_gt, fill=0.0,
                                         base=0, pattern=[[1, P]], channel_multiplier=-1))
            link(nc.gpsimd.memset(ones_bf[:, :], 1.0))
            link(nc.gpsimd.iota(slot_iota[:, :], [[1, CAP]], base=0, channel_multiplier=0, allow_small_or_imprecise_dtypes=True))
            link(nc.gpsimd.iota(exp_iota[:, :], [[1, E]], base=0, channel_multiplier=0, allow_small_or_imprecise_dtypes=True))
            nc.gpsimd.tensor_copy(ident_bf[:, :], ident[:, :]).then_inc(pool_const, 1)
            pool.wait_ge(pool_const, 5)
            pool.wait_ge(d_bo, 16)
            pool.wait_ge(xn_done, NG)
            nc.gpsimd.tensor_tensor(X[:, :, :], X[:, :, :], bo_b[:, :].unsqueeze(1).broadcast_to([P, T, D]), ALU.add).then_inc(xb_done, 1)
            pool.wait_ge(xb_done, 1)
            for g in range(NG):
                pool.wait_ge(var2_done, g + 1)
                nc.gpsimd.tensor_tensor(rstd[:, tiles(g)], vare[:, tiles(g)], half_neg[:, tiles(g)], ALU.pow).then_inc(rstd2_done, 1)
            pool.wait_ge(mv2_done, T)
            nc.gpsimd.memset(G1[:, :, :].rearrange("p t n -> p (t n)").bitcast(F32), 0.0).then_inc(g1_zero, 1)
            pool.wait_ge(f_done, 1)
            pool.wait_ge(vs_done, 1)
            link(nc.gpsimd.tensor_tensor(w2[:, :, :], v8[:, :, 0:2], vs[:, :].unsqueeze(2).broadcast_to([P, T, 2]), ALU.mult))
            for k_ in range(2):
                last = nc.gpsimd.tensor_tensor(we[:, k_], eq[:, k_], w2[:, :, k_:k_ + 1].broadcast_to([P, T, E]), ALU.mult)
            link(last)
            link(nc.gpsimd.tensor_tensor(Wt[:, :, :], we[:, 0], we[:, 1], ALU.add))
            w3 = [XW[:, :, 3 * D + s * E:3 * D + (s + 1) * E] for s in range(3)]
            link(nc.gpsimd.tensor_copy(w3[0], Wt[:, :, :]))
            link(nc.gpsimd.tensor_tensor(Wr[:, :, :], Wt[:, :, :], w3[0], ALU.subtract))
            link(nc.gpsimd.tensor_copy(w3[1], Wr[:, :, :]))
            nc.gpsimd.tensor_tensor(w3[2], Wr[:, :, :], w3[1], ALU.subtract).then_inc(w3_done, 1)

        @block.scalar
        def _(act):
            act.dma_start(tab[:, :], emb[0:NB, :].unsqueeze(0).broadcast_to([JB, NB, H])).then_inc(d_tab, 16)
            act.dma_start(tab_last[:, :], emb[NB:NB + 1, :].broadcast_to([P, H])).then_inc(d_tab, 16)
            act.dma_start(base_f[:, 0].rearrange("p h c -> p (h c)"), emb[NB:NB + 1, :].broadcast_to([BR, H])).then_inc(d_tab, 16)
            for g in range(NG):
                act.dma_start(CX[:, tiles(g), :], cx_dram[:, tiles(g), :]).then_inc(d_cx[g], 16)
                if g == 0:
                    for i, w in ((1, Wk), (2, Wv)):
                        act.dma_start(w_att[:, i, :], w).then_inc(d_watt, 16)
                    for i, v in enumerate((bq, bk, bv)):
                        act.dma_start(bcols[:, i:i + 1], col(v)).then_inc(d_small, 16)
            for i, w in ((0, Wq), (3, Wo)):
                act.dma_start(w_att[:, i, :], w).then_inc(d_watt2, 16)
            act.dma_start(bo_b[:, :], row(bo).broadcast_to([P, D])).then_inc(d_bo, 16)

            def base_values(a, c):
                nc.scalar.activation(QS[PR_ROWS:KR, a, c:c + 2, :], base_m[:, c:c + 2].unsqueeze(2).broadcast_to([BR, 2, GTOK]),
                                     ACT.Copy).then_inc(base_rows, 1)

            def evac_ct(g):
                act.wait_ge(ct_tr, g + 1)
                if g >= 2:
                    act.wait_ge(k_mm, g - 1)
                    act.wait_ge(v_mm, g - 1)
                nc.scalar.activation(CT[:, g % 2, :].rearrange("p (b i j) -> p b i j", b=BG, j=JB),
                                     PTP[g % 2][:, :].rearrange("p (b j i) -> p b i j", b=BG, j=JB), ACT.Copy).then_inc(ct_ev, 1)

            def k_first(g):
                act.wait_ge(k_mm, g + 1)
                if g >= 2:
                    act.wait_ge(d_part["k"][g % 2], 16 * STORES * (g // 2))
                nc.scalar.activation(parts["k"][:, g % 2, 0, :], bank[g][:, :], ACT.Identity, bias=bcols[:, 1:2]).then_inc(k_hi, 1)

            def values(g):
                act.wait_ge(v_mm, g + 1)
                for h2 in range(2):
                    q = slice(h2 * L, (h2 + 1) * L)
                    nc.scalar.activation(VD[q, BG * g:BG * (g + 1), :, h2 * HD:(h2 + 1) * HD],
                                         (OPS, MPS)[g % 2][q, :].rearrange("p (b c d) -> p b c d", b=BG, c=HP), ACT.Copy).then_inc(v_ev, 1)

            def layer_norm(src, dst, g, done):
                for t in range(TG * g, TG * g + TG):
                    last = nc.scalar.activation(dst(t), src[:, t, :], ACT.Identity, scale=rstd[:, t:t + 1], bias=shift[:, t:t + 1])
                last.then_inc(done, 1)

            def ln_group(g):
                act.wait_ge(d_x[g], 16)
                act.wait_ge(shift_done, 1)
                if g >= 2:
                    act.wait_ge(xt_tr, g - 1)
                layer_norm(X, lambda t: XN[:, g % 2, t % TG, :], g, xn_done)

            def norm2(g):
                act.wait_ge(shift_done, g + 2)
                layer_norm(X, lambda t: XN2[:, t, :], g, n2_done)

            def evac_xt(g):
                act.wait_ge(xt_tr, g + 1)
                if g >= 2:
                    act.wait_ge(q_mm, g - 1)
                nc.scalar.activation(XT[:, g % 2, :], PTP[g % 2][:, :], ACT.Copy).then_inc(xt_ev, 1)

            def q_first(g):
                act.wait_ge(q_mm, g + 1)
                if g >= 2:
                    act.wait_ge(d_part["q"][g % 2], 16 * STORES * (g // 2))
                nc.scalar.activation(parts["q"][:, g % 2, 0, :], bank[g][:, :], ACT.Identity, bias=bcols[:, 3:4]).then_inc(q_hi, 1)

            evac_ct(0)
            evac_ct(1)
            act.wait_ge(df_done, 1)
            nc.scalar.activation(df, df, ACT.Square).then_inc(sq_done, 1)
            act.wait_ge(bcol_ready, 1)
            k_first(0)
            act.wait_ge(pool_const, 3)
            values(0)
            evac_ct(2)
            k_first(1)
            values(1)
            evac_ct(3)
            act.wait_ge(d2_clamped, 1)
            nc.scalar.activation(dv, d2, ACT.Sqrt).then_inc(sqrt_done, 1)
            ln_group(0)
            values(2)
            act.wait_ge(near_done, 1)
            nc.scalar.activation(sm, rt, ACT.Square, scale=MAX_DIST / NB).then_inc(edge_done, 1)
            evac_xt(0)
            ln_group(1)
            q_first(0)
            evac_xt(1)
            k_first(2)
            q_first(1)
            ln_group(2)
            values(3)
            evac_xt(2)
            ln_group(3)
            act.wait_ge(base_ready, 1)
            for c in range(0, HP, 2):
                base_values(0, c)
            k_first(3)
            q_first(2)
            evac_xt(3)
            q_first(3)
            def aot(t):
                act.wait_ge(ao_tr, t + 1)
                if t >= 2:
                    act.wait_ge(wo_mm, t - 1)
                nc.scalar.activation(AOT[:, t % 2, :], MPS[:, 0:P], ACT.Identity, bias=bcols[:, 2:3]).then_inc(aot_ev, 1)

            def first_part(g):
                act.wait_ge(n2_done, g + 1)
                nc.scalar.activation(XW[:, tiles(g), 0:D], XN2[:, tiles(g), :], ACT.Copy).then_inc(p0_done, 1)

            def second_part(g):
                act.wait_ge(x2r_done, g + 1)
                nc.scalar.activation(XW[:, tiles(g), D:2 * D], x2r[:, :, :], ACT.Copy).then_inc(p1_done, 1)

            def evac_n2(g):
                act.wait_ge(n2_tr, g + 1)
                if g == 0:
                    act.wait_ge(s_mm, T)
                nc.scalar.activation(XN2T[:, GTOK * g:GTOK * (g + 1)], PTP[g % 2][:, :], ACT.Copy).then_inc(n2_ev, 1)

            for t in range(T):
                act.wait_ge(sub_done, t + 1)
                nc.scalar.activation(PR[:, t % 2], PR[:, t % 2], ACT.Exp).then_inc(exp_done, 1)
                if t >= 2:
                    act.wait_ge(pv_mm, t - 1)
                for half in range(2):
                    act.wait_ge(p_tr, 2 * t + half + 1)
                    nc.scalar.activation(PT[:, t % 2, 4 * half:4 * half + 4, :].rearrange("p c n -> p (c n)"),
                                         PTP[half][:, :], ACT.Copy).then_inc(pt_ev, 1)
                if t >= 1:
                    aot(t - 1)
                if t < 2:
                    base_values(1, 4 * t)
                    base_values(1, 4 * t + 2)
                if 6 <= t < T - 2 and t % TG == 2:
                    norm2(t // TG - 1)
                    first_part(t // TG - 1)
                if 7 <= t < T - 2 and t % TG == 3:
                    second_part(t // TG - 1)
                if t == T - 2:
                    evac_n2(0)

            act.wait_ge(consts2, 1)
            for g in range(NG):
                for c in range(FC):
                    n = FC * g + c
                    act.wait_ge(h_mm, n + 1)
                    if n >= 2:
                        act.wait_ge(sg_done, n - 1)
                    nc.scalar.activation(GE[:, n % 2, :], SPS[n % 4][:, :], ACT.Exp, bias=gb_exp[:, c:c + 1])
                    nc.scalar.activation(GR[:, n % 2, :], SPS[n % 4][:, :], ACT.Relu, bias=gbi[:, c:c + 1]).then_inc(ge_done, 1)
                    if g == 0 and c == 1:
                        aot(T - 1)
                    if c == FC - 2 and g < NG - 1:
                        evac_n2(g + 1)
                if 1 <= g < NG - 1:
                    second_part(g + 1)
                if g < 2:
                    norm2(g + 2)
                    first_part(g + 2)
            act.wait_ge(d_ew, 16 * (2 * E + 2))
            for i in range(2):
                nc.scalar.activation(w_eo[:, 4 * i:4 * i + 4], w_eo[:, 4 * i:4 * i + 4], ACT.Copy, scale=SELU_SCALE).then_inc(eo_scaled, 1)
            for i in range(2):
                act.wait_ge(eb_mm, i + 1)
                nc.scalar.activation(ebo_rows[0:1, 4 * i:4 * i + 4, :].rearrange("a e h -> a (e h)"), SPS[2 + i][0:1, :], ACT.Copy).then_inc(eb_row, 1)
            act.wait_ge(consts2, 2)
            act.wait_ge(cnt_done, 1)
            outer = act.value_load(cnt_i[0:1, 0:1], min_val=1, max_val=P // CAND)
            inner = act.value_load(cnt_i[0:1, 1:2], min_val=1, max_val=MAXRI)
            with act.Fori(0, outer) as ro:
                for q in range(NC):
                    act.wait_ge(xc_mm, ro * NC + q + 1)
                    nc.scalar.activation(XC[:, q, :], bank[q][:, 0:XWW], ACT.Copy).then_inc(xc_ev, 1)
                for half in range(2):
                    act.wait_ge(g1_tr, ro * 2 + half + 1)
                    nc.scalar.activation(GT1[:, half * (T // 2):(half + 1) * (T // 2), :].rearrange("p t n -> p (t n)"),
                                         PTP[half][:, :].bitcast(BF16), ACT.Copy).then_inc(gt1_ev, 1)
                with act.Fori(ro * inner, ro * inner + inner) as k:
                    for i in range(2):
                        act.wait_ge(xg_mm, k * 2 + i + 1)
                        nc.scalar.activation(XG[:, i * 512:(i + 1) * 512], (OPS, MPS)[i][:, :], ACT.Copy).then_inc(xg_ev, 1)

                    def weigh(i):
                        if i == 0:
                            act.wait_ge(wsl_done, k + 1)
                        act.wait_ge(y_mm, k * NY + i + 1)
                        for j in range(2):
                            e = 2 * i + j
                            last = nc.scalar.activation(Y3[:, 0, e, :], YB[i][:, j * D:(j + 1) * D], ACT.Identity, scale=wsl[:, e:e + 1])
                        last.then_inc(y0_done, 1)

                    for e in range(E):
                        act.wait_ge(eh_mm, k * E + e + 1)
                        if e >= 2:
                            act.wait_ge(se_done, k * E + e - 1)
                        h = bank[e % 4]
                        for c in range(FC):
                            nc.scalar.activation(he[:, e % 2, c, :], h[:, c * CAP:(c + 1) * CAP], ACT.Exp, bias=eb_exp[:, e, c:c + 1])
                        for c in range(FC // 2):
                            last = nc.scalar.activation(hr[:, e % 2, c, :], h[:, c * CAP:(c + 1) * CAP], ACT.Relu, bias=ebi[:, e, c:c + 1])
                        last.then_inc(he_done, 1)
                        if e % 2 == 1 and e >= 3:
                            weigh((e - 3) // 2)
                    weigh(NY - 1)

        @block.vector
        def _(dve):
            link, _n = chain(dve, dve_c)

            nc.vector.memset(BD[:, :, :, :], 0.0).then_inc(bd_zero, 1)
            nc.vector.memset(VD[:, :, :, :], 0.0).then_inc(vd_zero, 1)
            dve.wait_ge(d_pos, 48)
            nc.vector.tensor_tensor(df, posq[:, :, :].unsqueeze(2).broadcast_to([P, T, L, 3]), posk, ALU.subtract).then_inc(df_done, 1)
            for g in range(NG):
                dve.wait_ge(d_x[g], 16)
                for t in range(TG * g, TG * g + TG):
                    last = nc.vector.bn_stats(stats[:, t, :], X[:, t, :])
                if g == 1:
                    dve.wait_ge(d_small, 48)
                    nc.vector.tensor_scalar(bcols[:, 3:4], bcols[:, 0:1], SC, None, ALU.mult).then_inc(bcol_ready, 1)
            link(last)
            for t in range(T):
                last = nc.vector.bn_aggr(mv[:, t, :], stats[:, t, :])
            link(last)
            nc.vector.tensor_scalar(vare[:, :], mv[:, :, 1], EPS, None, ALU.add).then_inc(var_done, 1)
            dve.wait_ge(d_watt2, 32)
            nc.vector.tensor_scalar(w_q[:, :], w_att[:, 0, :], SC, None, ALU.mult).then_inc(wq_scaled, 1)

            dve.wait_ge(sq_done, 1)
            link(nc.vector.tensor_tensor(d2, df[:, :, :, 0], df[:, :, :, 1], ALU.add))
            link(nc.vector.tensor_tensor(d2, d2, df[:, :, :, 2], ALU.add))
            nc.vector.tensor_scalar(d2, d2, 1e-30, 1e30, ALU.max, ALU.min).then_inc(d2_clamped, 1)

            def split(s, g, first_step=False):
                hi, bias, done_r = ((k_hi, bcols[:, 1:2], k_r), (q_hi, bcols[:, 3:4], q_r))[s == "q"]
                dve.wait_ge(hi, g + 1)
                p3 = parts[s][:, g % 2]
                nc.vector.scalar_tensor_tensor(out=rest[:, :], in0=bank[g][:, :], scalar=bias, in1=p3[:, 0, :],
                                               op0=ALU.add, op1=ALU.subtract).then_inc(done_r, 1)
                if first_step:
                    return
                split_end(s, g)

            def split_end(s, g):
                done_r, done = ((k_r, k_parts), (q_r, q_parts))[s == "q"]
                p3 = parts[s][:, g % 2]
                dve.wait_ge(done_r, g + 1)
                link(nc.vector.tensor_copy(p3[:, 1, :], rest[:, :]))
                nc.vector.tensor_tensor(p3[:, 2, :], rest[:, :], p3[:, 1, :], ALU.subtract).then_inc(done, 1)
                dve.wait_ge(done, g + 1)

            def shifts(ts):
                return nc.vector.scalar_tensor_tensor(out=shift[:, ts], in0=mv[:, ts, 0], scalar=-1.0, in1=rstd[:, ts], op0=ALU.mult, op1=ALU.mult)

            dve.wait_ge(rstd_done, 1)
            shifts(slice(0, T)).then_inc(shift_done, 1)
            dve.wait_ge(shift_done, 1)
            split("k", 0)
            dve.wait_ge(sqrt_done, 1)
            link(nc.vector.tensor_scalar(dv, dv, NB / MAX_DIST, float(NB), ALU.mult, ALU.min))
            nc.vector.tensor_scalar(rt, dv, 2.0 ** 23, -2.0 ** 23, ALU.add, ALU.add).then_inc(near_done, 1)
            dve.wait_ge(d_tab, 48)
            link(nc.vector.tensor_tensor(tab[:, :], tab[:, :], tab_last[:, :], ALU.subtract))
            link(nc.vector.tensor_copy(tab_h[:, 0], tab[:, :]))
            link(nc.vector.tensor_tensor(tab_r[:, :], tab[:, :], tab_h[:, 0], ALU.subtract))
            link(nc.vector.tensor_copy(tab_h[:, 1], tab_r[:, :]))
            link(nc.vector.tensor_tensor(tab_h[:, 2], tab_r[:, :], tab_h[:, 1], ALU.subtract))
            dve.wait_ge(bd_zero, 1)
            for j in range(JB):
                q = slice(NB * j, NB * (j + 1))
                nc.vector.tensor_copy(BD[q, :, :, j], tab_h[q, :, :]).then_inc(bd_ready, 1)
            dve.wait_ge(edge_done, 1)
            link(nc.vector.tensor_tensor(dv, sm, d2, ALU.is_gt))
            nc.vector.tensor_tensor(binv[:, :, :], rt, dv, ALU.subtract).then_inc(bins_done, 1)
            split("q", 0)
            split("k", 1)
            odd_even = base_f[:, 0].rearrange("p a b -> p (a b)").rearrange("p (c h) -> p c h", h=2)
            link(nc.vector.tensor_copy(base_f[:, 1, 0, :], odd_even[:, :, 0]))
            link(nc.vector.tensor_tensor(base_f[:, 1, 1, :], odd_even[:, :, 1], odd_even[:, :, 0], ALU.subtract))
            for s in range(3):
                link(nc.vector.tensor_copy(base_s[:, s], base_f[:, 1]))
                if s < 2:
                    link(nc.vector.tensor_tensor(base_f[:, 1], base_f[:, 1], base_s[:, s], ALU.subtract))
            dve.wait_ge(pool_const, 1)
            link(nc.vector.memset(base_m[:, :], 0.0))
            for r in range(BR):
                last = nc.vector.scalar_tensor_tensor(out=base_m[:, :], in0=base_s[:, r % 3, r // 3], scalar=ident[PR_ROWS:KR, PR_ROWS + r:PR_ROWS + r + 1],
                                                      in1=base_m[:, :], op0=ALU.mult, op1=ALU.add)
                if r < BR - 1:
                    link(last)
            last.then_inc(base_ready, 1)

            def one_hot(t):
                dve.wait_ge(d_bb[t % 4], 16 * (t // 4 + 1))
                if t >= 2:
                    dve.wait_ge(s_mm, t - 1)
                nc.vector.tensor_scalar(OH[:, t % 2, :], BB[:, t % 4, :], bin_id[:, 0:1], None, ALU.is_equal).then_inc(oh_done, 1)

            def shifts2(g):
                dve.wait_ge(rstd2_done, g + 1)
                shifts(tiles(g)).then_inc(shift_done, 1)

            def parts2(g):
                dve.wait_ge(p0_done, g + 1)
                nc.vector.tensor_tensor(x2r[:, :, :], XN2[:, tiles(g), :], XW[:, tiles(g), 0:D], ALU.subtract).then_inc(x2r_done, 1)

            def parts2_end(g):
                dve.wait_ge(x2r_done, g + 1)
                dve.wait_ge(p1_done, g + 1)
                nc.vector.tensor_tensor(XW[:, tiles(g), 2 * D:3 * D], x2r[:, :, :], XW[:, tiles(g), D:2 * D], ALU.subtract).then_inc(p2_done, 1)
                dve.wait_ge(p2_done, g + 1)

            def after_attention(r, t):
                if r is not None:
                    dve.wait_ge(wo_mm, r + 1)
                    nc.vector.tensor_tensor(X[:, r, :], X[:, r, :], MPS[:, P:2 * P], ALU.add).then_inc(x2_done, 1)
                if t is not None:
                    dve.wait_ge(pv_mm, t + 1)
                    o = OPS[:, 0:HP * VW].rearrange("p (c w) -> p c w", w=VW)
                    nc.vector.reciprocal(rsum[:, :].rearrange("p (c h) -> p c h", h=2), o[:, :, 2 * HD:VW]).then_inc(rsum_done, 1)
                if r is not None:
                    dve.wait_ge(x2_done, r + 1)
                    nc.vector.bn_stats(stats[:, r, :], X[:, r, :]).then_inc(stats_done, 1)
                if t is not None:
                    dve.wait_ge(rsum_done, t + 1)
                    if t >= 2:
                        dve.wait_ge(ao_tr, t - 1)
                    nc.vector.tensor_tensor(AO[:, t % 2, :].rearrange("p (c h d) -> p c h d", c=HP, h=2),
                                            o[:, :, 0:2 * HD].rearrange("p c (h d) -> p c h d", h=2),
                                            rsum[:, :].rearrange("p (c h) -> p c h", h=2).unsqueeze(3).broadcast_to([P, HP, 2, HD]),
                                            ALU.mult).then_inc(ao_done, 1)
                if r is not None:
                    dve.wait_ge(stats_done, r + 1)
                    nc.vector.bn_aggr(mv[:, r, :], stats[:, r, :]).then_inc(mv2_done, 1)
                    if r % TG == TG - 1:
                        dve.wait_ge(mv2_done, r + 1)
                        g = r // TG
                        nc.vector.tensor_scalar(vare[:, tiles(g)], mv[:, tiles(g), 1], EPS, None, ALU.add).then_inc(var2_done, 1)

            dve.wait_ge(pool_const, 4)
            split("q", 1)
            one_hot(0)
            split("k", 2)
            split("k", 3)
            split("q", 2)
            one_hot(1)
            split("q", 3, first_step=True)
            for t in range(T):
                if t == 2:
                    dve.wait_ge(xb_done, 1)
                dve.wait_ge(s_mm, t + 1)
                rows = pair[t % 2][:, :].rearrange("p (i h k) -> p h i k", i=2, h=H)
                link(nc.vector.reduce_max(mx[:, t % 2], rows, AX.XY))
                if t >= 2:
                    dve.wait_ge(p_tr, 2 * (t - 1))
                nc.vector.tensor_tensor(PR[:, t % 2].rearrange("p h (i k) -> p h i k", i=2), rows,
                                        mx[:, t % 2].unsqueeze(2).unsqueeze(3).broadcast_to([P, H, 2, L // 2]), ALU.subtract).then_inc(sub_done, 1)
                if t + 2 < T:
                    one_hot(t + 2)
                if t >= 1:
                    after_attention(t - 2 if t >= 2 else None, t - 1)
                if t == 0:
                    split_end("q", NG - 1)
                if t >= 6 and t % TG == 2:
                    shifts2(t // TG - 1)
                if 7 <= t < T - 1 and t % TG == 3:
                    parts2(t // TG - 1)
                if t >= 8 and t % TG == 0:
                    parts2_end(t // TG - 2)
                if t == 9:
                    dve.wait_ge(d_gate, 64)
                    nc.vector.tensor_scalar(w_go[:, :, :], w_go[:, :, :], SELU_SCALE, None, ALU.mult)
                    nc.vector.tensor_scalar(gb_exp[:, :], gbi[:, :], float(np.log(SELU_ALPHA)), None, ALU.add).then_inc(consts2, 1)
            after_attention(None, T - 1)
            after_attention(T - 2, None)

            dve.wait_ge(pool_const, 5)

            def gate_logits(g, us, n, o):
                dve.wait_ge(lg_mm, n)
                nc.vector.tensor_tensor(LG[:, us, :], o[:, :].rearrange("p (t h) -> p t h", t=TG)[:, us, :],
                                        gbo_b[:, :].unsqueeze(1).broadcast_to([P, us.stop - us.start, D]), ALU.add).then_inc(lg_ev, 1)
                dve.wait_ge(lg_ev, n)

            def maxima(g, us):
                for u in range(us.start, us.stop):
                    last = nc.vector.max(v8[:, TG * g + u, :], LG[:, u, :])
                link(last)

            def places_of_maxima(g, us):
                for u in range(us.start, us.stop):
                    last = nc.vector.max_index(i8[:, TG * g + u, :], v8[:, TG * g + u, :], LG[:, u, :])
                return last

            every = slice(0, TG)

            def choose():
                ts = slice(0, T)
                e_ = lambda a: a[:, :].unsqueeze(1).broadcast_to([P, T, E])
                link(nc.vector.tensor_copy(i2f[:, ts, :], i8[:, ts, 0:2]))
                for k_ in range(2):
                    last = nc.vector.tensor_tensor(eq[:, k_, ts], i2f[:, ts, k_:k_ + 1].broadcast_to([P, T, E]), e_(exp_iota), ALU.is_equal)
                link(last)
                link(nc.vector.tensor_tensor(XW[:, ts, 3 * D + 3 * E:], eq[:, 0, ts], eq[:, 1, ts], ALU.add))
                nc.vector.reduce_max(Ub[:, ts], XW[:, ts, 3 * D + 3 * E:], AX.X).then_inc(f_done, 1)
                link(nc.vector.tensor_tensor(vs[:, ts], v8[:, ts, 0], v8[:, ts, 1], ALU.add))
                nc.vector.reciprocal(vs[:, ts], vs[:, ts]).then_inc(vs_done, 1)

            for g in range(NG):
                for c in range(FC):
                    n = FC * g + c
                    dve.wait_ge(ge_done, n + 1)
                    if c == 0 and g >= 2:
                        dve.wait_ge(lg_mm, g - 1)
                    nc.vector.scalar_tensor_tensor(out=SG[:, g % 2, c, :], in0=GE[:, n % 2, :], scalar=SELU_ALPHA,
                                                   in1=GR[:, n % 2, :], op0=ALU.min, op1=ALU.add).then_inc(sg_done, 1)
                    if n == 1:
                        after_attention(T - 1, None)
                    if g == 2 and c == 0:
                        parts2(NG - 1)
                    if g == 3 and c == 0:
                        link(places_of_maxima(1, every))
                    if g == 3 and c == 1:
                        parts2_end(NG - 1)
                if g == 0:
                    dve.wait_ge(gb_mm, 1)
                    nc.vector.tensor_tensor(gbo_b[:, :], gbo_b[:, :], OPS[:, 0:D], ALU.add).then_inc(gb_ready, 1)
                    dve.wait_ge(gb_ready, 1)
                    shifts2(NG - 1)
                    parts2(NG - 2)
                    dve.wait_ge(d_ew, 16 * (2 * E + 2))
                    nc.vector.tensor_scalar(eb_lin[:, :, :], ebi[:, :, :], -SELU_ALPHA, None, ALU.add)
                    nc.vector.tensor_scalar(eb_exp[:, :, :], ebi[:, :, :], float(np.log(SELU_ALPHA)), None, ALU.add).then_inc(consts2, 1)
                    dve.wait_ge(consts2, 2)
                if g >= 1:
                    gate_logits(g - 1, every, g, (OPS, MPS)[(g - 1) % 2])
                    maxima(g - 1, every)
                    if g != 2:
                        link(places_of_maxima(g - 1, every))
                if g == 1:
                    parts2_end(NG - 2)
            for u in range(TG):
                one = slice(u, u + 1)
                gate_logits(NG - 1, one, NG + u, LGB[u])
                maxima(NG - 1, one)
                last = places_of_maxima(NG - 1, one)
            link(last)
            choose()
            ts = slice(0, T)
            FAR = 4.0 * B * L
            link(nc.vector.tensor_scalar(rank[:, :], Ub[:, :], -FAR, FAR, ALU.mult, ALU.add))
            dve.wait_ge(rank_mm, 1)
            link(nc.vector.tensor_tensor(rank[:, :], rank[:, :], MPS[:, T * E:T * E + T], ALU.add))
            nc.vector.reduce_max(cnt[:, 0:1], MPS[:, T * E + T:T * E + 2 * T], AX.X)
            link(nc.vector.reduce_sum(cnt[:, 2:], MPS[:, 0:T * E].rearrange("p (t e) -> p e t", e=E), AX.X))
            link(nc.vector.reduce_max(cnt[:, 1:2], cnt[:, 2:], AX.X))
            nc.vector.tensor_scalar(cnt[:, 0:1], cnt[:, 0:1], float(CAND - 1), float(CAND), ALU.add, ALU.max)
            link(nc.vector.tensor_scalar(cnt[:, 1:2], cnt[:, 1:2], float(CAP - 1), float(CAP), ALU.add, ALU.max))
            link(nc.vector.tensor_scalar(cnt[:, 1:2], cnt[:, 1:2], float(MAXRI * CAP), None, ALU.min))
            link(nc.vector.tensor_copy(cnt_i[:, :], cnt[:, 0:2]))
            nc.vector.tensor_scalar(cnt_i[:, 0:1], cnt_i[:, 0:1], CAND.bit_length() - 1, None, ALU.logical_shift_right).then_inc(cnt_half, 1)
            nc.vector.tensor_scalar(cnt_i[:, 1:2], cnt_i[:, 1:2], CAP.bit_length() - 1, None, ALU.logical_shift_right).then_inc(cnt_done, 1)
            dve.wait_ge(cnt_half, 1)
            dve.wait_ge(cnt_done, 1)
            outer = dve.value_load(cnt_i[0:1, 0:1], min_val=1, max_val=P // CAND)
            inner = dve.value_load(cnt_i[0:1, 1:2], min_val=1, max_val=MAXRI)
            OSTEPS, ISTEPS = 4, 9
            dve.wait_ge(g1_zero, 1)
            with dve.Fori(0, outer) as ro:
                olink, on = chain(dve, dve_outer, ro * OSTEPS)
                for j in range(TG):
                    last = nc.vector.tensor_tensor(G1[:, j::TG, j * CAND:(j + 1) * CAND],
                                                   rank[:, j::TG].unsqueeze(2).broadcast_to([P, NC, CAND]),
                                                   slot_iota[:, 0:CAND].unsqueeze(1).broadcast_to([P, NC, CAND]), ALU.is_equal)
                last.then_inc(g1_done, 1)
                dve.wait_ge(g1_done, ro + 1)
                olink(nc.vector.tensor_scalar(rank[:, :], rank[:, :], -float(CAND), None, ALU.add))
                olink(nc.vector.memset(OC[:, :, :], 0.0))
                dve.wait_ge(mem_mm, ro + 1)
                nc.vector.tensor_copy(memc[:, :, :], OPS[:, 0:NC * E].rearrange("p (q e) -> p q e", e=E)).then_inc(mem_ev, 1)
                dve.wait_ge(mem_ev, ro + 1)
                olink(nc.vector.tensor_scalar(slot[:, :, :], memc[:, :, :], -FAR, FAR, ALU.mult, ALU.add))
                dve.wait_ge(slot_mm, ro + 1)
                olink(nc.vector.tensor_tensor(slot[:, :, :], slot[:, :, :], MPS[:, 0:NC * E].rearrange("p (q e) -> p q e", e=E), ALU.add))
                with dve.Fori(ro * inner, ro * inner + inner) as k:
                    ilink, inn = chain(dve, dve_inner, k * ISTEPS)
                    for q in range(NC):
                        last = nc.vector.tensor_tensor(G2[:, q, :].rearrange("p (e s) -> p e s", e=E),
                                                       slot[:, q, :].unsqueeze(2).broadcast_to([P, E, CAP]),
                                                       slot_iota[:, :].unsqueeze(1).broadcast_to([P, E, CAP]), ALU.is_equal)
                        last.then_inc(g2_done, 1)
                    dve.wait_ge(g2_done, k * NC + NC)
                    ilink(nc.vector.tensor_scalar(slot[:, :, :], slot[:, :, :], -float(CAP), None, ALU.add))

                    def evac_gt2(q):
                        dve.wait_ge(g2_tr, k * NC + q + 1)
                        nc.vector.tensor_copy(GT2[:, q].rearrange("p e n -> p (e n)"), PTP[q % 2][:, :].bitcast(BF16)).then_inc(gt2_ev, 1)

                    def selu(e):
                        dve.wait_ge(he_done, k * E + e + 1)
                        for c in range(FC // 2, FC):
                            last = nc.vector.tensor_scalar(hr[:, e % 2, c, :], bank[e % 4][:, c * CAP:(c + 1) * CAP],
                                                           eb_lin[:, e, c:c + 1], -SELU_ALPHA, ALU.add, ALU.max)
                        last.then_inc(hr_done, 1)
                        dve.wait_ge(hr_done, k * E + e + 1)
                        nc.vector.scalar_tensor_tensor(out=SE[:, e], in0=he[:, e % 2], scalar=SELU_ALPHA, in1=hr[:, e % 2],
                                                       op0=ALU.min, op1=ALU.add).then_inc(se_done, 1)

                    def weigh_rest(i):
                        dve.wait_ge(y0_done, k * NY + i + 1)
                        for j in range(2):
                            e = 2 * i + j
                            last = nc.vector.scalar_tensor_tensor(out=Yr[:, i % 2, j], in0=YB[i][:, j * D:(j + 1) * D], scalar=wsl[:, e:e + 1],
                                                                  in1=Y3[:, 0, e, :], op0=ALU.mult, op1=ALU.subtract)
                        last.then_inc(yr_done, 1)
                        dve.wait_ge(yr_done, k * NY + i + 1)
                        es = slice(2 * i, 2 * i + 2)
                        nc.vector.tensor_copy(Y3[:, 1, es], Yr[:, i % 2]).then_inc(yb_done, 1)
                        dve.wait_ge(yb_done, k * NY + i + 1)
                        nc.vector.tensor_tensor(Y3[:, 2, es], Yr[:, i % 2], Y3[:, 1, es], ALU.subtract).then_inc(y3_done, 1)

                    evac_gt2(0)
                    evac_gt2(1)
                    dve.wait_ge(ws_mm, k + 1)
                    nc.vector.reduce_sum(wsl[:, :], OPS[:, 0:3 * E].rearrange("p (e s) -> p e s", s=3), AX.X).then_inc(wsl_done, 1)
                    dve.wait_ge(wsl_done, k + 1)
                    evac_gt2(2)
                    selu(0)
                    evac_gt2(3)
                    for e in range(1, E):
                        selu(e)
                        if e % 2 == 1 and e >= 3:
                            weigh_rest((e - 3) // 2)
                    weigh_rest(NY - 1)
                    for half in range(2):
                        qs = slice(2 * half, 2 * half + 2)
                        dve.wait_ge(sc_mm, k * 2 + half + 1)
                        ilink(nc.vector.tensor_tensor(OC[:, qs, :], OC[:, qs, :], SCB[half][:, :].rearrange("p (q h) -> p q h", q=NC)[:, qs, :], ALU.add))
                        ilink(nc.vector.tensor_copy(OC3[:, 0, qs], OC[:, qs, :]))
                        ilink(nc.vector.tensor_tensor(OCr[:, qs, :], OC[:, qs, :], OC3[:, 0, qs], ALU.subtract))
                        ilink(nc.vector.tensor_copy(OC3[:, 1, qs], OCr[:, qs, :]))
                        nc.vector.tensor_tensor(OC3[:, 2, qs], OCr[:, qs, :], OC3[:, 1, qs], ALU.subtract).then_inc(oc3_done[half], 1)
                    assert inn[0] == ISTEPS, inn
                for q in range(NC):
                    dve.wait_ge(back_mm, ro * NC + q + 1)
                    nc.vector.tensor_tensor(X[:, tiles(q), :], X[:, tiles(q), :], BKB[q][:, :].rearrange("p (t h) -> p t h", t=TG), ALU.add).then_inc(x_back[q], 1)
                for q in range(NC):
                    dve.wait_ge(x_back[q], ro + 1)
                assert on[0] == OSTEPS, on

        @block.tensor
        def _(pe):
            mm, tr = nc.tensor.matmul, nc.tensor.transpose

            def ctx_transposes(g):
                pe.wait_ge(d_cx[g], 16)
                if g >= 2:
                    pe.wait_ge(ct_ev, g - 1)
                for u in range(TG):
                    last = tr(PTP[g % 2][:, u * P:(u + 1) * P], CX[:, TG * g + u, :], ident[:, :])
                last.then_inc(ct_tr, 1)

            def project_kv(g):
                pe.wait_ge(ct_ev, g + 1)
                mm(bank[g][:, :], w_att[:, 1, :], CT[:, g % 2, :], start=True, stop=True).then_inc(k_mm, 1)
                if g >= 2:
                    pe.wait_ge(v_ev, 2 * (g - 1))
                wv = w_att[:, 2, :].rearrange("p (c h d) -> p h c d", h=2, d=HD)
                for b in range(BG):
                    for h2 in range(2):
                        last = mm((OPS, MPS)[g % 2][h2 * L:(h2 + 1) * L, b * L:(b + 1) * L],
                                  CT[:, g % 2, b * L:(b + 1) * L], wv[:, h2], start=True, stop=True)
                last.then_inc(v_mm, 1)

            pe.wait_ge(pool_const, 1)
            ctx_transposes(0)
            ctx_transposes(1)
            pe.wait_ge(d_watt, 32)
            for g in range(NG):
                project_kv(g)
                if g + 2 < NG:
                    ctx_transposes(g + 2)

            def x_transposes(g):
                pe.wait_ge(xn_done, g + 1)
                if g >= 2:
                    pe.wait_ge(xt_ev, g - 1)
                else:
                    pe.wait_ge(ct_ev, NG)
                for u in range(TG):
                    last = tr(PTP[g % 2][:, u * P:(u + 1) * P], XN[:, g % 2, u, :], ident[:, :])
                last.then_inc(xt_tr, 1)

            def project_q(g):
                pe.wait_ge(xt_ev, g + 1)
                pe.wait_ge(k_r, g + 1)
                mm(bank[g][:, :], w_q[:, :], XT[:, g % 2, :], start=True, stop=True).then_inc(q_mm, 1)

            pe.wait_ge(wq_scaled, 1)
            for g in range(2):
                x_transposes(g)
                project_q(g)

            def biases(t):
                two = 2 * (t % 2)
                if t == 0:
                    pe.wait_ge(bd_ready, JB)
                if t < 2:
                    pe.wait_ge(q_r, 2 * (t + 1))
                else:
                    pe.wait_ge(sub_done, t - 1)
                pe.wait_ge(oh_done, t + 1)
                for i in range(IB):
                    ih, i8_ = i // 8, i % 8
                    o = SPS[two + ih][:, :].rearrange("p (h i j) -> p i h j", h=H, i=8)[:, i8_]
                    for s in range(3):
                        mm(o, OH[:, t % 2, i * P:(i + 1) * P], BD[:, s], start=(i8_ == 0 and s == 0), stop=False, skip_group_check=True)

            def scores(t):
                g, two = t // TG, 2 * (t % 2)
                if t % TG == 0 and g < 2:
                    pe.wait_ge(base_rows, HP // 2 * (g + 1))
                if t % TG == 0:
                    for s in "qk":
                        pe.wait_ge(d_stack[s][g % 2], 16 * STACKS[s] * (g // 2 + 1))
                for b2 in range(2):
                    q0 = (t % TG) * P + b2 * L
                    for c in range(HP):
                        for ih in range(2):
                            last = mm(SPS[two + ih][b2 * L:(b2 + 1) * L, c * L:(c + 1) * L],
                                      QS[:, g % 2, c, q0:q0 + L],
                                      KS[:, g % 2, c, :, q0 + ih * (L // 2):q0 + (ih + 1) * (L // 2)],
                                      start=False, stop=True, skip_group_check=True)
                last.then_inc(s_mm, 1)

            def p_transposes(t):
                pe.wait_ge(exp_done, t + 1)
                for half in range(2):
                    if t >= 1:
                        pe.wait_ge(pt_ev, 2 * (t - 1) + half + 1)
                    else:
                        pe.wait_ge(xt_ev, NG)
                    for c in range(4):
                        cc = 4 * half + c
                        last = tr(PTP[half][:, c * P:(c + 1) * P], PR[:, t % 2, 2 * cc:2 * cc + 2, :].rearrange("p h k -> p (h k)"), ident[:, :])
                    last.then_inc(p_tr, 1)

            def p_v(t):
                if t >= 1:
                    pe.wait_ge(ao_done, t)
                else:
                    pe.wait_ge(v_ev, 2 * NG)
                for c in range(HP):
                    if c % 4 == 0:
                        pe.wait_ge(pt_ev, 2 * t + c // 4 + 1)
                    for b2 in range(2):
                        last = mm(OPS[b2 * L:(b2 + 1) * L, c * VW:(c + 1) * VW], PT[:, t % 2, c, b2 * L:(b2 + 1) * L],
                                  VD[:, 2 * t + b2, c, :], start=True, stop=True)
                last.then_inc(pv_mm, 1)

            def ao_transpose(t):
                pe.wait_ge(ao_done, t + 1)
                if t >= 1:
                    pe.wait_ge(x2_done, t)
                tr(MPS[:, 0:P], AO[:, t % 2, :], ident[:, :]).then_inc(ao_tr, 1)

            def out_project(t):
                pe.wait_ge(aot_ev, t + 1)
                mm(MPS[:, P:2 * P], AOT[:, t % 2, :], w_att[:, 3, :], start=True, stop=True).then_inc(wo_mm, 1)

            x_transposes(2)
            biases(0)
            project_q(2)
            x_transposes(3)
            scores(0)
            project_q(3)
            biases(1)
            scores(1)
            def n2_transposes(g):
                pe.wait_ge(n2_done, g + 1)
                if g >= 2:
                    pe.wait_ge(n2_ev, g - 1)
                else:
                    pe.wait_ge(pt_ev, 2 * (T - 1 + g) - 1 + g)
                for u in range(TG):
                    last = tr(PTP[g % 2][:, u * P:(u + 1) * P], XN2[:, TG * g + u, :], ident[:, :])
                last.then_inc(n2_tr, 1)

            def hidden(g, c):
                n = FC * g + c
                if n == 0:
                    pe.wait_ge(d_gate, 64)
                if n in (0, 2):
                    pe.wait_ge(sub_done, T - 1 + n // 2)
                if c == 0:
                    pe.wait_ge(n2_ev, g + 1)
                if n >= 4:
                    pe.wait_ge(sg_done, n - 3)
                mm(SPS[n % 4][:, :], w_gi[:, c * P:(c + 1) * P], XN2T[:, GTOK * g:GTOK * (g + 1)], start=True, stop=True).then_inc(h_mm, 1)

            for t in range(T):
                if t == T - 1:
                    hidden(0, 0)
                    pe.wait_ge(n2_ev, 1)
                p_transposes(t)
                if t >= 1:
                    ao_transpose(t - 1)
                if t + 2 < T:
                    biases(t + 2)
                if t == T - 2:
                    n2_transposes(0)
                if t == T - 1:
                    hidden(0, 1)
                p_v(t)
                if t >= 1:
                    out_project(t - 1)
                if t + 2 < T:
                    scores(t + 2)

            def gate_correction():
                for c in range(FC):
                    last = mm(OPS[:, 0:D], neg_alpha[:, :], w_go[:, c, :], start=(c == 0), stop=(c == FC - 1))
                last.then_inc(gb_mm, 1)

            def expert_corrections():
                for i in range(2):
                    pe.wait_ge(eo_scaled, i + 1)
                    for c in range(FC // 2):
                        last = mm(SPS[2 + i][0:1, :], neg_alpha[:, 0:1], w_eo[:, 4 * i:4 * i + 4, c, :], start=(c == 0), stop=(c == FC // 2 - 1))
                    last.then_inc(eb_mm, 1)

            def logits(g):
                pe.wait_ge(sg_done, FC * (g + 1))
                if g >= 2:
                    pe.wait_ge(lg_ev, g - 1)
                else:
                    pe.wait_ge(x2_done, T)
                last_group = g == NG - 1
                if g == 0:
                    pe.wait_ge(gb_ready, 1)
                for u in range(TG):
                    o = LGB[u] if last_group else (OPS, MPS)[g % 2]
                    for c in range(FC):
                        last = mm(o[:, u * D:(u + 1) * D], SG[:, g % 2, c, u * P:(u + 1) * P], w_go[:, c, :], start=(c == 0), stop=(c == FC - 1))
                    if last_group or u == TG - 1:
                        last.then_inc(lg_mm, 1)

            hidden(0, 2)
            ao_transpose(T - 1)
            hidden(0, 3)
            n2_transposes(1)
            out_project(T - 1)
            pe.wait_ge(consts2, 1)
            gate_correction()
            for g in range(1, NG):
                for c in range(FC):
                    hidden(g, c)
                if g < NG - 1:
                    n2_transposes(g + 1)
                logits(g - 1)
            pe.wait_ge(pool_const, 5)
            logits(NG - 1)
            pe.wait_ge(f_done, 1)
            mm(MPS[:, 0:T * E].rearrange("p (t e) -> p t e", e=E), ones_bf[:, :], XW[:, :, 3 * D + 3 * E:], start=True, stop=True)
            mm(MPS[:, T * E:T * E + T], lower[:, :], Ub[:, :], start=True, stop=True)
            mm(MPS[:, T * E + T:T * E + 2 * T], ones_bf[:, :], Ub[:, :], start=True, stop=True).then_inc(rank_mm, 1)
            expert_corrections()
            pe.wait_ge(cnt_done, 1)
            pe.wait_ge(d_ew, 16 * (2 * E + 2))
            outer = pe.value_load(cnt_i[0:1, 0:1], min_val=1, max_val=P // CAND)
            inner = pe.value_load(cnt_i[0:1, 1:2], min_val=1, max_val=MAXRI)
            pe.wait_ge(eb_row, 2)
            with pe.Fori(0, outer) as ro:
                pe.wait_ge(g1_done, ro + 1)
                for q in range(NC):
                    for j in range(TG):
                        last = mm(OPS[:, q * E:(q + 1) * E], G1[:, TG * q + j, :], XW[:, TG * q + j, 3 * D + 3 * E:], start=(j == 0), stop=(j == TG - 1))
                last.then_inc(mem_mm, 1)

                def places():
                    pe.wait_ge(mem_ev, ro + 1)
                    for q in range(NC - 1):
                        mm(MPS[:, (q + 1) * E:NC * E].rearrange("p (q e) -> p q e", e=E), ones_bf[:, :],
                           memc[:, q:q + 1, :].broadcast_to([P, NC - 1 - q, E]), start=(q == 0), stop=False, skip_group_check=True)
                    mm(MPS[:, 0:NC * E].rearrange("p (q e) -> p q e", e=E), lower[:, :], memc[:, :, :], start=False, stop=True,
                       skip_group_check=True).then_inc(slot_mm, 1)

                def g1_transposes(half):
                    pb = PTP[half][:, :].bitcast(BF16)
                    for u in range(T // 2):
                        last = tr(pb[:, u * P:(u + 1) * P], G1[:, half * (T // 2) + u, :], ident_bf[:, :])
                    last.then_inc(g1_tr, 1)

                g1_transposes(0)
                places()
                pe.wait_ge(w3_done, 1)
                for q in range(NC):
                    for j in range(TG):
                        last = mm(bank[q][:, 0:XWW], G1[:, TG * q + j, :], XW[:, TG * q + j, :], start=(j == 0), stop=(j == TG - 1))
                    last.then_inc(xc_mm, 1)
                g1_transposes(1)
                with pe.Fori(ro * inner, ro * inner + inner) as k:
                    for q in range(NC):
                        pe.wait_ge(g2_done, k * NC + q + 1)
                        pe.wait_ge(xc_ev, ro * NC + q + 1)
                        for s in range(3):
                            for i in range(2):
                                last = mm((OPS, MPS)[i][:, :], XC[:, q, s * D:(s + 1) * D], G2[:, q, i * 512:(i + 1) * 512],
                                          start=(q == 0 and s == 0), stop=(q == NC - 1 and s == 2))
                                if q == NC - 1 and s == 2:
                                    last.then_inc(xg_mm, 1)
                    def g2_transposes(q):
                        if q >= 2:
                            pe.wait_ge(gt2_ev, k * NC + q - 1)
                        pb = PTP[q % 2][:, :].bitcast(BF16)
                        for e in range(E):
                            last = tr(pb[:, e * P:(e + 1) * P], G2[:, q, e * CAP:(e + 1) * CAP], ident_bf[:, :])
                        last.then_inc(g2_tr, 1)

                    def hidden(e):
                        if e >= 4:
                            pe.wait_ge(se_done, k * E + e - 3)
                        b = bank[e % 4]
                        for c in range(FC):
                            last = mm(b[:, c * CAP:(c + 1) * CAP], w_ei[:, e, c * P:(c + 1) * P], XG[:, e * CAP:(e + 1) * CAP],
                                      start=True, stop=True)
                        last.then_inc(eh_mm, 1)

                    def output(e):
                        i, j = e // 2, e % 2
                        pe.wait_ge(se_done, k * E + e + 1)
                        if e == 0:
                            pe.wait_ge(wsl_done, k + 1)
                        if e == 4:
                            pe.wait_ge(gt2_ev, k * NC + NC)
                        if e == E - 2:
                            pe.wait_ge(yr_done, k * NY + 1)
                        o = YB[i][:, j * D:(j + 1) * D]
                        mm(o, ones_row[:, :], ebo_rows[:, e, :], start=True, stop=False)
                        for c in range(FC):
                            last = mm(o, SE[:, e, c, :], w_eo[:, e, c, :], start=False, stop=(c == FC - 1))
                        if j == 1:
                            last.then_inc(y_mm, 1)

                    def scatter(i, half):
                        pe.wait_ge(y3_done, k * NY + i + 1)
                        for q in range(2 * half, 2 * half + 2):
                            for e in range(2 * i, 2 * i + 2):
                                for s in range(3):
                                    last = mm(SCB[half][:, q * D:(q + 1) * D], GT2[:, q, e, :], Y3[:, s, e, :],
                                              start=(i == 0 and q == 2 * half and e == 0 and s == 0), stop=(e == E - 1 and s == 2), skip_group_check=True)
                        return last

                    pe.wait_ge(gt1_ev, ro * 2 + 2)
                    g2_transposes(0)
                    g2_transposes(1)
                    pe.wait_ge(xg_ev, k * 2 + 2)
                    hidden(0)
                    for e in range(E):
                        for q in range(NC):
                            last = mm(OPS[:, 3 * e:3 * e + 3], G2[:, q, e * CAP:(e + 1) * CAP],
                                      XC[:, q, 3 * D + e:3 * D + 3 * E:E], start=(q == 0), stop=(q == NC - 1))
                    last.then_inc(ws_mm, 1)
                    g2_transposes(2)
                    hidden(1)
                    g2_transposes(3)
                    for e in range(2, E + 2):
                        if e < E:
                            hidden(e)
                        output(e - 2)
                        if e == E - 1:
                            scatter(0, 0)
                            scatter(0, 1)
                    for half in range(2):
                        for i in range(1, NY - 1):
                            scatter(i, half)
                    for half in range(2):
                        scatter(NY - 1, half).then_inc(sc_mm, 1)
                for q in range(NC):
                    if q % 2 == 0:
                        pe.wait_ge(oc3_done[q // 2], ro * inner + inner)
                    for j in range(TG):
                        for s in range(3):
                            last = mm(BKB[q][:, j * D:(j + 1) * D], GT1[:, TG * q + j, :], OC3[:, s, q, :], start=(s == 0), stop=(s == 2))
                    last.then_inc(back_mm, 1)


_INS = ['x', 'ctx_1024', 'fside_BxSx3_0', 'L0_xattn_Wq', 'L0_xattn_bq', 'L0_xattn_Wk', 'L0_xattn_bk', 'L0_xattn_Wv',
        'L0_xattn_bv', 'L0_xattn_Wo', 'L0_xattn_bo', 'L0_xattn_dist_emb', 'L0_ffn_gate_wi', 'L0_ffn_gate_bi',
        'L0_ffn_gate_wo', 'L0_ffn_gate_bo', 'L0_ffn_exp_wi', 'L0_ffn_exp_bi', 'L0_ffn_exp_wo', 'L0_ffn_exp_bo']


def kernel(**inputs):
    import numpy as _np
    import concourse.bacc as _bacc
    from concourse import mybir as _mybir
    from concourse.bass_utils import run_bass_kernel_spmd as _run

    nc = _bacc.Bacc("TRN2", target_bir_lowering=False, num_devices=1)
    arrays, args = {}, []
    for name in _INS:
        a = _np.ascontiguousarray(inputs[name])
        arrays[f"in_{name}_dram"] = a
        args.append(nc.dram_tensor(f"in_{name}_dram", a.shape, _mybir.dt.from_np(a.dtype), kind="ExternalInput").ap())
    out = nc.dram_tensor("out_dram", inputs['x'].shape, _mybir.dt.float32, kind="ExternalOutput").ap()
    build(nc, *args, out)
    r = _run(nc, [arrays], core_ids=[0])
    return r.results[0]["out_dram"]
```
